# Optimizing a Trainium2 kernel written in Bass

```python
import numpy as np
import jax
import jax.numpy as jnp

def _softmax(x, axis=-1):
    return jax.nn.softmax(x, axis=axis)

def _gelu(x):
    return jax.nn.gelu(x, approximate=True)

def _silu(x):
    return jax.nn.silu(x)

def _sigmoid(x):
    return jax.nn.sigmoid(x)

def _layernorm(x, axis=-1, eps=1e-05):
    m = jnp.mean(x, axis=axis, keepdims=True)
    v = jnp.var(x, axis=axis, keepdims=True)
    return (x - m) / jnp.sqrt(v + eps)

def _scatter_add(tgt, idx, src, axis=0):
    return tgt.at[idx].add(src)

def _segment_sum(src, seg, n):
    return jax.ops.segment_sum(src, seg, n)
kernel_name = 'mk_xattn_ffn_d4_seqx_r8_29944e'

def setup_inputs(seed: int=0):
    np.random.seed(seed)
    _w = jnp.asarray

    def _rec_inputs():
        import jax
        import jax.numpy as jnp
        _rk = jax.random.key(seed)
        x = -0.0002928 + 1 * jax.random.normal(jax.random.fold_in(_rk, 1), (8, 256, 128), jnp.float32)
        _lenS = 256 - jax.random.randint(jax.random.fold_in(_rk, 7), (8,), 0, max(1, 256 // 4) + 1, jnp.int32)
        _lenS2 = 256 - jax.random.randint(jax.random.fold_in(_rk, 8), (8,), 0, max(1, 256 // 4) + 1, jnp.int32)
        _ctx_768P = jax.random.normal(jax.random.fold_in(_rk, 11), (8, 16, 96), jnp.float32)
        _ctx_768c = jax.random.dirichlet(jax.random.fold_in(_rk, 511), 0.3 * jnp.ones((16,), jnp.float32), (8, 256))
        _ctx_768t = jnp.einsum('bsk,bkd->bsd', _ctx_768c, _ctx_768P)
        _ctx_768t = _ctx_768t * jax.lax.rsqrt(jnp.mean(jnp.square(_ctx_768t)) + 1e-12) * 0.953939
        ctx_768 = -8.43904e-05 + 0.999875 * (_ctx_768t + 0.3 * jax.random.normal(jax.random.fold_in(_rk, 611), (8, 256, 96), jnp.float32))
        return (x, ctx_768)
    x, ctx_768 = _rec_inputs()

    def _L0_xattn_setup():
        import jax, jax.numpy as jnp
        import numpy as np
        LATENT_CH = 128
        INPUT_CH = 96
        QK_CH = 128
        V_CH = 128
        OUT_CH = 128
        NHEADS = 8
        EPS = 1e-05

        def layer_norm(x, gamma, beta):
            mu = jnp.mean(x, axis=-1, keepdims=True)
            var = jnp.var(x, axis=-1, keepdims=True)
            return (x - mu) * jax.lax.rsqrt(var + EPS) * gamma + beta
        key = jax.random.key(seed)
        ks = jax.random.split(key, 6)
        B, Lq, Lkv = (8, 64, 2048)
        latent_q = jax.random.normal(ks[0], (B, Lq, LATENT_CH), dtype=jnp.float32)
        input_kv = jax.random.normal(ks[1], (B, Lkv, INPUT_CH), dtype=jnp.float32)
        W_Q = jax.random.normal(ks[2], (LATENT_CH, QK_CH), dtype=jnp.float32) / np.sqrt(LATENT_CH)
        W_K = jax.random.normal(ks[3], (INPUT_CH, QK_CH), dtype=jnp.float32) / np.sqrt(INPUT_CH)
        W_V = jax.random.normal(ks[4], (INPUT_CH, V_CH), dtype=jnp.float32) / np.sqrt(INPUT_CH)
        W_O = jax.random.normal(ks[5], (V_CH, OUT_CH), dtype=jnp.float32) / np.sqrt(V_CH)
        ln_lat_g = jnp.ones((LATENT_CH,), jnp.float32)
        ln_lat_b = jnp.zeros((LATENT_CH,), jnp.float32)
        ln_in_g = jnp.ones((INPUT_CH,), jnp.float32)
        ln_in_b = jnp.zeros((INPUT_CH,), jnp.float32)
        return dict(latent_q=latent_q, input_kv=input_kv, W_Q=W_Q, W_K=W_K, W_V=W_V, W_O=W_O, ln_lat_g=ln_lat_g, ln_lat_b=ln_lat_b, ln_in_g=ln_in_g, ln_in_b=ln_in_b)
    _L0_xattn_all = _L0_xattn_setup()
    _L0_xattn_in = {k: v for k, v in _L0_xattn_all.items() if k in ('W_Q', 'W_K', 'W_V', 'W_O', 'ln_lat_g', 'ln_lat_b', 'ln_in_g', 'ln_in_b')}
    del _L0_xattn_all

    def _L0_ffn_setup():
        import jax, jax.numpy as jnp
        import numpy as np
        DIM = 128

        def _reference_tuple_inner(x, W_r, W_k, W_v, mu_r, mu_k):
            B, T, C = x.shape
            x_prev = jnp.concatenate([jnp.zeros((B, 1, C), x.dtype), x[:, :-1, :]], axis=1)
            xr = mu_r * x + (1.0 - mu_r) * x_prev
            xk = mu_k * x + (1.0 - mu_k) * x_prev
            r = jax.nn.sigmoid(jnp.einsum('btc,dc->btd', xr, W_r))
            k = jnp.einsum('btc,dc->btd', xk, W_k)
            k_act = jnp.square(jax.nn.relu(k))
            out = r * jnp.einsum('btc,dc->btd', k_act, W_v)
            new_state = x[:, -1, :]
            return (out, new_state)
        key = jax.random.key(seed)
        ks = jax.random.split(key, 6)
        B, T, C = (8, 256, DIM)
        x = jax.random.normal(ks[0], (B, T, C), dtype=jnp.float32)
        s = 1.0 / np.sqrt(C)
        W_r = jax.random.uniform(ks[1], (C, C), jnp.float32, -s, s)
        W_k = jax.random.uniform(ks[2], (C, C), jnp.float32, -s, s)
        W_v = jax.random.uniform(ks[3], (C, C), jnp.float32, -s, s)
        mu_r = jax.random.uniform(ks[4], (C,), jnp.float32)
        mu_k = jax.random.uniform(ks[5], (C,), jnp.float32)
        return {'x': x, 'W_r': W_r, 'W_k': W_k, 'W_v': W_v, 'mu_r': mu_r, 'mu_k': mu_k}
    _L0_ffn_all = _L0_ffn_setup()
    _L0_ffn_in = {k: v for k, v in _L0_ffn_all.items() if k in ('W_r', 'W_k', 'W_v', 'mu_r', 'mu_k')}
    del _L0_ffn_all

    def _L1_xattn_setup():
        import jax, jax.numpy as jnp
        import numpy as np
        IMAGE_DIM = 128
        TEXT_DIM = 96
        NUM_HEADS = 16
        HEAD_DIM = IMAGE_DIM // NUM_HEADS
        key = jax.random.key(seed)
        ks = jax.random.split(key, 14)
        B, N, M = (4, 512, 64)
        s_img = 1.0 / np.sqrt(IMAGE_DIM)
        s_txt = 1.0 / np.sqrt(TEXT_DIM)
        s_ff = 1.0 / np.sqrt(2 * IMAGE_DIM)
        return {'x': jax.random.normal(ks[0], (B, N, IMAGE_DIM), jnp.float32), 'y': jax.random.normal(ks[1], (B, M, TEXT_DIM), jnp.float32), 'Wq': jax.random.normal(ks[2], (IMAGE_DIM, IMAGE_DIM), jnp.float32) * s_img, 'bq': jax.random.normal(ks[3], (IMAGE_DIM,), jnp.float32) * s_img, 'Wk': jax.random.normal(ks[4], (TEXT_DIM, IMAGE_DIM), jnp.float32) * s_txt, 'bk': jax.random.normal(ks[5], (IMAGE_DIM,), jnp.float32) * s_txt, 'Wv': jax.random.normal(ks[6], (TEXT_DIM, IMAGE_DIM), jnp.float32) * s_txt, 'bv': jax.random.normal(ks[7], (IMAGE_DIM,), jnp.float32) * s_txt, 'W1': jax.random.normal(ks[8], (IMAGE_DIM, 2 * IMAGE_DIM), jnp.float32) * s_img, 'b1': jax.random.normal(ks[9], (2 * IMAGE_DIM,), jnp.float32) * s_img, 'W2': jax.random.normal(ks[10], (2 * IMAGE_DIM, IMAGE_DIM), jnp.float32) * s_ff, 'b2': jax.random.normal(ks[11], (IMAGE_DIM,), jnp.float32) * s_ff}
    _L1_xattn_all = _L1_xattn_setup()
    _L1_xattn_in = {k: v for k, v in _L1_xattn_all.items() if k in ('Wq', 'bq', 'Wk', 'bk', 'Wv', 'bv', 'W1', 'b1', 'W2', 'b2')}
    del _L1_xattn_all

    def _L1_ffn_setup():
        import jax, jax.numpy as jnp
        import numpy as np
        from jax import lax
        DIM = 128
        HID = 256
        E = 8
        K = 2
        B, T = (2, 64)
        key = jax.random.key(seed)
        ks = jax.random.split(key, 5)
        scale = 1.0 / np.sqrt(DIM)
        x = jax.random.normal(ks[0], (B, T, DIM), dtype=jnp.float32)
        router_w = jax.random.normal(ks[1], (E, DIM), dtype=jnp.float32) * scale
        w_gate = jax.random.normal(ks[2], (E, HID, DIM), dtype=jnp.float32) * scale
        w_up = jax.random.normal(ks[3], (E, HID, DIM), dtype=jnp.float32) * scale
        w_down = jax.random.normal(ks[4], (E, DIM, HID), dtype=jnp.float32) * (1.0 / np.sqrt(HID))
        return {'x': x, 'router_w': router_w, 'w_gate': w_gate, 'w_up': w_up, 'w_down': w_down}
    _L1_ffn_all = _L1_ffn_setup()
    _L1_ffn_in = {k: v for k, v in _L1_ffn_all.items() if k in ('router_w', 'w_gate', 'w_up', 'w_down')}
    del _L1_ffn_all

    def _L2_xattn_setup():
        import jax, jax.numpy as jnp
        import numpy as np
        N_HEADS = 8
        D_EMBED = 128
        D_CROSS = 96
        D_HEAD = D_EMBED // N_HEADS
        key = jax.random.key(seed)
        ks = jax.random.split(key, 10)
        B, SQ, SKV = (8, 512, 77)
        scale_e = 1.0 / np.sqrt(D_EMBED)
        scale_c = 1.0 / np.sqrt(D_CROSS)
        return {'x': jax.random.normal(ks[0], (B, SQ, D_EMBED), dtype=jnp.float32), 'y': jax.random.normal(ks[1], (B, SKV, D_CROSS), dtype=jnp.float32), 'Wq': jax.random.normal(ks[2], (D_EMBED, D_EMBED), dtype=jnp.float32) * scale_e, 'bq': jnp.zeros((D_EMBED,), dtype=jnp.float32), 'Wk': jax.random.normal(ks[3], (D_CROSS, D_EMBED), dtype=jnp.float32) * scale_c, 'bk': jnp.zeros((D_EMBED,), dtype=jnp.float32), 'Wv': jax.random.normal(ks[4], (D_CROSS, D_EMBED), dtype=jnp.float32) * scale_c, 'bv': jnp.zeros((D_EMBED,), dtype=jnp.float32), 'Wo': jax.random.normal(ks[5], (D_EMBED, D_EMBED), dtype=jnp.float32) * scale_e, 'bo': jnp.zeros((D_EMBED,), dtype=jnp.float32)}
    _L2_xattn_all = _L2_xattn_setup()
    _L2_xattn_in = {k: v for k, v in _L2_xattn_all.items() if k in ('Wq', 'bq', 'Wk', 'bk', 'Wv', 'bv', 'Wo', 'bo')}
    del _L2_xattn_all

    def _L2_ffn_setup():
        import jax, jax.numpy as jnp
        import numpy as np
        E = 8
        TOP_K = 2
        LN_EPS = 1e-05

        def _layernorm(x, g, b):
            mu = jnp.mean(x, axis=-1, keepdims=True)
            var = jnp.var(x, axis=-1, keepdims=True)
            return (x - mu) * jax.lax.rsqrt(var + LN_EPS) * g + b
        key = jax.random.key(seed)
        ks = jax.random.split(key, 4)
        B, T, H, HF = (4, 256, 128, 256)
        s_in = 1.0 / np.sqrt(H)
        s_hid = 1.0 / np.sqrt(HF)
        return {'x': jax.random.normal(ks[0], (B, T, H), dtype=jnp.float32), 'ln_g': jnp.ones((H,), dtype=jnp.float32), 'ln_b': jnp.zeros((H,), dtype=jnp.float32), 'rW': jax.random.normal(ks[1], (H, E), dtype=jnp.float32) * s_in, 'rb': jnp.zeros((E,), dtype=jnp.float32), 'W1': jax.random.normal(ks[2], (E, H, HF), dtype=jnp.float32) * s_in, 'b1': jnp.zeros((E, HF), dtype=jnp.float32), 'W2': jax.random.normal(ks[3], (E, HF, H), dtype=jnp.float32) * s_hid, 'b2': jnp.zeros((E, H), dtype=jnp.float32)}
    _L2_ffn_all = _L2_ffn_setup()
    _L2_ffn_in = {k: v for k, v in _L2_ffn_all.items() if k in ('ln_g', 'ln_b', 'rW', 'rb', 'W1', 'b1', 'W2', 'b2')}
    del _L2_ffn_all

    def _L3_xattn_setup():
        import jax, jax.numpy as jnp
        import numpy as np
        EPS = 1e-05

        def layernorm(x, g, b):
            mu = jnp.mean(x, axis=-1, keepdims=True)
            var = jnp.mean(jnp.square(x - mu), axis=-1, keepdims=True)
            return (x - mu) * jax.lax.rsqrt(var + EPS) * g + b
        key = jax.random.key(seed)
        ks = jax.random.split(key, 12)
        B, L1, L2 = (8, 256, 256)
        D1, D2, E = (128, 96, 128)
        s1, s2, se = (D1 ** (-0.5), D2 ** (-0.5), E ** (-0.5))
        return {'modality1': jax.random.normal(ks[0], (B, L1, D1), jnp.float32), 'modality2': jax.random.normal(ks[1], (B, L2, D2), jnp.float32), 'ln1_g': jnp.ones((D1,), jnp.float32), 'ln1_b': jnp.zeros((D1,), jnp.float32), 'ln2_g': jnp.ones((D2,), jnp.float32), 'ln2_b': jnp.zeros((D2,), jnp.float32), 'Wq': jax.random.normal(ks[2], (D1, E), jnp.float32) * s1, 'bq': jax.random.normal(ks[3], (E,), jnp.float32) * 0.01, 'Wk': jax.random.normal(ks[4], (D2, E), jnp.float32) * s2, 'bk': jax.random.normal(ks[5], (E,), jnp.float32) * 0.01, 'Wv': jax.random.normal(ks[6], (D2, E), jnp.float32) * s2, 'bv': jax.random.normal(ks[7], (E,), jnp.float32) * 0.01, 'Wo': jax.random.normal(ks[8], (E, D1), jnp.float32) * se, 'bo': jax.random.normal(ks[9], (D1,), jnp.float32) * 0.01}
    _L3_xattn_all = _L3_xattn_setup()
    _L3_xattn_in = {k: v for k, v in _L3_xattn_all.items() if k in ('ln1_g', 'ln1_b', 'ln2_g', 'ln2_b', 'Wq', 'bq', 'Wk', 'bk', 'Wv', 'bv', 'Wo', 'bo')}
    del _L3_xattn_all

    def _L3_ffn_setup():
        import jax, jax.numpy as jnp
        import numpy as np
        DIM = 128
        HIDDEN = 128
        NUM_EXPERTS = 8
        TOP_K = 2
        key = jax.random.key(seed)
        ks = jax.random.split(key, 8)
        std = 0.02
        x = jax.random.normal(ks[0], (2, 128, DIM), dtype=jnp.float32)
        gate_w = jax.random.normal(ks[1], (NUM_EXPERTS, DIM), dtype=jnp.float32) * std
        w1 = jax.random.normal(ks[2], (NUM_EXPERTS, DIM, HIDDEN), dtype=jnp.float32) * std
        w2 = jax.random.normal(ks[3], (NUM_EXPERTS, HIDDEN, DIM), dtype=jnp.float32) * std
        w3 = jax.random.normal(ks[4], (NUM_EXPERTS, DIM, HIDDEN), dtype=jnp.float32) * std
        w1s = jax.random.normal(ks[5], (1, DIM, HIDDEN), dtype=jnp.float32) * std
        w2s = jax.random.normal(ks[6], (1, HIDDEN, DIM), dtype=jnp.float32) * std
        w3s = jax.random.normal(ks[7], (1, DIM, HIDDEN), dtype=jnp.float32) * std
        return {'x': x, 'gate_w': gate_w, 'w1': w1, 'w2': w2, 'w3': w3, 'w1s': w1s, 'w2s': w2s, 'w3s': w3s}
    _L3_ffn_all = _L3_ffn_setup()
    _L3_ffn_in = {k: v for k, v in _L3_ffn_all.items() if k in ('gate_w', 'w1', 'w2', 'w3', 'w1s', 'w2s', 'w3s')}
    del _L3_ffn_all
    return {'x': x, 'ctx_768': ctx_768, 'L0_xattn_W_Q': _L0_xattn_in['W_Q'], 'L0_xattn_W_K': _L0_xattn_in['W_K'], 'L0_xattn_W_V': _L0_xattn_in['W_V'], 'L0_xattn_W_O': _L0_xattn_in['W_O'], 'L0_xattn_ln_lat_g': _L0_xattn_in['ln_lat_g'], 'L0_xattn_ln_lat_b': _L0_xattn_in['ln_lat_b'], 'L0_xattn_ln_in_g': _L0_xattn_in['ln_in_g'], 'L0_xattn_ln_in_b': _L0_xattn_in['ln_in_b'], 'L0_ffn_W_r': _L0_ffn_in['W_r'], 'L0_ffn_W_k': _L0_ffn_in['W_k'], 'L0_ffn_W_v': _L0_ffn_in['W_v'], 'L0_ffn_mu_r': _L0_ffn_in['mu_r'], 'L0_ffn_mu_k': _L0_ffn_in['mu_k'], 'L1_xattn_Wq': _L1_xattn_in['Wq'], 'L1_xattn_bq': _L1_xattn_in['bq'], 'L1_xattn_Wk': _L1_xattn_in['Wk'], 'L1_xattn_bk': _L1_xattn_in['bk'], 'L1_xattn_Wv': _L1_xattn_in['Wv'], 'L1_xattn_bv': _L1_xattn_in['bv'], 'L1_xattn_W1': _L1_xattn_in['W1'], 'L1_xattn_b1': _L1_xattn_in['b1'], 'L1_xattn_W2': _L1_xattn_in['W2'], 'L1_xattn_b2': _L1_xattn_in['b2'], 'L1_ffn_router_w': _L1_ffn_in['router_w'], 'L1_ffn_w_gate': _L1_ffn_in['w_gate'], 'L1_ffn_w_up': _L1_ffn_in['w_up'], 'L1_ffn_w_down': _L1_ffn_in['w_down'], 'L2_xattn_Wq': _L2_xattn_in['Wq'], 'L2_xattn_bq': _L2_xattn_in['bq'], 'L2_xattn_Wk': _L2_xattn_in['Wk'], 'L2_xattn_bk': _L2_xattn_in['bk'], 'L2_xattn_Wv': _L2_xattn_in['Wv'], 'L2_xattn_bv': _L2_xattn_in['bv'], 'L2_xattn_Wo': _L2_xattn_in['Wo'], 'L2_xattn_bo': _L2_xattn_in['bo'], 'L2_ffn_ln_g': _L2_ffn_in['ln_g'], 'L2_ffn_ln_b': _L2_ffn_in['ln_b'], 'L2_ffn_rW': _L2_ffn_in['rW'], 'L2_ffn_rb': _L2_ffn_in['rb'], 'L2_ffn_W1': _L2_ffn_in['W1'], 'L2_ffn_b1': _L2_ffn_in['b1'], 'L2_ffn_W2': _L2_ffn_in['W2'], 'L2_ffn_b2': _L2_ffn_in['b2'], 'L3_xattn_ln1_g': _L3_xattn_in['ln1_g'], 'L3_xattn_ln1_b': _L3_xattn_in['ln1_b'], 'L3_xattn_ln2_g': _L3_xattn_in['ln2_g'], 'L3_xattn_ln2_b': _L3_xattn_in['ln2_b'], 'L3_xattn_Wq': _L3_xattn_in['Wq'], 'L3_xattn_bq': _L3_xattn_in['bq'], 'L3_xattn_Wk': _L3_xattn_in['Wk'], 'L3_xattn_bk': _L3_xattn_in['bk'], 'L3_xattn_Wv': _L3_xattn_in['Wv'], 'L3_xattn_bv': _L3_xattn_in['bv'], 'L3_xattn_Wo': _L3_xattn_in['Wo'], 'L3_xattn_bo': _L3_xattn_in['bo'], 'L3_ffn_gate_w': _L3_ffn_in['gate_w'], 'L3_ffn_w1': _L3_ffn_in['w1'], 'L3_ffn_w2': _L3_ffn_in['w2'], 'L3_ffn_w3': _L3_ffn_in['w3'], 'L3_ffn_w1s': _L3_ffn_in['w1s'], 'L3_ffn_w2s': _L3_ffn_in['w2s'], 'L3_ffn_w3s': _L3_ffn_in['w3s']}

def reference(x, ctx_768, L0_xattn_W_Q, L0_xattn_W_K, L0_xattn_W_V, L0_xattn_W_O, L0_xattn_ln_lat_g, L0_xattn_ln_lat_b, L0_xattn_ln_in_g, L0_xattn_ln_in_b, L0_ffn_W_r, L0_ffn_W_k, L0_ffn_W_v, L0_ffn_mu_r, L0_ffn_mu_k, L1_xattn_Wq, L1_xattn_bq, L1_xattn_Wk, L1_xattn_bk, L1_xattn_Wv, L1_xattn_bv, L1_xattn_W1, L1_xattn_b1, L1_xattn_W2, L1_xattn_b2, L1_ffn_router_w, L1_ffn_w_gate, L1_ffn_w_up, L1_ffn_w_down, L2_xattn_Wq, L2_xattn_bq, L2_xattn_Wk, L2_xattn_bk, L2_xattn_Wv, L2_xattn_bv, L2_xattn_Wo, L2_xattn_bo, L2_ffn_ln_g, L2_ffn_ln_b, L2_ffn_rW, L2_ffn_rb, L2_ffn_W1, L2_ffn_b1, L2_ffn_W2, L2_ffn_b2, L3_xattn_ln1_g, L3_xattn_ln1_b, L3_xattn_ln2_g, L3_xattn_ln2_b, L3_xattn_Wq, L3_xattn_bq, L3_xattn_Wk, L3_xattn_bk, L3_xattn_Wv, L3_xattn_bv, L3_xattn_Wo, L3_xattn_bo, L3_ffn_gate_w, L3_ffn_w1, L3_ffn_w2, L3_ffn_w3, L3_ffn_w1s, L3_ffn_w2s, L3_ffn_w3s):
    import jax
    import jax.numpy as jnp

    def _L0_xattn_ref(latent_q, input_kv, W_Q, W_K, W_V, W_O, ln_lat_g, ln_lat_b, ln_in_g, ln_in_b):
        import jax, jax.numpy as jnp
        import numpy as np
        LATENT_CH = 128
        INPUT_CH = 96
        QK_CH = 128
        V_CH = 128
        OUT_CH = 128
        NHEADS = 8
        EPS = 1e-05

        def layer_norm(x, gamma, beta):
            mu = jnp.mean(x, axis=-1, keepdims=True)
            var = jnp.var(x, axis=-1, keepdims=True)
            return (x - mu) * jax.lax.rsqrt(var + EPS) * gamma + beta
        B, Lq, _ = latent_q.shape
        _, Lkv, _ = input_kv.shape
        H = NHEADS
        dqk = QK_CH // H
        dv = V_CH // H
        lat = layer_norm(latent_q, ln_lat_g, ln_lat_b)
        inp = layer_norm(input_kv, ln_in_g, ln_in_b)
        Q = (lat @ W_Q).reshape(B, Lq, H, dqk)
        K = (inp @ W_K).reshape(B, Lkv, H, dqk)
        V = (inp @ W_V).reshape(B, Lkv, H, dv)
        scale = 1.0 / np.sqrt(dqk).astype(np.float32)
        attn = jnp.einsum('bqhd,bkhd->bhqk', Q, K) * scale
        attn = jax.nn.softmax(attn, axis=-1)
        out = jnp.einsum('bhqk,bkhd->bqhd', attn, V).reshape(B, Lq, V_CH)
        return out @ W_O

    def _L0_ffn_ref(x, W_r, W_k, W_v, mu_r, mu_k):
        import jax, jax.numpy as jnp
        import numpy as np
        DIM = 128

        def _reference_tuple_inner(x, W_r, W_k, W_v, mu_r, mu_k):
            B, T, C = x.shape
            x_prev = jnp.concatenate([jnp.zeros((B, 1, C), x.dtype), x[:, :-1, :]], axis=1)
            xr = mu_r * x + (1.0 - mu_r) * x_prev
            xk = mu_k * x + (1.0 - mu_k) * x_prev
            r = jax.nn.sigmoid(jnp.einsum('btc,dc->btd', xr, W_r))
            k = jnp.einsum('btc,dc->btd', xk, W_k)
            k_act = jnp.square(jax.nn.relu(k))
            out = r * jnp.einsum('btc,dc->btd', k_act, W_v)
            new_state = x[:, -1, :]
            return (out, new_state)
        return _reference_tuple_inner(x, W_r, W_k, W_v, mu_r, mu_k)[0]

    def _L1_xattn_ref(x, y, Wq, bq, Wk, bk, Wv, bv, W1, b1, W2, b2):
        import jax, jax.numpy as jnp
        import numpy as np
        IMAGE_DIM = 128
        TEXT_DIM = 96
        NUM_HEADS = 16
        HEAD_DIM = IMAGE_DIM // NUM_HEADS
        B, N, _ = x.shape
        M = y.shape[1]
        q = (x @ Wq + bq).reshape(B, N, NUM_HEADS, HEAD_DIM)
        k = (y @ Wk + bk).reshape(B, M, NUM_HEADS, HEAD_DIM)
        v = (y @ Wv + bv).reshape(B, M, NUM_HEADS, HEAD_DIM)
        scale = 1.0 / np.sqrt(HEAD_DIM)
        scores = jnp.einsum('bnhd,bmhd->bhnm', q, k) * scale
        attn = jax.nn.softmax(scores, axis=-1)
        out = jnp.einsum('bhnm,bmhd->bnhd', attn, v).reshape(B, N, IMAGE_DIM)
        h = jax.nn.relu(out @ W1 + b1)
        return h @ W2 + b2

    def _L1_ffn_ref(x, router_w, w_gate, w_up, w_down):
        import jax, jax.numpy as jnp
        import numpy as np
        from jax import lax
        DIM = 128
        HID = 256
        E = 8
        K = 2
        B, T = (2, 64)
        Bb, Tt, D = x.shape
        N = Bb * Tt
        xf = x.reshape(N, D)
        logits = xf @ router_w.T
        routing = jax.nn.softmax(logits, axis=-1)
        top_w, top_i = lax.top_k(routing, K)
        top_w = top_w / jnp.sum(top_w, axis=-1, keepdims=True)
        combine = jnp.zeros((N, E), dtype=x.dtype)
        combine = combine.at[jnp.arange(N)[:, None], top_i].add(top_w)
        g = jnp.einsum('nd,ehd->neh', xf, w_gate)
        u = jnp.einsum('nd,ehd->neh', xf, w_up)
        h = jax.nn.silu(g) * u
        y = jnp.einsum('neh,edh->ned', h, w_down)
        out = jnp.einsum('ned,ne->nd', y, combine)
        return out.reshape(Bb, Tt, D)

    def _L2_xattn_ref(x, y, Wq, bq, Wk, bk, Wv, bv, Wo, bo):
        import jax, jax.numpy as jnp
        import numpy as np
        N_HEADS = 8
        D_EMBED = 128
        D_CROSS = 96
        D_HEAD = D_EMBED // N_HEADS
        B, SQ, _ = x.shape
        q = x @ Wq + bq
        k = y @ Wk + bk
        v = y @ Wv + bv
        q = q.reshape(B, SQ, N_HEADS, D_HEAD).transpose(0, 2, 1, 3)
        k = k.reshape(B, -1, N_HEADS, D_HEAD).transpose(0, 2, 1, 3)
        v = v.reshape(B, -1, N_HEADS, D_HEAD).transpose(0, 2, 1, 3)
        scale = 1.0 / jnp.sqrt(jnp.asarray(D_HEAD, dtype=q.dtype))
        weight = jnp.einsum('bhqd,bhkd->bhqk', q, k) * scale
        weight = jax.nn.softmax(weight, axis=-1)
        out = jnp.einsum('bhqk,bhkd->bhqd', weight, v)
        out = out.transpose(0, 2, 1, 3).reshape(B, SQ, D_EMBED)
        return out @ Wo + bo

    def _L2_ffn_ref(x, ln_g, ln_b, rW, rb, W1, b1, W2, b2):
        import jax, jax.numpy as jnp
        import numpy as np
        E = 8
        TOP_K = 2
        LN_EPS = 1e-05

        def _layernorm(x, g, b):
            mu = jnp.mean(x, axis=-1, keepdims=True)
            var = jnp.var(x, axis=-1, keepdims=True)
            return (x - mu) * jax.lax.rsqrt(var + LN_EPS) * g + b
        z = _layernorm(x, ln_g, ln_b)
        logits = jnp.einsum('bth,he->bte', z, rW) + rb
        probs = jax.nn.softmax(logits, axis=-1)
        topv, topi = jax.lax.top_k(probs, TOP_K)
        mask = jnp.sum(jax.nn.one_hot(topi, E, dtype=probs.dtype) * topv[..., None], axis=-2)
        denom = jnp.maximum(jnp.sum(mask, axis=-1, keepdims=True), 1e-08)
        w = mask / denom
        hid = jax.nn.gelu(jnp.einsum('bth,ehf->btef', z, W1) + b1, approximate=False)
        outs = jnp.einsum('btef,efh->bteh', hid, W2) + b2
        mixed = jnp.sum(outs * w[..., None], axis=2)
        return x + mixed

    def _L3_xattn_ref(modality1, modality2, ln1_g, ln1_b, ln2_g, ln2_b, Wq, bq, Wk, bk, Wv, bv, Wo, bo):
        import jax, jax.numpy as jnp
        import numpy as np
        EPS = 1e-05

        def layernorm(x, g, b):
            mu = jnp.mean(x, axis=-1, keepdims=True)
            var = jnp.mean(jnp.square(x - mu), axis=-1, keepdims=True)
            return (x - mu) * jax.lax.rsqrt(var + EPS) * g + b
        E = Wq.shape[1]
        scaling = E ** (-0.5)
        x1 = layernorm(modality1, ln1_g, ln1_b)
        x2 = layernorm(modality2, ln2_g, ln2_b)
        q = x1 @ Wq + bq
        k = x2 @ Wk + bk
        v = x2 @ Wv + bv
        scores = jnp.einsum('bqe,bke->bqk', q, k) * scaling
        attn = jax.nn.softmax(scores, axis=-1)
        ctx = jnp.einsum('bqk,bke->bqe', attn, v)
        return ctx @ Wo + bo

    def _L3_ffn_ref(x, gate_w, w1, w2, w3, w1s, w2s, w3s):
        import jax, jax.numpy as jnp
        import numpy as np
        DIM = 128
        HIDDEN = 128
        NUM_EXPERTS = 8
        TOP_K = 2
        bs, slen, dim = x.shape
        xt = x.reshape(bs * slen, dim)
        logits = xt @ gate_w.T
        scores = jax.nn.softmax(logits.astype(jnp.float32), axis=1).astype(x.dtype)
        top_scores, sel = jax.lax.top_k(scores, TOP_K)
        sel_flat = sel.reshape(-1)
        order = jnp.argsort(sel_flat, stable=True)
        top_scores_sorted = top_scores.reshape(-1)[order]
        token_idx = order // TOP_K
        eid = sel_flat[order]
        routed_in = xt[token_idx] * top_scores_sorted[:, None]
        out_routed = jnp.zeros_like(routed_in)
        for e in range(NUM_EXPERTS):
            m = (eid == e)[:, None]
            xe = jnp.where(m, routed_in, 0.0)
            h = jax.nn.silu(xe @ w1[e]) * (xe @ w3[e])
            out_routed = out_routed + jnp.where(m, h @ w2[e], 0.0)
        hs = jax.nn.silu(xt @ w1s[0]) * (xt @ w3s[0])
        out = hs @ w2s[0]
        out = out.at[token_idx].add(out_routed)
        return out.reshape(bs, slen, dim)
    x = x + _L0_xattn_ref(_layernorm(x, axis=-1), ctx_768, L0_xattn_W_Q, L0_xattn_W_K, L0_xattn_W_V, L0_xattn_W_O, L0_xattn_ln_lat_g, L0_xattn_ln_lat_b, L0_xattn_ln_in_g, L0_xattn_ln_in_b)
    x = x + _L0_ffn_ref(_layernorm(x, axis=-1), L0_ffn_W_r, L0_ffn_W_k, L0_ffn_W_v, L0_ffn_mu_r, L0_ffn_mu_k)
    x = x + _L1_xattn_ref(_layernorm(x, axis=-1), ctx_768, L1_xattn_Wq, L1_xattn_bq, L1_xattn_Wk, L1_xattn_bk, L1_xattn_Wv, L1_xattn_bv, L1_xattn_W1, L1_xattn_b1, L1_xattn_W2, L1_xattn_b2)
    x = x + _L1_ffn_ref(_layernorm(x, axis=-1), L1_ffn_router_w, L1_ffn_w_gate, L1_ffn_w_up, L1_ffn_w_down)
    x = x + _L2_xattn_ref(_layernorm(x, axis=-1), ctx_768, L2_xattn_Wq, L2_xattn_bq, L2_xattn_Wk, L2_xattn_bk, L2_xattn_Wv, L2_xattn_bv, L2_xattn_Wo, L2_xattn_bo)
    x = x + _L2_ffn_ref(_layernorm(x, axis=-1), L2_ffn_ln_g, L2_ffn_ln_b, L2_ffn_rW, L2_ffn_rb, L2_ffn_W1, L2_ffn_b1, L2_ffn_W2, L2_ffn_b2)
    x = x + _L3_xattn_ref(_layernorm(x, axis=-1), ctx_768, L3_xattn_ln1_g, L3_xattn_ln1_b, L3_xattn_ln2_g, L3_xattn_ln2_b, L3_xattn_Wq, L3_xattn_bq, L3_xattn_Wk, L3_xattn_bk, L3_xattn_Wv, L3_xattn_bv, L3_xattn_Wo, L3_xattn_bo)
    x = x + _L3_ffn_ref(_layernorm(x, axis=-1), L3_ffn_gate_w, L3_ffn_w1, L3_ffn_w2, L3_ffn_w3, L3_ffn_w1s, L3_ffn_w2s, L3_ffn_w3s)
    return x

_drawn_inputs = setup_inputs


def setup_inputs(seed=0):
    import zlib

    import numpy as np

    out = dict(_drawn_inputs(seed))
    spreads = {'L0_xattn_ln_lat_g': (1.0, 0.2),
     'L0_xattn_ln_lat_b': (0.0, 0.1),
     'L0_xattn_ln_in_g': (1.0, 0.2),
     'L0_xattn_ln_in_b': (0.0, 0.1),
     'L2_xattn_bq': (0.0, 0.415),
     'L2_xattn_bk': (0.0, 2.0),
     'L2_xattn_bv': (0.0, 0.1),
     'L2_xattn_bo': (0.0, 0.1),
     'L2_ffn_ln_g': (1.0, 0.2),
     'L2_ffn_ln_b': (0.0, 0.1),
     'L2_ffn_rb': (0.0, 0.1),
     'L2_ffn_b1': (0.0, 0.423),
     'L2_ffn_b2': (0.0, 0.285),
     'L3_xattn_ln1_g': (1.0, 0.6),
     'L3_xattn_ln1_b': (0.0, 0.8),
     'L3_xattn_ln2_g': (1.0, 0.2),
     'L3_xattn_ln2_b': (0.0, 0.1)}
    factors = {'L0_ffn_mu_r': 2.81,
     'L1_xattn_bk': 64.0,
     'L3_xattn_bq': 52.349,
     'L3_xattn_bk': 64.0,
     'L3_xattn_bv': 8.0,
     'L3_xattn_bo': 8.0,
     'L3_ffn_gate_w': 8.0,
     'L3_ffn_w1': 8.0,
     'L3_ffn_w2': 8.0,
     'L3_ffn_w3': 8.0,
     'L3_ffn_w1s': 8.0,
     'L3_ffn_w2s': 8.0,
     'L3_ffn_w3s': 8.0}
    for name, (base, spread) in spreads.items():
        noise = np.random.default_rng([zlib.crc32(name.encode()), seed]).standard_normal(out[name].shape)
        drawn = base * np.exp(spread * noise) if base else spread * noise
        out[name] = jnp.asarray(drawn.astype(out[name].dtype))
    for name, factor in factors.items():
        out[name] = (out[name] * factor).astype(out[name].dtype)
    return out
```

```python
from contextlib import ExitStack

import concourse.bass as bass
from concourse import mybir
import numpy as np

F32 = mybir.dt.float32
BF16 = mybir.dt.bfloat16
F16 = mybir.dt.float16
ALU = mybir.AluOpType
ACT = mybir.ActivationFunctionType
AX = mybir.AxisListType.X

P = 128
B = 8
T = 256
D = 128
C = 96
NT = B * T // P
EPS = 1e-5
NBLK = 4
BLK = B * T // NBLK
BT = BLK // P
E = 8

HEADS = {"att0": 8, "att1": 16, "att2": 8}
SLOTS = {
    "att0": [(0, 0), (0, 1), (1, 0), (1, 1), (0, 2), (2, 0)],
    "att1": [(0, 0), (0, 1), (1, 0), (1, 1), (0, 2), (2, 0), (1, 2), (2, 1), (2, 2)],
    "att2": [(0, 0), (0, 1), (1, 0), (1, 1), (0, 2), (2, 0)],
}
MAXROW = 96

PACKS = {
    "consts": [("ident", 128), ("index", 8)],
    "att0": [("wq", 128), ("wk", 128), ("wv", 128), ("xg", 1), ("xb", 1), ("cg", 1), ("cb", 1), ("wo", 128)],
    "ffn0": [("wr", 128), ("wk", 128), ("wv", 128), ("mur", 1), ("muk", 1)],
    "att1": [("wq", 128), ("wk", 128), ("wv", 128), ("bq", 1), ("bk", 1), ("bv", 128),
             ("w1", 256), ("b1", 2), ("w2", 256), ("bo", 128)],
    "moe1": [("router", 8), ("wg", 2048), ("wu", 2048), ("wd", 2048)],
    "att2": [("wq", 128), ("wk", 128), ("wv", 128), ("bq", 1), ("bk", 1), ("bv", 128), ("wo", 128), ("bo", 128)],
    "moe2": [("router", 8), ("rb", 8), ("xg", 1), ("xb", 1), ("w1", 2048), ("b1", 16), ("w2", 2048), ("b2", 128)],
    "att3": [("wq", 128), ("wk", 128), ("wv", 128), ("bq", 1), ("bk", 1), ("bv", 128), ("wo", 128), ("bo", 128),
             ("xg", 1), ("xb", 1), ("cg", 1), ("cb", 1)],
    "moe3": [("router", 8), ("w1", 9 * 128), ("w3", 9 * 128), ("w2", 9 * 128)],
}
STAGES = [s for s in PACKS if s != "consts"]
ATT = ("att0", "att1", "att2")
MOE = ("moe1", "moe2", "moe3")

FIRST_ROWS = 1
ROW_SLOTS = {"att0": 5, "att1": 11, "att2": 5}
LOW_BY_DVE = {"att0": (3, 6, 7), "att1": (6, 12, 13, 14, 15), "att2": (3, 6, 7)}
RING = 6
LAG = 3

H = HEADS
PER_BATCH = {s: (1, 8) for s in ATT}
ALL_ATT = {s: (1, 8) for s in (*ATT, "att3")}
AT_ONCE = ("ffn0", "moe1", "moe2", "att3", "moe3")
EVENTS = {
    "stats_taken": {**PER_BATCH, **{s: (1, 1) for s in AT_ONCE}},
    "moments_ready": {**PER_BATCH, **{s: (1, 1) for s in AT_ONCE}},
    "var_ready": {**PER_BATCH, **{s: (1, 1) for s in AT_ONCE}},
    "rstd_ready": {**PER_BATCH, **{s: (1, 1) for s in AT_ONCE}},
    "z_ready": {**PER_BATCH, **{s: (4, 1) for s in AT_ONCE}},
    "zt_psum": {**PER_BATCH, **{s: (4, 1) for s in AT_ONCE}, "att3": (8, 1)},
    "zt_ready": {**PER_BATCH, **{s: (4, 1) for s in AT_ONCE}, "att3": (8, 1)},
    "x_plus": {"moe2": (1, 1)},
    "x_updated": {**{s: (1, 8) for s in STAGES}, "ffn0": (1, 4), "moe1": (8, 4), "moe2": (8, 4), "moe3": (1, 4)},
    "qk_psum": ALL_ATT,
    "v_psum": ALL_ATT,
    "qk_ready": ALL_ATT,
    "v_ready": ALL_ATT,
    "o_ready": ALL_ATT,
    "ot_psum": ALL_ATT,
    "ot_ready": ALL_ATT,
    "proj_psum": {**ALL_ATT, "ffn0": (1, 4)},
    "xb_ready": {s: (1, 8) for s in ("att1", "att2", "att3")},
    "qk0_ready": PER_BATCH, "qkrest_ready": PER_BATCH, "qk1_ready": PER_BATCH, "qk2_ready": PER_BATCH,
    "v0_ready": PER_BATCH, "vrest_ready": PER_BATCH, "v1_ready": PER_BATCH, "v2_ready": PER_BATCH,
    "rows_psum": {s: (H[s], 8) for s in ATT},
    "max_done": {s: (H[s], 8) for s in ATT},
    "max_split": {s: (3, 8) for s in ATT},
    "max_ready": PER_BATCH,
    "maxt_psum": PER_BATCH,
    "maxt_ready": PER_BATCH,
    "cols_psum": {s: (H[s], 8) for s in ATT},
    "exp_ready": {s: (H[s], 8) for s in ATT},
    "low_by_dve": {s: (len(LOW_BY_DVE[s]), 8) for s in ATT},
    "low_by_pool": {s: (H[s] - len(LOW_BY_DVE[s]), 8) for s in ATT},
    "sums_done": {s: (H[s], 8) for s in ATT},
    "sums_read": PER_BATCH,
    "hid_psum": {"att1": (1, 8)},
    "hid_ready": {"att1": (1, 8)},
    "diff_ready": {"ffn0": (1, 4)},
    "mix_ready": {"ffn0": (1, 4)},
    "rk_psum": {"ffn0": (1, 4)},
    "gate_ready": {"ffn0": (1, 4)},
    "kact_ready": {"ffn0": (1, 4)},
    "gated": {"ffn0": (1, 4)},
    "s_psum": {"att3": (1, 8)},
    "smax_ready": {"att3": (1, 8)},
    "nbias_ready": {"att3": (1, 8)},
    "p_ready": {"att3": (1, 8)},
    "rden_ready": {"att3": (1, 8)},
    "pt_psum": {"att3": (1, 8)},
    "pt_ready": {"att3": (1, 8)},
    "pv_psum": {"att3": (1, 8)},
    "logits_psum": {s: (1, 1) for s in MOE},
    "route_steps": {"moe1": (20, 1), "moe2": (21, 1), "moe3": (17, 1)},
    "route_exp_in": {s: (1, 1) for s in MOE},
    "route_exp": {s: (1, 1) for s in MOE},
    "weights_ready": {s: (1, 1) for s in MOE},
    "wt_psum": {s: (1, 1) for s in ("moe2", "moe3")},
    "wt_ready": {s: (1, 1) for s in ("moe2", "moe3")},
    "bias_psum": {"moe2": (1, 1)},
    "bias_added": {"moe2": (1, 1)},
    "up_psum": {"moe1": (16, 4), "moe2": (16, 4), "moe3": (9, 4)},
    "gate_done": {"moe1": (16, 4), "moe3": (9, 4)},
    "h_ready": {"moe1": (16, 4), "moe2": (16, 4), "moe3": (9, 4)},
    "y_psum": {"moe1": (8, 4), "moe2": (8, 4), "moe3": (9, 4)},
    "zs_ready": {"moe3": (8, 4)},
}


class Counts:

    def __init__(self):
        self.base = {}
        for name, stages in EVENTS.items():
            total = 0
            for s in STAGES:
                self.base[name, s] = total
                per, steps = stages.get(s, (0, 0))
                total += per * steps

    def done(self, name, stage, b, k=None):
        per, steps = EVENTS[name][stage]
        base = self.base[name, stage]
        k = per - 1 if k is None else k
        if isinstance(b, int) and b == 0 and k < 0:
            return base
        if isinstance(b, int):
            if b < 0:
                return base
            if b >= steps:
                return base + per * steps
        return b * per + (base + k + 1)


def build(nc, args, out):
    counts = Counts()
    done = counts.done

    with ExitStack() as ctx:
        def sb(name, shape, dt=F32):
            return ctx.enter_context(nc.sbuf_tensor(name, shape, dt))

        sem = {name: ctx.enter_context(nc.semaphore(name)) for name in EVENTS}
        loaded = {name: ctx.enter_context(nc.semaphore(f"loaded_{name}")) for name in (*PACKS, "x", "ctx", "ctxt")}
        stack_in = [ctx.enter_context(nc.semaphore(f"stack_in{i}")) for i in range(3)]
        maxrow_in = [ctx.enter_context(nc.semaphore(f"maxrow_in{i}")) for i in range(3)]
        const_ready = ctx.enter_context(nc.semaphore("const_ready"))
        maxrow_ones = ctx.enter_context(nc.semaphore("maxrow_ones"))
        rows_padded = ctx.enter_context(nc.semaphore("rows_padded"))
        wt_out = ctx.enter_context(nc.semaphore("wt_out"))
        scale_in = [ctx.enter_context(nc.semaphore(f"scale_in{i}")) for i in range(2)]
        stored = ctx.enter_context(nc.semaphore("stored"))

        x_sb = sb("x_sb", [P, NT, D])
        ctx_sb = sb("ctx_sb", [P, NT, C])
        ctxt_sb = sb("ctxt_sb", [C, B * T])
        cols = {s: sum(n for _, n in PACKS[s]) for s in PACKS}
        pack = {s: sb(f"pack_{s}", [P, cols[s]]) for s in PACKS if s not in MOE}
        moe_pack = sb("pack_moe", [P, max(cols[s] for s in MOE)])
        for s in MOE:
            pack[s] = moe_pack

        def par(stage, name, rows=P):
            at = 0
            for n, w in PACKS[stage]:
                if n == name:
                    return pack[stage][0:rows, at:at + w]
                at += w
            raise KeyError(name)

        ident = par("consts", "ident")
        ident16 = sb("ident16", [P, P], BF16)
        index8 = par("consts", "index")

        stats = sb("stats", [P, NT, 6])
        moments = sb("moments", [P, NT, 2])
        var_eps = sb("var_eps", [P, 2, NT])
        rstd = sb("rstd", [P, 2, NT])
        neghalf = sb("neghalf", [P, 2, NT])
        z = sb("z", [P, NT, D])
        zt = sb("zt", [P, B, 1 + T])
        ct = sb("ct", [C, 2, T])

        qk = sb("qk", [P, 2, T])
        qk_rest = sb("qk_rest", [P, 2, T])
        qk_parts = sb("qk_parts", [P, 6, T], BF16)
        v = sb("v", [P, 2, D])
        v_rest = sb("v_rest", [P, 2, D])
        v_parts = [sb(f"v_parts{i}", [P, 2, 400], BF16) for i in range(3)]
        stack = [sb(f"stack{i}", [P, 16, 2, T], BF16) for i in range(3)]
        negmax = sb("negmax", [P, 2, 16])
        negmax_rest = sb("negmax_rest", [P, 2, 16])
        negmax_parts = sb("negmax_parts", [P, 2, 48], BF16)
        maxt = sb("maxt", [48, T], BF16)
        exps = sb("exps", [P, RING, 2 * T])
        high = sb("high", [P, RING, 2 * T], F16)
        low = sb("low", [P, RING, 2 * T], F16)
        osum = sb("osum", [P, 2, D])
        rden = sb("rden", [P, 2, 16])
        o = sb("o", [P, 2, D])
        ot = sb("ot", [P, T])
        hid = sb("hid", [P, 2, T])
        xb = sb("xb", [P, 2, D])

        lg = sb("lg", [P, NT, E])
        rt = [sb(f"rt{i}", [P, NT, E]) for i in range(3)]
        rs = [sb(f"rs{i}", [P, NT]) for i in range(4)]
        weights = sb("weights", [P, NT, E])
        wt = sb("wt", [E, B * T])
        gated = sb("gated", [P, 2, BLK])
        ht = sb("ht", [P, 2, 2, BLK])
        scale_sb = sb("scale_sb", [P, 2, BLK])
        zs = sb("zs", [P, 2, BLK])

        mixd = sb("mixd", [P, 2, T])
        mixr, mixk, gate, krelu, kact, gv = (exps[:, i, :] for i in range(RING))

        v2 = exps[:, 0:2, :].rearrange("p r c -> p (r c)")[:, 0:3 * 2 * D].rearrange("p (i t c) -> p i t c", i=3, t=2)
        prob = exps[:, 2, :].rearrange("p (t k) -> p t k", t=2)
        pt = exps[:, 3, :]
        nbias = sb("nbias", [P, 2])
        den3 = sb("den3", [P, 2, 2])
        rden3 = sb("rden3", [P, 2, 2])

        scratch = nc.dram_tensor("weights_t", (E, B * T), F32, kind="Internal").ap()

        ps = ctx.enter_context(nc.psum_tensor("ps", [P, 8, 512], F32))
        TURN, SIDE = 4, 7

        def parts_view(i, s, j):
            dv = D // H[s]
            w = 3 * dv + 1
            return v_parts[i][:, :, 0:H[s] * w].rearrange("p t (h w) -> p t h w", w=w)[:, :, :, j * dv:(j + 1) * dv]

        def sums_view(s, t):
            w = 3 * (D // H[s]) + 1
            return ps[:, 5 + t, 0:H[s] * w].rearrange("p (h w) -> p h w", w=w)

        def rows_at(s, u):
            n, span = H[s], ROW_SLOTS[s]
            i = u - FIRST_ROWS
            return range(i * n // span, (i + 1) * n // span) if 0 <= i < span else range(0)

        def last_rows(s):
            return FIRST_ROWS + ROW_SLOTS[s] - 1

        def low_index(s, u):
            mine = LOW_BY_DVE[s]
            return ("low_by_dve", mine.index(u)) if u in mine else ("low_by_pool", u - sum(i < u for i in mine))

        def slot(s, a, u):
            return (a * H[s] + u) % RING

        def wait_sums(eng, s, a, u):
            g = a * H[s] + u - RING
            if g >= 0:
                wait(eng, "sums_done", s, g // H[s], g % H[s])

        def valid(b):
            return 0 <= b < B

        def wait(eng, name, stage, b, k=None):
            value = done(name, stage, b, k)
            if isinstance(value, int) and value <= 0:
                return
            eng.wait_ge(sem[name], value)

        def before(stage):
            return STAGES[STAGES.index(stage) - 1] if STAGES.index(stage) else None

        def wait_x(eng, stage):
            prev = before(stage)
            if prev:
                eng.wait_ge(sem["x_updated"], done("x_updated", prev, 99))

        def stack_total(s, b):
            total = 0
            for st in ATT:
                for i in range(B):
                    if i % 3 == b % 3 and (ATT.index(st), i) <= (ATT.index(s), b):
                        total += 16 * len(SLOTS[st])
            return total

        def maxrow_total(s, b):
            total = 0
            for st in ATT:
                for i in range(B):
                    if i % 3 == b % 3 and (ATT.index(st), i) <= (ATT.index(s), b):
                        total += 16
            return total

        block = ctx.enter_context(nc.Block())

        @block.sync
        def _(sp):
            xin = args["x"].rearrange("(n p) d -> p n d", p=P)
            cin = args["ctx"].rearrange("(n p) d -> p n d", p=P)
            sp.dma_start(x_sb[:, :, :], xin).then_inc(loaded["x"], 16)
            sp.dma_start(ctx_sb[:, :, :], cin).then_inc(loaded["ctx"], 16)
            for s in ("consts", "att0", "ffn0", "att1"):
                sp.dma_start(pack[s][:, :], args[s]).then_inc(loaded[s], 16)
            sp.dma_start(ctxt_sb[:, :], args["ctxt"]).then_inc(loaded["ctxt"], 16)
            for s in ("moe1", "att2", "att3"):
                sp.dma_start(pack[s][:, 0:cols[s]], args[s]).then_inc(loaded[s], 16)

            for s in ATT:
                nh, dh = H[s], D // H[s]
                if s == "att2":
                    sp.wait_ge(sem["x_updated"], done("x_updated", "moe1", 99))
                    sp.dma_start(pack["moe2"][:, 0:cols["moe2"]], args["moe2"]).then_inc(loaded["moe2"], 16)
                for step in range(B + 1):
                    p, m = step, step - 1
                    if valid(p):
                        if p < 3:
                            sp.wait_ge(rows_padded, 1 + ATT.index(s))
                            sp.wait_ge(maxrow_ones, 3) if s == "att1" else None
                        wait(sp, "cols_psum", s, p - 3)
                        for j, (a, c) in enumerate(SLOTS[s]):
                            if j == 0:
                                wait(sp, "qk0_ready", s, p)
                            if j == 1:
                                wait(sp, "qk1_ready", s, p)
                            if j == 4:
                                wait(sp, "qk2_ready", s, p)
                            sp.dma_start(stack[p % 3][j * dh:(j + 1) * dh, 0:nh, :, :],
                                         qk_parts[:, a:3 + c + 1:3 + c - a, :]).then_inc(stack_in[p % 3], 16)
                    if valid(m):
                        wait(sp, "maxt_ready", s, m)
                        wait(sp, "cols_psum", s, m - 3)
                        sp.dma_start(stack[m % 3][MAXROW:MAXROW + 3, 0:nh, 0, :], maxt[0:3 * nh, :])\
                            .then_inc(maxrow_in[m % 3], 16)
            sp.wait_ge(sem["x_updated"], done("x_updated", "moe2", 99))
            sp.dma_start(pack["moe3"][:, 0:cols["moe3"]], args["moe3"]).then_inc(loaded["moe3"], 16)

            wait(sp, "wt_ready", "moe3", 0)
            sp.dma_start(scratch, wt[:, :]).then_inc(wt_out, 16)
            sp.wait_ge(wt_out, 16)
            def store(blk):
                wait(sp, "x_updated", "moe3", blk)
                sp.dma_start(out.rearrange("(n p) d -> p n d", p=P)[:, blk * BT:(blk + 1) * BT, :],
                             x_sb[:, blk * BT:(blk + 1) * BT, :]).then_inc(stored, 16)

            for blk in range(NBLK):
                for e in range(E):
                    n = blk * E + e
                    if n >= 2:
                        wait(sp, "zs_ready", "moe3", (n - 2) // E, (n - 2) % E)
                    src = scratch[e:e + 1, blk * BLK:(blk + 1) * BLK].broadcast_to([P, BLK])
                    sp.dma_start(scale_sb[:, n % 2, :], src).then_inc(scale_in[n % 2], 16)
                    if e == 1 and blk:
                        store(blk - 1)
            store(NBLK - 1)
            sp.wait_ge(stored, 16 * NBLK)

        @block.vector
        def _(dve):
            dve.memset(zt[:, :, 0:1], 0.0)
            dve.memset(neghalf[:, :, :], -0.5)
            dve.wait_ge(loaded["consts"], 16)
            dve.tensor_copy(ident16[:, :], ident).then_inc(const_ready, 1)
            dve.wait_ge(const_ready, 1)

            def take_stats(s, n, context):
                if n == 0:
                    if s == "att0":
                        dve.wait_ge(loaded["x"], 16)
                        dve.wait_ge(loaded["ctx"], 16)
                    wait_x(dve, s)
                wait(dve, "rstd_ready", s, n - 1)
                for t in range(2):
                    last = dve.bn_stats(stats[:, t, :], x_sb[:, 2 * n + t, :])
                if context:
                    for t in range(2):
                        last = dve.bn_stats(stats[:, 2 + t, :], ctx_sb[:, 2 * n + t, :])
                last.then_inc(sem["stats_taken"], 1)
                wait(dve, "stats_taken", s, n)
                for t in range(4 if context else 2):
                    last = dve.bn_aggr(moments[:, t, :], stats[:, t, :])
                last.then_inc(sem["moments_ready"], 1)

            def apply_norm(s, n, context):
                wait(dve, "rstd_ready", s, n)
                wait(dve, "moments_ready", s, n)
                if n == 0 and before(s):
                    wait(dve, "zt_psum", before(s), 99)
                wait(dve, "zt_psum", s, n - 1)
                for t in range(2):
                    last = dve.tensor_scalar(z[:, t, :], x_sb[:, 2 * n + t, :], moments[:, t, 0:1], rstd[:, 0, t:t + 1],
                                             ALU.subtract, ALU.mult)
                if context:
                    for t in range(2):
                        cn = ctx_sb[:, 2 * n + t, :]
                        last = dve.tensor_scalar(cn, cn, moments[:, 2 + t, 0:1], rstd[:, 0, 2 + t:3 + t],
                                                 ALU.subtract, ALU.mult)
                last.then_inc(sem["z_ready"], 1)

            def norm_all(s):
                wait_x(dve, s)
                wait(dve, "rstd_ready", before(s), 99)
                for t in range(NT):
                    last = dve.bn_stats(stats[:, t, :], x_sb[:, t, :])
                last.then_inc(sem["stats_taken"], 1)
                wait(dve, "stats_taken", s, 0)
                for t in range(NT):
                    last = dve.bn_aggr(moments[:, t, :], stats[:, t, :])
                last.then_inc(sem["moments_ready"], 1)
                wait(dve, "moments_ready", s, 0)
                wait(dve, "rstd_ready", s, 0)
                wait(dve, "zt_psum", before(s), 99)
                for t in range(NT):
                    last = dve.tensor_scalar(z[:, t, :], x_sb[:, t, :], moments[:, t, 0:1], rstd[:, 0, t:t + 1],
                                             ALU.subtract, ALU.mult)
                    if t % 4 == 3:
                        last.then_inc(sem["z_ready"], 1)

            def plus_norm(s):
                wait(dve, "zt_psum", s, 0)
                for t in range(NT):
                    last = dve.tensor_scalar(z[:, t, :], x_sb[:, t, :], moments[:, t, 0:1], rstd[:, 1, t:t + 1],
                                             ALU.subtract, ALU.mult)
                last.then_inc(sem["x_plus"], 1)
                wait(dve, "x_plus", s, 0)
                for t in range(0, NT, 4):
                    last = dve.tensor_tensor(x_sb[:, t:t + 4, :], x_sb[:, t:t + 4, :], z[:, t:t + 4, :], ALU.add)

            def attention(s):
                nh, dh = H[s], D // H[s]
                context = s == "att0"
                bias = s != "att0"
                dve.wait_ge(loaded[s], 16)
                if s != "att0":
                    prev = ATT[ATT.index(s) - 1]
                    wait(dve, "cols_psum", prev, 99)
                    wait(dve, "sums_done", prev, 99)
                if s == "att1":
                    for i in range(3):
                        dve.memset(stack[i][64:MAXROW, 0:8, 1, :], 0.0)
                w = 3 * dh + 1
                for i in range(3):
                    ones = v_parts[i][:, :, 0:nh * w].rearrange("p t (h w) -> p t h w", w=w)[:, :, :, 3 * dh:w]
                    last = dve.memset(ones, 1.0)
                last.then_inc(rows_padded, 1)

                def finish(d):
                    wait(dve, "sums_done", s, d)
                    for t in range(2):
                        dve.tensor_reduce(osum[:, t, :].rearrange("p (h c) -> p h c", h=nh),
                                          sums_view(s, t)[:, :, 0:3 * dh].rearrange("p h (j c) -> p h c j", j=3),
                                          AX, ALU.add)
                    for t in range(2):
                        last = dve.reciprocal(rden[:, t, 0:nh], sums_view(s, t)[:, :, 3 * dh])
                    last.then_inc(sem["sums_read"], 1)
                    wait(dve, "sums_read", s, d)
                    wait(dve, "ot_psum", s, d - 1)
                    for t in range(2):
                        last = dve.tensor_tensor(o[:, t, :].rearrange("p (h c) -> p h c", h=nh),
                                                 osum[:, t, :].rearrange("p (h c) -> p h c", h=nh),
                                                 rden[:, t, 0:nh].unsqueeze(2).to_broadcast([P, nh, dh]), ALU.mult)
                    last.then_inc(sem["o_ready"], 1)

                def split_max(m):
                    wait(dve, "max_done", s, m)
                    wait(dve, "maxt_psum", s, m - 1)
                    parts = [negmax_parts[:, :, j * nh:(j + 1) * nh] for j in range(3)]
                    whole, rest = negmax[:, :, 0:nh], negmax_rest[:, :, 0:nh]
                    dve.tensor_copy(parts[0], whole).then_inc(sem["max_split"], 1)
                    wait(dve, "max_split", s, m, 0)
                    dve.tensor_tensor(rest, whole, parts[0], ALU.subtract).then_inc(sem["max_split"], 1)
                    wait(dve, "max_split", s, m, 1)
                    dve.tensor_copy(parts[1], rest).then_inc(sem["max_split"], 1)
                    wait(dve, "max_split", s, m, 2)
                    dve.tensor_tensor(parts[2], rest, parts[1], ALU.subtract).then_inc(sem["max_ready"], 1)

                def residual(d):
                    wait(dve, "proj_psum", s, d)
                    if bias:
                        wait(dve, "xb_ready", s, d)
                    base = xb[:, :, :] if bias else x_sb[:, 2 * d:2 * d + 2, :]
                    bank = SIDE if s == "att1" else TURN
                    dve.tensor_tensor(x_sb[:, 2 * d:2 * d + 2, :],
                                      ps[:, bank, 0:2 * D].rearrange("p (t c) -> p t c", t=2), base, ALU.add)\
                        .then_inc(sem["x_updated"], 1)

                by_head = "p t (h c) -> p t h c"
                take_stats(s, 0, context)
                apply_norm(s, 0, context)
                for step in range(B + 3):
                    p, m, a, d, n = step, step - 1, step - 2, step - 3, step + 1
                    for u in range(nh):
                        if u == 0 and valid(n):
                            take_stats(s, n, context)
                        if u == 0 and valid(d):
                            finish(d)
                        if valid(m):
                            for h in rows_at(s, u):
                                wait(dve, "rows_psum", s, m, h)
                                dve.tensor_reduce(negmax[:, :, h:h + 1].rearrange("p t h -> p (t h)"),
                                                  ps[:, h % 2, :].rearrange("p (t k) -> p t k", t=2),
                                                  AX, ALU.max, negate=True).then_inc(sem["max_done"], 1)
                        if valid(a) and u in LOW_BY_DVE[s]:
                            i = slot(s, a, u)
                            wait(dve, "exp_ready", s, a, u)
                            dve.tensor_tensor(low[:, i, :], exps[:, i, :], high[:, i, :], ALU.subtract)\
                                .then_inc(sem["low_by_dve"], 1)
                        if valid(p) and u == 1:
                            wait(dve, "qk_ready", s, p)
                            if p > 0:
                                dve.wait_ge(stack_in[(p - 1) % 3], stack_total(s, p - 1))
                            dve.tensor_copy(qk_parts[:, 0:6:3, :], qk[:, :, :]).then_inc(sem["qk0_ready"], 1)
                        if valid(p) and u == 2:
                            wait(dve, "qkrest_ready", s, p)
                            dve.tensor_copy(qk_parts[:, 1:6:3, :], qk_rest[:, :, :]).then_inc(sem["qk1_ready"], 1)
                        if valid(p) and u == 5:
                            wait(dve, "v_psum", s, p)
                            wait(dve, "vrest_ready", s, p - 1)
                            vp = ps[:, SIDE, 0:2 * D].rearrange("p (t c) -> p t c", t=2)
                            if bias:
                                bv = par(s, "bv").unsqueeze(1).to_broadcast([P, 2, D])
                                dve.tensor_tensor(v[:, :, :], vp, bv, ALU.add).then_inc(sem["v_ready"], 1)
                            else:
                                dve.tensor_copy(v[:, :, :], vp).then_inc(sem["v_ready"], 1)
                            wait(dve, "v_ready", s, p)
                            wait(dve, "sums_done", s, p - 3)
                            dve.tensor_copy(parts_view(p % 3, s, 0), v[:, :, :].rearrange(by_head, h=nh))\
                                .then_inc(sem["v0_ready"], 1)
                        if valid(p) and u == 6:
                            wait(dve, "vrest_ready", s, p)
                            dve.tensor_copy(parts_view(p % 3, s, 1), v_rest[:, :, :].rearrange(by_head, h=nh))\
                                .then_inc(sem["v1_ready"], 1)
                        if valid(m) and u == last_rows(s):
                            split_max(m)
                        if valid(d) and u == (10 if s == "att1" else 6):
                            residual(d)
                        if valid(n) and u == nh - 2:
                            apply_norm(s, n, context)

            def token_mix():
                s = "ffn0"
                dve.wait_ge(loaded[s], 16)
                norm_all(s)
                for step in range(NBLK + 1):
                    a, m = step, step - 1
                    if a < NBLK:
                        this, prev = zt[:, 2 * a:2 * a + 2, 1:1 + T], zt[:, 2 * a:2 * a + 2, 0:T]
                        wait(dve, "zt_ready", s, 0, a)
                        wait(dve, "mix_ready", s, a - 1)
                        dve.tensor_tensor(mixd[:, :, :], this, prev, ALU.subtract).then_inc(sem["diff_ready"], 1)
                        wait(dve, "diff_ready", s, a)
                        wait(dve, "rk_psum", s, a - 1)
                        for name, mix in (("muk", mixk), ("mur", mixr)):
                            last = dve.scalar_tensor_tensor(out=mix[:, :].rearrange("p (b t) -> p b t", b=2),
                                                            in0=mixd[:, :, :], scalar=par(s, name), in1=prev,
                                                            op0=ALU.mult, op1=ALU.add)
                        last.then_inc(sem["mix_ready"], 1)
                    if m >= 0:
                        wait(dve, "proj_psum", s, m)
                        wait(dve, "x_updated", s, m - 1)
                        dve.tensor_tensor(gv[:, :], ps[:, 6, :], gate[:, :], ALU.mult).then_inc(sem["gated"], 1)
                        wait(dve, "gated", s, m)
                        xm = x_sb[:, BT * m:BT * m + BT, :]
                        dve.tensor_tensor(xm, xm, gv[:, :].rearrange("p (t c) -> p t c", t=BT), ALU.add)\
                            .then_inc(sem["x_updated"], 1)

            def single_head():
                s = "att3"
                dve.wait_ge(loaded[s], 16)
                norm_all(s)
                for step in range(B + 2):
                    p, m, d = step, step - 1, step - 2
                    if valid(m):
                        wait(dve, "s_psum", s, m)
                        dve.tensor_reduce(negmax[:, :, 0:1].rearrange("p t h -> p (t h)"),
                                          ps[:, 2, :].rearrange("p (t k) -> p t k", t=2), AX, ALU.max, negate=True)\
                            .then_inc(sem["smax_ready"], 1)
                    if valid(p):
                        wait(dve, "v_psum", s, p)
                        wait(dve, "pv_psum", s, p - 3)
                        bv = par(s, "bv").unsqueeze(1).to_broadcast([P, 2, D])
                        dve.tensor_tensor(v2[:, p % 3, :, :], ps[:, 1, 0:2 * D].rearrange("p (t c) -> p t c", t=2), bv,
                                          ALU.add).then_inc(sem["v_ready"], 1)
                    if valid(d):
                        wait(dve, "rden_ready", s, d)
                        wait(dve, "pv_psum", s, d)
                        wait(dve, "ot_psum", s, d - 1)
                        for t in range(2):
                            last = dve.tensor_scalar(o[:, t, :], ps[:, 4, t * D:(t + 1) * D], rden3[:, d % 2, t:t + 1], None,
                                                     ALU.mult)
                        last.then_inc(sem["o_ready"], 1)
                    if valid(m):
                        wait(dve, "p_ready", s, m)
                        dve.reciprocal(rden3[:, m % 2, :], den3[:, m % 2, :]).then_inc(sem["rden_ready"], 1)
                    if valid(d):
                        wait(dve, "proj_psum", s, d)
                        wait(dve, "xb_ready", s, d)
                        dve.tensor_tensor(x_sb[:, 2 * d:2 * d + 2, :], ps[:, 6, 0:2 * D].rearrange("p (t c) -> p t c", t=2),
                                          xb[:, :, :], ALU.add).then_inc(sem["x_updated"], 1)

            def route(s):
                k = [0]

                def chain(ins):
                    ins.then_inc(sem["route_steps"], 1)
                    wait(dve, "route_steps", s, 0, k[0])
                    k[0] += 1

                def over(a):
                    return a.unsqueeze(2).to_broadcast([P, NT, E])

                idx = index8.unsqueeze(1).to_broadcast([P, NT, E])
                lp = ps[:, SIDE, 0:NT * E].rearrange("p (n e) -> p n e", e=E)
                wait(dve, "logits_psum", s, 0)
                if s == "moe2":
                    chain(dve.tensor_tensor(lg[:, :, :], lp, par(s, "rb").unsqueeze(1).to_broadcast([P, NT, E]), ALU.add))
                else:
                    chain(dve.tensor_copy(lg[:, :, :], lp))
                chain(dve.tensor_reduce(rs[0][:, :], lg[:, :, :], AX, ALU.max))
                dve.tensor_tensor(rt[0][:, :, :], lg[:, :, :], over(rs[0][:, :]), ALU.subtract).then_inc(sem["route_exp_in"], 1)
                wait(dve, "route_exp", s, 0)
                e_all = lg
                chain(dve.tensor_reduce(rs[0][:, :], e_all[:, :, :], AX, ALU.add))
                chain(dve.reciprocal(rs[3][:, :], rs[0][:, :]))
                src = e_all
                for r in range(2):
                    chain(dve.tensor_reduce(rs[1][:, :], src[:, :, :], AX, ALU.max))
                    chain(dve.tensor_tensor(rt[1][:, :, :], src[:, :, :], over(rs[1][:, :]), ALU.is_equal))
                    chain(dve.tensor_tensor(rt[1][:, :, :], rt[1][:, :, :], idx, ALU.mult))
                    chain(dve.tensor_reduce(rs[2][:, :], rt[1][:, :, :], AX, ALU.min))
                    mask = rt[2] if r == 0 else rt[1]
                    chain(dve.tensor_tensor(mask[:, :, :], over(rs[2][:, :]), idx, ALU.is_equal))
                    if r == 0:
                        chain(dve.scalar_tensor_tensor(out=rt[0][:, :, :], in0=rt[2][:, :, :], scalar=-2.0,
                                                       in1=e_all[:, :, :], op0=ALU.mult, op1=ALU.add))
                        src = rt[0]
                chain(dve.tensor_tensor(rt[2][:, :, :], rt[2][:, :, :], rt[1][:, :, :], ALU.add))
                chain(dve.tensor_tensor(rt[2][:, :, :], rt[2][:, :, :], e_all[:, :, :], ALU.mult))
                if s == "moe3":
                    dve.tensor_tensor(weights[:, :, :], rt[2][:, :, :], over(rs[3][:, :]), ALU.mult)\
                        .then_inc(sem["weights_ready"], 1)
                else:
                    chain(dve.tensor_tensor(rt[2][:, :, :], rt[2][:, :, :], over(rs[3][:, :]), ALU.mult))
                    chain(dve.tensor_reduce(rs[0][:, :], rt[2][:, :, :], AX, ALU.add))
                    if s == "moe2":
                        chain(dve.tensor_scalar(rs[0][:, :], rs[0][:, :], 1e-8, None, ALU.max))
                    chain(dve.reciprocal(rs[1][:, :], rs[0][:, :]))
                    dve.tensor_tensor(weights[:, :, :], rt[2][:, :, :], over(rs[1][:, :]), ALU.mult)\
                        .then_inc(sem["weights_ready"], 1)
                assert k[0] == EVENTS["route_steps"][s][0]
                wait(dve, "weights_ready", s, 0)

            def mul_h(s, blk, i):
                wait(dve, "gate_done", s, blk, i)
                wait(dve, "y_psum", s, blk, i - 2)
                dve.tensor_tensor(ht[:, i % 2, 0, :], ps[:, 2 * (i % 2) + 1, :], gated[:, i % 2, :], ALU.mult)\
                    .then_inc(sem["h_ready"], 1)

            def add_y(s, blk, e):
                wait(dve, "y_psum", s, blk, e)
                wait(dve, "x_updated", s, blk, e - 1)
                for t in range(BT):
                    xt = x_sb[:, bass.ds(blk * BT + t, 1), :].rearrange("p a d -> p (a d)")
                    w = weights[:, bass.ds(blk * BT + t, 1), e:e + 1].rearrange("p a d -> p (a d)")
                    last = dve.scalar_tensor_tensor(out=xt, in0=ps[:, 4 + e % 2, t * D:(t + 1) * D],
                                                    scalar=w, in1=xt, op0=ALU.mult, op1=ALU.add)
                last.then_inc(sem["x_updated"], 1)

            def block_of(s, blk, first):
                for e in range(E):
                    if s == "moe1":
                        for c in range(2):
                            wait(dve, "gate_done", s, blk, 2 * e + c)
                            wait(dve, "y_psum", s, blk, e - 2)
                            dve.tensor_tensor(ht[:, e % 2, c, :], ps[:, 2 * c + 1, :], gated[:, c, :], ALU.mult)\
                                .then_inc(sem["h_ready"], 1)
                    if e >= 1:
                        add_y(s, blk, e - 1)
                    elif not first:
                        add_y(s, blk - 1, E - 1)

            def experts(s):
                dve.wait_ge(loaded[s], 16)
                norm_all(s)
                if s == "moe2":
                    plus_norm(s)
                route(s)
                if s == "moe3":
                    for blk in range(NBLK):
                        for i in range(E + 1):
                            if i >= 1:
                                mul_h(s, blk, i - 1)
                            if i < E:
                                n = blk * E + i
                                dve.wait_ge(scale_in[n % 2], 16 * (n // 2 + 1))
                                wait(dve, "up_psum", s, blk, i - 1) if i >= 2 else \
                                    wait(dve, "up_psum", s, blk - 1, E - 1 + i)
                                dve.tensor_tensor(zs[:, i % 2, :].rearrange("p (b t) -> p b t", b=2),
                                                  zt[:, 2 * blk:2 * blk + 2, 1:1 + T],
                                                  scale_sb[:, n % 2, :].rearrange("p (b t) -> p b t", b=2), ALU.mult)\
                                    .then_inc(sem["zs_ready"], 1)
                        mul_h(s, blk, E)
                        wait(dve, "y_psum", s, blk)
                        xs = x_sb[:, blk * BT:(blk + 1) * BT, :]
                        dve.tensor_tensor(xs, xs, ps[:, 4 + blk % 2, :].rearrange("p (t c) -> p t c", t=BT), ALU.add)\
                            .then_inc(sem["x_updated"], 1)
                    return
                if s == "moe2":
                    wait(dve, "bias_psum", s, 0)
                    for blk in range(NBLK):
                        xs = x_sb[:, blk * BT:(blk + 1) * BT, :]
                        last = dve.tensor_tensor(xs, xs, ps[:, blk, :].rearrange("p (t c) -> p t c", t=BT), ALU.add)
                    last.then_inc(sem["bias_added"], 1)
                    wait(dve, "bias_added", s, 0)
                block_of(s, 0, True)
                with dve.Fori(1, NBLK) as blk:
                    block_of(s, blk, False)
                add_y(s, NBLK - 1, E - 1)

            for s in STAGES:
                if s in ATT:
                    attention(s)
                elif s == "ffn0":
                    token_mix()
                elif s == "att3":
                    single_head()
                else:
                    experts(s)

        @block.gpsimd
        def _(pool):
            pool.wait_ge(const_ready, 1)

            def make_rstd(s, n, context):
                wait(pool, "moments_ready", s, n)
                wait(pool, "z_ready", s, n - 1)
                if n == 0 and before(s):
                    wait(pool, "z_ready", before(s), 99)
                wait(pool, "x_plus", "moe2", 0) if s == "att3" else None
                c = 2 if s in ATT else NT
                twice = s in ("att0", "moe2", "att3")
                a, b = (1.0 + EPS, EPS * EPS) if twice else (1.0, EPS)
                last = pool.tensor_scalar(var_eps[:, 0, 0:c], moments[:, 0:c, 1], a, b, ALU.mult, ALU.add)
                if context:
                    last = pool.tensor_scalar(var_eps[:, 0, 2:4], moments[:, 2:4, 1], 1.0, EPS, ALU.mult, ALU.add)
                    c = 4
                rows = 1
                if s == "moe2":
                    last = pool.tensor_scalar(var_eps[:, 1, :], moments[:, :, 1], 1.0, EPS, ALU.mult, ALU.add)
                    rows = 2
                last.then_inc(sem["var_ready"], 1)
                wait(pool, "var_ready", s, n)
                pool.tensor_tensor(rstd[:, 0:rows, 0:c], var_eps[:, 0:rows, 0:c], neghalf[:, 0:rows, 0:c], ALU.pow)\
                    .then_inc(sem["rstd_ready"], 1)

            def add_bias(s, d):
                wait_x(pool, s)
                wait(pool, "x_updated", s, d - 1)
                bo = par(s, "bo").unsqueeze(1).to_broadcast([P, 2, D])
                pool.tensor_tensor(xb[:, :, :], x_sb[:, 2 * d:2 * d + 2, :], bo, ALU.add).then_inc(sem["xb_ready"], 1)

            def make_low(s, a, u):
                i = slot(s, a, u)
                wait(pool, "exp_ready", s, a, u)
                pool.tensor_tensor(low[:, i, :], exps[:, i, :], high[:, i, :], ALU.subtract)\
                    .then_inc(sem["low_by_pool"], 1)

            by_head = "p t (h c) -> p t h c"
            for s in STAGES:
                pool.wait_ge(loaded[s], 16)
                if s in ATT:
                    nh = H[s]
                    context = s == "att0"
                    make_rstd(s, 0, context)
                    if s == "att0":
                        wait(pool, "rstd_ready", s, 0)
                        for i in range(3):
                            last = pool.memset(stack[i][MAXROW:MAXROW + 3, 0:8, 1, :], 1.0)
                        last.then_inc(maxrow_ones, 1)
                        pool.wait_ge(maxrow_ones, 1)
                    for step in range(B + 3):
                        p, m, a, d, n = step, step - 1, step - 2, step - 3, step + 1
                        for u in range(nh):
                            if u == 0 and valid(n):
                                make_rstd(s, n, context)
                            if valid(a) and u not in LOW_BY_DVE[s]:
                                make_low(s, a, u)
                            if u == 1 and valid(p):
                                wait(pool, "qk0_ready", s, p)
                                pool.tensor_tensor(qk_rest[:, :, :], qk[:, :, :], qk_parts[:, 0:6:3, :], ALU.subtract)\
                                    .then_inc(sem["qkrest_ready"], 1)
                            if u == 2 and valid(p):
                                wait(pool, "qk1_ready", s, p)
                                wait(pool, "qkrest_ready", s, p)
                                pool.tensor_tensor(qk_parts[:, 2:6:3, :], qk_rest[:, :, :], qk_parts[:, 1:6:3, :],
                                                   ALU.subtract).then_inc(sem["qk2_ready"], 1)
                            if u == 3 and valid(d) and s != "att0":
                                add_bias(s, d)
                            if u == 5 and valid(p):
                                wait(pool, "v0_ready", s, p)
                                pool.tensor_tensor(v_rest[:, :, :].rearrange(by_head, h=nh),
                                                   v[:, :, :].rearrange(by_head, h=nh), parts_view(p % 3, s, 0),
                                                   ALU.subtract).then_inc(sem["vrest_ready"], 1)
                            if u == 6 and valid(p):
                                wait(pool, "v1_ready", s, p)
                                wait(pool, "vrest_ready", s, p)
                                pool.tensor_tensor(parts_view(p % 3, s, 2), v_rest[:, :, :].rearrange(by_head, h=nh),
                                                   parts_view(p % 3, s, 1), ALU.subtract).then_inc(sem["v2_ready"], 1)
                    continue
                if s == "ffn0":
                    wait(pool, "low_by_pool", "att0", 99)
                    for i in range(3):
                        last = pool.memset(stack[i][64:MAXROW, 8:16, :, :], 0.0)
                    last.then_inc(maxrow_ones, 1)
                    pool.wait_ge(maxrow_ones, 2)
                    for i in range(3):
                        last = pool.memset(stack[i][MAXROW:MAXROW + 3, 8:16, 1, :], 1.0)
                    last.then_inc(maxrow_ones, 1)
                    pool.wait_ge(maxrow_ones, 3)
                make_rstd(s, 0, False)
                if s == "ffn0":
                    for a in range(NBLK):
                        wait(pool, "gate_ready", s, a)
                        wait(pool, "proj_psum", s, a - 1)
                        pool.tensor_tensor(kact[:, :], krelu[:, :], krelu[:, :], ALU.mult).then_inc(sem["kact_ready"], 1)
                if s == "att3":
                    for d in range(B):
                        add_bias(s, d)

        @block.scalar
        def _(act):
            act.wait_ge(const_ready, 1)

            def copy_turned(s, p):
                wait(act, "zt_psum", s, p)
                wait(act, "qk_psum", s, p - 1)
                dst = zt[:, 0, 1:1 + T]
                if s == "att0":
                    wait(act, "v_psum", s, p - 1)
                    nc.scalar.activation(dst, ps[:, TURN, 0:T], ACT.Identity, bias=par(s, "xb"), scale=par(s, "xg"))
                    last = nc.scalar.activation(ct[:, 0, :], ps[0:C, TURN, T:2 * T], ACT.Identity, bias=par(s, "cb", C),
                                                scale=par(s, "cg", C))
                else:
                    last = nc.scalar.activation(dst, ps[:, TURN, 0:T], ACT.Copy)
                last.then_inc(sem["zt_ready"], 1)

            def copy_all(s):
                for i in range(4):
                    wait(act, "zt_psum", s, 0, i)
                    dst, src = zt[:, 2 * i:2 * i + 2, 1:1 + T], ps[:, i, :].rearrange("p (b t) -> p b t", b=2)
                    if s in ("moe2", "att3"):
                        last = nc.scalar.activation(dst, src, ACT.Identity, bias=par(s, "xb"), scale=par(s, "xg"))
                    else:
                        last = nc.scalar.activation(dst, src, ACT.Copy)
                    last.then_inc(sem["zt_ready"], 1)

            def attention(s):
                nh = H[s]
                scale = float(D // nh) ** -0.5
                copy_turned(s, 0)
                for step in range(B + 3):
                    p, m, a, d, n = step, step - 1, step - 2, step - 3, step + 1
                    for u in range(nh):
                        if u == 3 and valid(d):
                            wait(act, "ot_psum", s, d)
                            wait(act, "hid_psum" if s == "att1" else "proj_psum", s, d - 1)
                            nc.scalar.activation(ot[:, :], ps[:, SIDE, 0:T], ACT.Copy).then_inc(sem["ot_ready"], 1)
                        if u == 6 and valid(d) and s == "att1":
                            wait(act, "hid_psum", s, d)
                            wait(act, "proj_psum", s, d - 1)
                            for c in range(2):
                                last = nc.scalar.activation(hid[:, c, :], ps[:, TURN, c * T:(c + 1) * T], ACT.Relu,
                                                            bias=par(s, "b1")[:, c:c + 1])
                            last.then_inc(sem["hid_ready"], 1)
                        if valid(a):
                            i = slot(s, a, u)
                            wait(act, "cols_psum", s, a, u)
                            wait_sums(act, s, a, u)
                            nc.scalar.activation(exps[:, i, :], ps[:, 2 + u % 2, :], ACT.Exp, scale=scale)
                            nc.scalar.activation(high[:, i, :], ps[:, 2 + u % 2, :], ACT.Exp, scale=scale)\
                                .then_inc(sem["exp_ready"], 1)
                        if u == 0 and valid(p):
                            wait(act, "qk_psum", s, p)
                            wait(act, "qkrest_ready", s, p - 1)
                            if s == "att0":
                                nc.scalar.activation(qk[:, :, :], ps[:, TURN, :].rearrange("p (a t) -> p a t", a=2),
                                                     ACT.Copy).then_inc(sem["qk_ready"], 1)
                            else:
                                nc.scalar.activation(qk[:, 0, :], ps[:, TURN, 0:T], ACT.Identity, bias=par(s, "bq"))
                                nc.scalar.activation(qk[:, 1, :], ps[:, TURN, T:2 * T], ACT.Identity, bias=par(s, "bk"))\
                                    .then_inc(sem["qk_ready"], 1)
                    if valid(m):
                        wait(act, "maxt_psum", s, m)
                        if m > 0:
                            act.wait_ge(maxrow_in[(m - 1) % 3], maxrow_total(s, m - 1))
                        nc.scalar.activation(maxt[0:3 * nh, :], ps[0:3 * nh, SIDE, 0:T // 2].bitcast(BF16), ACT.Copy)\
                            .then_inc(sem["maxt_ready"], 1)
                    if valid(n):
                        copy_turned(s, n)

            def token_mix():
                s = "ffn0"
                copy_all(s)
                for a in range(NBLK):
                    wait(act, "rk_psum", s, a)
                    wait(act, "gated", s, a - 1)
                    wait(act, "kact_ready", s, a - 1)
                    nc.scalar.activation(krelu[:, :], ps[:, 5, :], ACT.Relu)
                    nc.scalar.activation(gate[:, :], ps[:, 4, :], ACT.Sigmoid).then_inc(sem["gate_ready"], 1)

            def single_head():
                s = "att3"
                scale = float(D) ** -0.5
                copy_all(s)
                for step in range(B + 2):
                    p, m, d = step, step - 1, step - 2
                    if valid(p):
                        if p % 2 == 0:
                            wait(act, "zt_psum", s, 0, 4 + p // 2)
                            wait(act, "v_psum", s, p - 1)
                            nc.scalar.activation(ct[:, :, :], ps[0:C, 7, :].rearrange("p (b t) -> p b t", b=2),
                                                 ACT.Identity, bias=par(s, "cb", C), scale=par(s, "cg", C))\
                                .then_inc(sem["zt_ready"], 1)
                        wait(act, "qk_psum", s, p)
                        wait(act, "s_psum", s, p - 1)
                        nc.scalar.activation(qk[:, 0, :], ps[:, 0, 0:T], ACT.Identity, bias=par(s, "bq"))
                        nc.scalar.activation(qk[:, 1, :], ps[:, 0, T:2 * T], ACT.Identity, bias=par(s, "bk"))\
                            .then_inc(sem["qk_ready"], 1)
                    if valid(d):
                        wait(act, "pt_psum", s, d)
                        wait(act, "pv_psum", s, d - 1)
                        nc.scalar.activation(pt[:, :], ps[:, 3, :], ACT.Copy).then_inc(sem["pt_ready"], 1)
                    if valid(m):
                        wait(act, "smax_ready", s, m)
                        nc.scalar.activation(nbias[:, :], negmax[:, :, 0:1].rearrange("p t h -> p (t h)"), ACT.Copy,
                                             scale=scale).then_inc(sem["nbias_ready"], 1)
                        wait(act, "nbias_ready", s, m)
                        wait(act, "pt_psum", s, m - 1)
                        for t in range(2):
                            last = nc.scalar.activation(prob[:, t, :], ps[:, 2, t * T:(t + 1) * T], ACT.Exp,
                                                        bias=nbias[:, t:t + 1], scale=scale,
                                                        accum_out=den3[:, m % 2, t:t + 1])
                        last.then_inc(sem["p_ready"], 1)
                    if valid(d):
                        wait(act, "ot_psum", s, d)
                        wait(act, "proj_psum", s, d - 1)
                        nc.scalar.activation(ot[:, :], ps[:, 5, 0:T], ACT.Copy).then_inc(sem["ot_ready"], 1)

            def block_of(s, blk):
                for e in range(E):
                    for c in range(2):
                        k = 2 * e + c
                        wait(act, "up_psum", s, blk, k)
                        if s == "moe1":
                            wait(act, "h_ready", s, blk, k - 2)
                            nc.scalar.activation(gated[:, c, :], ps[:, 2 * c, :], ACT.Silu).then_inc(sem["gate_done"], 1)
                        else:
                            wait(act, "y_psum", s, blk, e - 2)
                            nc.scalar.activation(ht[:, e % 2, c, :], ps[:, 2 * (e % 2) + c, :], ACT.Gelu,
                                                 bias=par(s, "b1")[:, k:k + 1]).then_inc(sem["h_ready"], 1)

            def experts(s):
                copy_all(s)
                wait(act, "route_exp_in", s, 0)
                nc.scalar.activation(lg[:, :, :], rt[0][:, :, :], ACT.Exp).then_inc(sem["route_exp"], 1)
                if s != "moe1":
                    wait(act, "wt_psum", s, 0)
                    nc.scalar.activation(wt[:, :].rearrange("e (b t) -> e b t", b=4), ps[0:E, 0:4, :], ACT.Copy)\
                        .then_inc(sem["wt_ready"], 1)
                if s == "moe3":
                    for blk in range(NBLK):
                        for i in range(E + 1):
                            wait(act, "up_psum", s, blk, i)
                            wait(act, "h_ready", s, blk, i - 2) if i >= 2 else wait(act, "h_ready", s, blk - 1)
                            nc.scalar.activation(gated[:, i % 2, :], ps[:, 2 * (i % 2), :], ACT.Silu)\
                                .then_inc(sem["gate_done"], 1)
                    return
                block_of(s, 0)
                with act.Fori(1, NBLK) as blk:
                    block_of(s, blk)

            for s in STAGES:
                act.wait_ge(loaded[s], 16)
                if s in ATT:
                    attention(s)
                elif s == "ffn0":
                    token_mix()
                elif s == "att3":
                    single_head()
                else:
                    experts(s)

        @block.tensor
        def _(pe):
            pe.wait_ge(const_ready, 1)

            def turn(s, p):
                wait(pe, "z_ready", s, p)
                for t in range(2):
                    last = pe.transpose(ps[:, TURN, t * P:(t + 1) * P], z[:, t, :], ident)
                if s == "att0":
                    for t in range(2):
                        last = pe.transpose(ps[0:C, TURN, T + t * P:T + (t + 1) * P], ctx_sb[:, 2 * p + t, :], ident)
                last.then_inc(sem["zt_psum"], 1)

            def turn_all(s):
                for i in range(4):
                    wait(pe, "z_ready", s, 0, i)
                    for t in range(4):
                        last = pe.transpose(ps[:, i, t * P:(t + 1) * P], z[:, 4 * i + t, :], ident)
                    last.then_inc(sem["zt_psum"], 1)

            def turn_o(s, d, bank):
                wait(pe, "o_ready", s, d)
                for t in range(2):
                    last = pe.transpose(ps[:, bank, t * P:(t + 1) * P], o[:, t, :], ident)
                last.then_inc(sem["ot_psum"], 1)

            def project_o(s, d, bank):
                wait(pe, "ot_ready", s, d)
                for t in range(2):
                    last = pe.matmul(ps[:, bank, t * D:(t + 1) * D], ot[:, t * P:(t + 1) * P], par(s, "wo"),
                                     start=True, stop=True)
                last.then_inc(sem["proj_psum"], 1)

            def attention(s):
                nh, dh = H[s], D // H[s]
                w = 3 * dh + 1

                def rows(m, h):
                    st = stack[m % 3]
                    if h == 0:
                        pe.wait_ge(stack_in[m % 3], stack_total(s, m))
                    wait(pe, "max_done", s, m, h - 2) if h >= 2 else wait(pe, "max_done", s, m - 1, nh + h - 2)
                    for t in range(2):
                        last = pe.matmul(ps[:, h % 2, t * T:(t + 1) * T], st[0:MAXROW, h, 0, t * P:(t + 1) * P],
                                         st[0:MAXROW, h, 1, :], start=True, stop=True)
                    last.then_inc(sem["rows_psum"], 1)

                def columns(a, h):
                    st = stack[a % 3]
                    if h == 0:
                        pe.wait_ge(maxrow_in[a % 3], maxrow_total(s, a))
                        pe.wait_ge(maxrow_ones, 1 if s == "att0" else 3)
                    wait(pe, "exp_ready", s, a, h - 2) if h >= 2 else wait(pe, "exp_ready", s, a - 1, nh + h - 2)
                    for t in range(2):
                        last = pe.matmul(ps[:, 2 + h % 2, t * T:(t + 1) * T], st[0:MAXROW + 3, h, 1, t * P:(t + 1) * P],
                                         st[0:MAXROW + 3, h, 0, :], start=True, stop=True)
                    last.then_inc(sem["cols_psum"], 1)

                def sums(a, h):
                    name, k = low_index(s, h)
                    if h == 0:
                        wait(pe, "sums_read", s, a - 1)
                        wait(pe, "v2_ready", s, a)
                    wait(pe, "exp_ready", s, a, h)
                    wait(pe, name, s, a, k)
                    i = slot(s, a, h)
                    for t in range(2):
                        n = 0
                        for kt in range(2):
                            for part in (high, low):
                                last = pe.matmul(ps[:, 5 + t, h * w:(h + 1) * w],
                                                 part[:, i, kt * T + t * P:kt * T + (t + 1) * P],
                                                 v_parts[a % 3][:, kt, h * w:(h + 1) * w],
                                                 start=(n == 0), stop=(n == 3), skip_group_check=True)
                                n += 1
                    last.then_inc(sem["sums_done"], 1)

                turn(s, 0)
                for step in range(B + 3):
                    p, m, a, d, n = step, step - 1, step - 2, step - 3, step + 1
                    for u in range(nh):
                        if valid(a):
                            columns(a, u)
                        if u == 0 and valid(p):
                            wait(pe, "zt_ready", s, p)
                            kv = ct[:, 0, :] if s == "att0" else ctxt_sb[:, p * T:(p + 1) * T]
                            pe.matmul(ps[:, TURN, 0:T], par(s, "wq"), zt[:, 0, 1:1 + T], start=True, stop=True)
                            pe.matmul(ps[:, TURN, T:2 * T], par(s, "wk", C), kv, start=True, stop=True)\
                                .then_inc(sem["qk_psum"], 1)
                        if u == 2 and valid(d):
                            wait(pe, "maxt_ready", s, m - 1)
                            turn_o(s, d, SIDE)
                        if u == 4 and valid(d):
                            wait(pe, "qk_ready", s, p)
                            if s == "att1":
                                wait(pe, "ot_ready", s, d)
                                for c in range(2):
                                    last = pe.matmul(ps[:, TURN, c * T:(c + 1) * T], par(s, "w1")[:, c * P:(c + 1) * P],
                                                     ot[:, :], start=True, stop=True)
                                last.then_inc(sem["hid_psum"], 1)
                            else:
                                project_o(s, d, TURN)
                        if u == 4 and valid(p):
                            wait(pe, "ot_ready", s, d)
                            wait(pe, "maxt_ready", s, m - 1)
                            kv = ct[:, 0, :] if s == "att0" else ctxt_sb[:, p * T:(p + 1) * T]
                            for t in range(2):
                                last = pe.matmul(ps[:, SIDE, t * D:(t + 1) * D], kv[:, t * P:(t + 1) * P],
                                                 par(s, "wv", C), start=True, stop=True)
                            last.then_inc(sem["v_psum"], 1)
                        if u == 8 and valid(d) and s == "att1":
                            wait(pe, "hid_ready", s, d)
                            wait(pe, "v_ready", s, p)
                            for t in range(2):
                                for c in range(2):
                                    last = pe.matmul(ps[:, SIDE, t * D:(t + 1) * D], hid[:, c, t * P:(t + 1) * P],
                                                     par(s, "w2")[:, c * P:(c + 1) * P], start=(c == 0), stop=(c == 1))
                            last.then_inc(sem["proj_psum"], 1)
                        if valid(m):
                            for h in rows_at(s, u):
                                rows(m, h)
                        if valid(a) and u >= LAG:
                            sums(a, u - LAG)
                    if valid(m):
                        wait(pe, "max_ready", s, m)
                        wait(pe, "v_ready", s, p)
                        wait(pe, "x_updated", s, d) if s == "att1" else None
                        for t in range(2):
                            last = pe.transpose(ps[0:3 * nh, SIDE, t * 64:(t + 1) * 64].bitcast(BF16),
                                                negmax_parts[:, t, 0:3 * nh], ident16[:, :])
                        last.then_inc(sem["maxt_psum"], 1)
                    if valid(n):
                        wait(pe, "qk_ready", s, p)
                        wait(pe, "hid_ready", s, d) if s == "att1" else wait(pe, "x_updated", s, d)
                        turn(s, n)
                    if valid(a):
                        for h in range(nh - LAG, nh):
                            sums(a, h)

            def token_mix():
                s = "ffn0"
                turn_all(s)
                for a in range(NBLK):
                    wait(pe, "mix_ready", s, a)
                    wait(pe, "gate_ready", s, a - 1)
                    pe.matmul(ps[:, 5, :], par(s, "wk"), mixk[:, :], start=True, stop=True)
                    for t in range(BT):
                        last = pe.matmul(ps[:, 4, t * D:(t + 1) * D], mixr[:, t * P:(t + 1) * P], par(s, "wr"),
                                         start=True, stop=True)
                    last.then_inc(sem["rk_psum"], 1)
                    wait(pe, "kact_ready", s, a)
                    wait(pe, "gated", s, a - 1)
                    for t in range(BT):
                        last = pe.matmul(ps[:, 6, t * D:(t + 1) * D], kact[:, t * P:(t + 1) * P], par(s, "wv"),
                                         start=True, stop=True)
                    last.then_inc(sem["proj_psum"], 1)

            def single_head():
                s = "att3"
                turn_all(s)

                def turn_context(i):
                    wait(pe, "zt_ready", s, 0, 4 + i - 1)
                    for t in range(4):
                        last = pe.transpose(ps[0:C, 7, t * P:(t + 1) * P], ctx_sb[:, 4 * i + t, :], ident)
                    last.then_inc(sem["zt_psum"], 1)

                turn_context(0)
                for step in range(B + 2):
                    p, m, d = step, step - 1, step - 2
                    if valid(p):
                        wait(pe, "zt_ready", s, 0, 4 + p // 2)
                        wait(pe, "qk_ready", s, p - 1)
                        pe.matmul(ps[:, 0, 0:T], par(s, "wq"), zt[:, p, 1:1 + T], start=True, stop=True)
                        pe.matmul(ps[:, 0, T:2 * T], par(s, "wk", C), ct[:, p % 2, :], start=True, stop=True)\
                            .then_inc(sem["qk_psum"], 1)
                    if valid(d):
                        wait(pe, "p_ready", s, d)
                        wait(pe, "pt_ready", s, d - 1)
                        for kt in range(2):
                            for t in range(2):
                                last = pe.transpose(ps[:, 3, kt * T + t * P:kt * T + (t + 1) * P],
                                                    prob[:, t, kt * P:(kt + 1) * P], ident)
                        last.then_inc(sem["pt_psum"], 1)
                    if valid(p):
                        wait(pe, "v_ready", s, p - 1)
                        for t in range(2):
                            last = pe.matmul(ps[:, 1, t * D:(t + 1) * D], ct[:, p % 2, t * P:(t + 1) * P],
                                             par(s, "wv", C), start=True, stop=True)
                        last.then_inc(sem["v_psum"], 1)
                        if p % 2 == 1 and p < B - 1:
                            turn_context(p // 2 + 1)
                    if valid(d):
                        wait(pe, "pt_ready", s, d)
                        wait(pe, "v_ready", s, d)
                        wait(pe, "o_ready", s, d - 1)
                        for t in range(2):
                            for kt in range(2):
                                last = pe.matmul(ps[:, 4, t * D:(t + 1) * D], pt[:, kt * T + t * P:kt * T + (t + 1) * P],
                                                 v2[:, d % 3, kt, :], start=(kt == 0), stop=(kt == 1))
                        last.then_inc(sem["pv_psum"], 1)
                    if valid(p):
                        wait(pe, "qk_ready", s, p)
                        wait(pe, "p_ready", s, p - 1)
                        for t in range(2):
                            last = pe.matmul(ps[:, 2, t * T:(t + 1) * T], qk[:, 0, t * P:(t + 1) * P], qk[:, 1, :],
                                             start=True, stop=True)
                        last.then_inc(sem["s_psum"], 1)
                    if valid(d):
                        wait(pe, "ot_ready", s, d - 1)
                        turn_o(s, d, 5)
                        wait(pe, "x_updated", s, d - 1)
                        project_o(s, d, 6)

            def down(s, blk, e):
                wait(pe, "h_ready", s, blk, 2 * e + 1)
                wait(pe, "x_updated", s, blk, e - 2)
                for t in range(BT):
                    for c in range(2):
                        k = 2 * e + c
                        last = pe.matmul(ps[:, 4 + e % 2, t * D:(t + 1) * D], ht[:, e % 2, c, t * P:(t + 1) * P],
                                         par(s, "wd" if s == "moe1" else "w2")[:, k * P:(k + 1) * P],
                                         start=(c == 0), stop=(c == 1))
                last.then_inc(sem["y_psum"], 1)

            def block_of(s, blk, first):
                for e in range(E):
                    for c in range(2):
                        k = 2 * e + c
                        if s == "moe1":
                            wait(pe, "h_ready", s, blk, k - 2)
                            products = (("wg", 2 * c), ("wu", 2 * c + 1))
                        else:
                            wait(pe, "h_ready", s, blk, k - 4)
                            products = (("w1", 2 * (e % 2) + c),)
                        for name, bank in products:
                            last = pe.matmul(ps[:, bank, :], par(s, name)[:, k * P:(k + 1) * P],
                                             zt[:, bass.ds(2 * blk, 2), 1:1 + T], start=True, stop=True)
                        last.then_inc(sem["up_psum"], 1)
                    if e >= 1:
                        down(s, blk, e - 1)
                    elif not first:
                        down(s, blk - 1, E - 1)

            def experts(s):
                turn_all(s)
                for i in range(4):
                    wait(pe, "zt_ready", s, 0, i)
                    for t in range(4 * i, 4 * i + 4):
                        last = pe.matmul(ps[:, SIDE, t * E:(t + 1) * E], zt[:, t // 2, 1 + (t % 2) * P:1 + (t % 2 + 1) * P],
                                         par(s, "router"), start=True, stop=True)
                last.then_inc(sem["logits_psum"], 1)
                if s != "moe1":
                    wait(pe, "weights_ready", s, 0)
                    for t in range(NT):
                        last = pe.transpose(ps[0:E, t // 4, (t % 4) * P:(t % 4 + 1) * P], weights[:, t, :], ident)
                    last.then_inc(sem["wt_psum"], 1)
                    wait(pe, "wt_ready", s, 0)
                if s == "moe3":
                    for blk in range(NBLK):
                        for i in range(E + 2):
                            if i <= E:
                                w = E if i == 0 else i - 1
                                wait(pe, "h_ready", s, blk, i - 2) if i >= 2 else wait(pe, "h_ready", s, blk - 1)
                                if i:
                                    wait(pe, "zs_ready", s, blk, i - 1)
                                rhs = zs[:, (i - 1) % 2, :] if i else zt[:, 2 * blk:2 * blk + 2, 1:1 + T]
                                pe.matmul(ps[:, 2 * (i % 2), :], par(s, "w1")[:, w * P:(w + 1) * P], rhs,
                                          start=True, stop=True)
                                pe.matmul(ps[:, 2 * (i % 2) + 1, :], par(s, "w3")[:, w * P:(w + 1) * P], rhs,
                                          start=True, stop=True).then_inc(sem["up_psum"], 1)
                            if i >= 1:
                                q = i - 1
                                w = E if q == 0 else q - 1
                                wait(pe, "h_ready", s, blk, q)
                                if q == 0:
                                    wait(pe, "x_updated", s, blk - 2)
                                for t in range(BT):
                                    last = pe.matmul(ps[:, 4 + blk % 2, t * D:(t + 1) * D],
                                                     ht[:, q % 2, 0, t * P:(t + 1) * P],
                                                     par(s, "w2")[:, w * P:(w + 1) * P], start=(q == 0 and t == 0),
                                                     stop=(q == E), skip_group_check=True)
                                last.then_inc(sem["y_psum"], 1)
                    return
                if s == "moe2":
                    for t in range(NT):
                        last = pe.matmul(ps[:, t // BT, (t % BT) * D:(t % BT + 1) * D], wt[:, t * P:(t + 1) * P],
                                         par(s, "b2", E), start=True, stop=True)
                    last.then_inc(sem["bias_psum"], 1)
                    wait(pe, "bias_added", s, 0)
                block_of(s, 0, True)
                with pe.Fori(1, NBLK) as blk:
                    block_of(s, blk, False)
                down(s, NBLK - 1, E - 1)

            for s in STAGES:
                pe.wait_ge(loaded[s], 16)
                wait_x(pe, s)
                if s == "att1":
                    pe.wait_ge(loaded["ctxt"], 16)
                if s in ATT:
                    attention(s)
                elif s == "ffn0":
                    token_mix()
                elif s == "att3":
                    single_head()
                else:
                    experts(s)


def columns(inputs):
    f = {k: np.asarray(a) for k, a in inputs.items()}

    def col(v):
        return v[:, None]

    def row(v):
        return np.broadcast_to(v[None, :], (P, v.shape[0]))

    def heads_last(w, s):
        return w.reshape(w.shape[0], H[s], D // H[s]).transpose(0, 2, 1).reshape(w.shape[0], D)

    def att(s, name, bias=True):
        q, k = f[name + "Wq"], f[name + "Wk"]
        one = {"wq": q, "wk": k, "wv": f[name + "Wv"]}
        if s in H:
            one["wq"], one["wk"] = heads_last(q, s), heads_last(k, s)
        bq, bk = f[name + "bq"], f[name + "bk"]
        if s in H:
            bq, bk = heads_last(bq[None], s)[0], heads_last(bk[None], s)[0]
        one.update(bq=col(bq), bk=col(bk), bv=row(f[name + "bv"]))
        return one

    got = {}
    got["consts"] = {"ident": np.eye(P, dtype=np.float32), "index": row(np.arange(E, dtype=np.float32) - E)}
    n = "L0_xattn_"
    got["att0"] = {"wq": heads_last(f[n + "W_Q"], "att0"), "wk": heads_last(f[n + "W_K"], "att0"), "wv": f[n + "W_V"],
                   "xg": col(f[n + "ln_lat_g"]), "xb": col(f[n + "ln_lat_b"]),
                   "cg": col(f[n + "ln_in_g"]), "cb": col(f[n + "ln_in_b"]), "wo": f[n + "W_O"]}
    n = "L0_ffn_"
    got["ffn0"] = {"wr": f[n + "W_r"].T, "wk": f[n + "W_k"].T, "wv": f[n + "W_v"].T,
                   "mur": col(f[n + "mu_r"]), "muk": col(f[n + "mu_k"])}
    n = "L1_xattn_"
    got["att1"] = {**att("att1", n), "w1": f[n + "W1"], "b1": f[n + "b1"].reshape(2, P).T,
                   "w2": f[n + "W2"].reshape(2, P, D).transpose(1, 0, 2).reshape(P, 2 * D), "bo": row(f[n + "b2"])}
    n = "L1_ffn_"
    got["moe1"] = {"router": f[n + "router_w"].T, "wg": f[n + "w_gate"].transpose(2, 0, 1).reshape(P, -1),
                   "wu": f[n + "w_up"].transpose(2, 0, 1).reshape(P, -1),
                   "wd": f[n + "w_down"].reshape(E, D, 2, P).transpose(3, 0, 2, 1).reshape(P, -1)}
    n = "L2_xattn_"
    got["att2"] = {**att("att2", n), "wo": f[n + "Wo"], "bo": row(f[n + "bo"])}
    n = "L2_ffn_"
    got["moe2"] = {"router": f[n + "rW"], "rb": row(f[n + "rb"]), "xg": col(f[n + "ln_g"]), "xb": col(f[n + "ln_b"]),
                   "w1": f[n + "W1"].transpose(1, 0, 2).reshape(P, -1), "b1": f[n + "b1"].reshape(2 * E, P).T,
                   "w2": f[n + "W2"].reshape(E, 2, P, D).transpose(2, 0, 1, 3).reshape(P, -1), "b2": f[n + "b2"]}
    n = "L3_xattn_"
    got["att3"] = {**att("att3", n), "wo": f[n + "Wo"], "bo": row(f[n + "bo"]),
                   "xg": col(f[n + "ln1_g"]), "xb": col(f[n + "ln1_b"]),
                   "cg": col(f[n + "ln2_g"]), "cb": col(f[n + "ln2_b"])}
    n = "L3_ffn_"
    both = {w: np.concatenate([f[n + w], f[n + w + "s"]]).transpose(1, 0, 2).reshape(P, -1) for w in ("w1", "w2", "w3")}
    got["moe3"] = {"router": f[n + "gate_w"].T, **both}

    packed = {}
    for s, names in PACKS.items():
        a = np.zeros((P, sum(w for _, w in names)), np.float32)
        at = 0
        for name, w in names:
            part = got[s][name]
            a[0:part.shape[0], at:at + w] = part
            at += w
        packed[s] = a
    return packed


def kernel(**inputs):
    import concourse.bacc as bacc
    from concourse.bass_utils import run_bass_kernel_spmd

    x = np.asarray(inputs["x"])
    ctx = np.asarray(inputs["ctx_768"]).reshape(B * T, C)
    arrays = {"x": x.reshape(B * T, D), "ctx": ctx, "ctxt": ctx.T, **columns(inputs)}
    arrays = {f"in_{k}": np.ascontiguousarray(a) for k, a in arrays.items()}
    nc = bacc.Bacc("TRN2", target_bir_lowering=False, num_devices=1)
    args = {k[3:]: nc.dram_tensor(k, a.shape, mybir.dt.from_np(a.dtype), kind="ExternalInput").ap()
            for k, a in arrays.items()}
    out = nc.dram_tensor("out", (B * T, D), F32, kind="ExternalOutput").ap()
    build(nc, args, out)
    r = run_bass_kernel_spmd(nc, [arrays], core_ids=[0])
    return r.results[0]["out"].reshape(x.shape)
```

```python
from contextlib import ExitStack

import concourse.bass as bass
from concourse import mybir
import numpy as np

F32 = mybir.dt.float32
BF16 = mybir.dt.bfloat16
F16 = mybir.dt.float16
ALU = mybir.AluOpType
ACT = mybir.ActivationFunctionType
AX = mybir.AxisListType.X

P = 128
B = 8
T = 256
D = 128
C = 96
NT = B * T // P
EPS = 1e-5
NBLK = 4
BLK = B * T // NBLK
BT = BLK // P
E = 8

HEADS = {"att0": 8, "att1": 16, "att2": 8}
SLOTS = {
    "att0": [(0, 0), (0, 1), (1, 0), (1, 1), (0, 2), (2, 0)],
    "att1": [(0, 0), (0, 1), (1, 0), (1, 1), (0, 2), (2, 0), (1, 2), (2, 1), (2, 2)],
    "att2": [(0, 0), (0, 1), (1, 0), (1, 1), (0, 2), (2, 0)],
}
MAXROW = 96

PACKS = {
    "consts": [("ident", 128), ("index", 8)],
    "att0": [("wq", 128), ("wk", 128), ("wv", 128), ("xg", 1), ("xb", 1), ("cg", 1), ("cb", 1), ("wo", 128)],
    "ffn0": [("wr", 128), ("wk", 128), ("wv", 128), ("mur", 1), ("muk", 1)],
    "att1": [("wq", 128), ("wk", 128), ("wv", 128), ("bq", 1), ("bk", 1), ("bv", 128),
             ("w1", 256), ("b1", 2), ("w2", 256), ("bo", 128)],
    "moe1": [("router", 8), ("wg", 2048), ("wu", 2048), ("wd", 2048)],
    "att2": [("wq", 128), ("wk", 128), ("wv", 128), ("bq", 1), ("bk", 1), ("bv", 128), ("wo", 128), ("bo", 128)],
    "moe2": [("router", 8), ("rb", 8), ("xg", 1), ("xb", 1), ("w1", 2048), ("b1", 16), ("w2", 2048), ("b2", 128)],
    "att3": [("wq", 128), ("wk", 128), ("wv", 128), ("bq", 1), ("bk", 1), ("bv", 128), ("wo", 128), ("bo", 128),
             ("xg", 1), ("xb", 1), ("cg", 1), ("cb", 1)],
    "moe3": [("router", 8), ("w1", 9 * 128), ("w3", 9 * 128), ("w2", 9 * 128)],
}
STAGES = [s for s in PACKS if s != "consts"]
ATT = ("att0", "att1", "att2")
MOE = ("moe1", "moe2", "moe3")

FIRST_ROWS = 1
ROW_SLOTS = {"att0": 5, "att1": 11, "att2": 5}
LOW_BY_DVE = {"att0": (3, 6, 7), "att1": (6, 12, 13, 14, 15), "att2": (3, 6, 7)}
RING = 6
LAG = 3

H = HEADS
PER_BATCH = {s: (1, 8) for s in ATT}
ALL_ATT = {s: (1, 8) for s in (*ATT, "att3")}
AT_ONCE = ("ffn0", "moe1", "moe2", "att3", "moe3")
GROUPS = (range(0, NT - BT), range(NT - BT, NT))
ROUTE_STEPS = {"moe1": 20, "moe2": 21, "moe3": 17}
NORM_GROUPS = {s: (2 if s in MOE else 1, 1) for s in AT_ONCE}
EVENTS = {
    "stats_taken": {**PER_BATCH, **NORM_GROUPS},
    "moments_ready": {**PER_BATCH, **NORM_GROUPS},
    "var_ready": {**PER_BATCH, **NORM_GROUPS},
    "rstd_ready": {**PER_BATCH, **NORM_GROUPS},
    "z_ready": {**PER_BATCH, **{s: (4, 1) for s in AT_ONCE}},
    "zt_psum": {**PER_BATCH, **{s: (4, 1) for s in AT_ONCE}, "att3": (8, 1)},
    "zt_ready": {**PER_BATCH, **{s: (4, 1) for s in AT_ONCE}, "att3": (8, 1)},
    "x_plus": {"moe2": (2, 1)},
    "x_updated": {**{s: (1, 8) for s in STAGES}, "ffn0": (1, 4), "moe1": (8, 4), "moe2": (8, 4), "moe3": (1, 4)},
    "qk_psum": ALL_ATT,
    "v_psum": ALL_ATT,
    "qk_ready": ALL_ATT,
    "v_ready": ALL_ATT,
    "o_ready": ALL_ATT,
    "ot_psum": ALL_ATT,
    "ot_ready": ALL_ATT,
    "proj_psum": {**ALL_ATT, "ffn0": (1, 4)},
    "xb_ready": {s: (1, 8) for s in ("att1", "att2", "att3")},
    "qk0_ready": PER_BATCH, "qkrest_ready": PER_BATCH, "qk1_ready": PER_BATCH, "qk2_ready": PER_BATCH,
    "v0_ready": PER_BATCH, "vrest_ready": PER_BATCH, "v1_ready": PER_BATCH, "v2_ready": PER_BATCH,
    "rows_psum": {s: (H[s], 8) for s in ATT},
    "max_done": {s: (H[s], 8) for s in ATT},
    "max_split": {s: (3, 8) for s in ATT},
    "max_ready": PER_BATCH,
    "maxt_psum": PER_BATCH,
    "maxt_ready": PER_BATCH,
    "cols_psum": {s: (H[s], 8) for s in ATT},
    "exp_ready": {s: (H[s], 8) for s in ATT},
    "low_by_dve": {s: (len(LOW_BY_DVE[s]), 8) for s in ATT},
    "low_by_pool": {s: (H[s] - len(LOW_BY_DVE[s]), 8) for s in ATT},
    "sums_done": {s: (H[s], 8) for s in ATT},
    "sums_read": PER_BATCH,
    "hid_psum": {"att1": (1, 8)},
    "hid_ready": {"att1": (1, 8)},
    "diff_ready": {"ffn0": (1, 4)},
    "mix_ready": {"ffn0": (1, 4)},
    "rk_psum": {"ffn0": (1, 4)},
    "gate_ready": {"ffn0": (1, 4)},
    "kact_ready": {"ffn0": (1, 4)},
    "gated": {"ffn0": (1, 4)},
    "s_psum": {"att3": (1, 8)},
    "smax_ready": {"att3": (1, 8)},
    "nbias_ready": {"att3": (1, 8)},
    "p_ready": {"att3": (1, 8)},
    "rden_ready": {"att3": (1, 8)},
    "pt_psum": {"att3": (1, 8)},
    "pt_ready": {"att3": (1, 8)},
    "pv_psum": {"att3": (1, 8)},
    "logits_psum": {s: (2, 1) for s in MOE},
    "route_steps": {s: (2 * n, 1) for s, n in ROUTE_STEPS.items()},
    "route_exp_in": {s: (2, 1) for s in MOE},
    "route_exp": {s: (2, 1) for s in MOE},
    "weights_ready": {s: (2, 1) for s in MOE},
    "wt_psum": {s: (4, 1) for s in ("moe2", "moe3")},
    "wt_ready": {s: (4, 1) for s in ("moe2", "moe3")},
    "bias_psum": {"moe2": (4, 1)},
    "bias_added": {"moe2": (4, 1)},
    "up_psum": {"moe1": (16, 4), "moe2": (16, 4), "moe3": (9, 4)},
    "gate_done": {"moe1": (16, 4), "moe3": (9, 4)},
    "h_ready": {"moe1": (16, 4), "moe2": (16, 4), "moe3": (9, 4)},
    "y_psum": {"moe1": (8, 4), "moe2": (8, 4), "moe3": (9, 4)},
    "zs_ready": {"moe3": (8, 4)},
}


class Counts:

    def __init__(self):
        self.base = {}
        for name, stages in EVENTS.items():
            total = 0
            for s in STAGES:
                self.base[name, s] = total
                per, steps = stages.get(s, (0, 0))
                total += per * steps

    def done(self, name, stage, b, k=None):
        per, steps = EVENTS[name][stage]
        base = self.base[name, stage]
        k = per - 1 if k is None else k
        if isinstance(b, int) and b == 0 and k < 0:
            return base
        if isinstance(b, int):
            if b < 0:
                return base
            if b >= steps:
                return base + per * steps
        return b * per + (base + k + 1)


def build(nc, args, out):
    counts = Counts()
    done = counts.done

    with ExitStack() as ctx:
        def sb(name, shape, dt=F32):
            return ctx.enter_context(nc.sbuf_tensor(name, shape, dt))

        sem = {name: ctx.enter_context(nc.semaphore(name)) for name in EVENTS}
        loaded = {name: ctx.enter_context(nc.semaphore(f"loaded_{name}")) for name in (*PACKS, "x", "ctx", "ctxt")}
        stack_in = [ctx.enter_context(nc.semaphore(f"stack_in{i}")) for i in range(3)]
        maxrow_in = [ctx.enter_context(nc.semaphore(f"maxrow_in{i}")) for i in range(3)]
        const_ready = ctx.enter_context(nc.semaphore("const_ready"))
        maxrow_ones = ctx.enter_context(nc.semaphore("maxrow_ones"))
        rows_padded = ctx.enter_context(nc.semaphore("rows_padded"))
        wt_out = ctx.enter_context(nc.semaphore("wt_out"))
        scale_in = [ctx.enter_context(nc.semaphore(f"scale_in{i}")) for i in range(2)]
        stored = ctx.enter_context(nc.semaphore("stored"))

        x_sb = sb("x_sb", [P, NT, D])
        ctx_sb = sb("ctx_sb", [P, NT, C])
        ctxt_sb = sb("ctxt_sb", [C, B * T])
        cols = {s: sum(n for _, n in PACKS[s]) for s in PACKS}
        pack = {s: sb(f"pack_{s}", [P, cols[s]]) for s in PACKS if s not in MOE}
        moe_pack = sb("pack_moe", [P, max(cols[s] for s in MOE)])
        for s in MOE:
            pack[s] = moe_pack

        def par(stage, name, rows=P):
            at = 0
            for n, w in PACKS[stage]:
                if n == name:
                    return pack[stage][0:rows, at:at + w]
                at += w
            raise KeyError(name)

        ident = par("consts", "ident")
        ident16 = sb("ident16", [P, P], BF16)
        index8 = par("consts", "index")

        stats = sb("stats", [P, NT, 6])
        moments = sb("moments", [P, NT, 2])
        var_eps = sb("var_eps", [P, 2, NT])
        rstd = sb("rstd", [P, 2, NT])
        neghalf = sb("neghalf", [P, 2, NT])
        z = sb("z", [P, NT, D])
        zt = sb("zt", [P, B, 1 + T])
        ct = sb("ct", [C, 2, T])

        qk = sb("qk", [P, 2, T])
        qk_rest = sb("qk_rest", [P, 2, T])
        qk_parts = sb("qk_parts", [P, 6, T], BF16)
        v = sb("v", [P, 2, D])
        v_rest = sb("v_rest", [P, 2, D])
        v_parts = [sb(f"v_parts{i}", [P, 2, 400], BF16) for i in range(3)]
        stack = [sb(f"stack{i}", [P, 16, 2, T], BF16) for i in range(3)]
        negmax = sb("negmax", [P, 2, 16])
        negmax_rest = sb("negmax_rest", [P, 2, 16])
        negmax_parts = sb("negmax_parts", [P, 2, 48], BF16)
        maxt = sb("maxt", [48, T], BF16)
        exps = sb("exps", [P, RING, 2 * T])
        high = sb("high", [P, RING, 2 * T], F16)
        low = sb("low", [P, RING, 2 * T], F16)
        osum = sb("osum", [P, 2, D])
        rden = sb("rden", [P, 2, 16])
        o = sb("o", [P, 2, D])
        ot = sb("ot", [P, T])
        hid = sb("hid", [P, 2, T])
        xb = sb("xb", [P, 2, D])

        lg = sb("lg", [P, NT, E])
        rt = [sb(f"rt{i}", [P, NT, E]) for i in range(3)]
        rs = [sb(f"rs{i}", [P, NT]) for i in range(4)]
        weights = sb("weights", [P, NT, E])
        wt = sb("wt", [E, B * T])
        gated = sb("gated", [P, 2, BLK])
        ht = sb("ht", [P, 2, 2, BLK])
        scale_sb = sb("scale_sb", [P, 2, BLK])
        zs = sb("zs", [P, 2, BLK])

        mixd = sb("mixd", [P, 2, T])
        mixr, mixk, gate, krelu, kact, gv = (exps[:, i, :] for i in range(RING))

        v2 = exps[:, 0:2, :].rearrange("p r c -> p (r c)")[:, 0:3 * 2 * D].rearrange("p (i t c) -> p i t c", i=3, t=2)
        prob = exps[:, 2, :].rearrange("p (t k) -> p t k", t=2)
        pt = exps[:, 3, :]
        nbias = sb("nbias", [P, 2])
        den3 = sb("den3", [P, 2, 2])
        rden3 = sb("rden3", [P, 2, 2])

        scratch = nc.dram_tensor("weights_t", (E, B * T), F32, kind="Internal").ap()

        ps = ctx.enter_context(nc.psum_tensor("ps", [P, 8, 512], F32))
        TURN, SIDE = 4, 7

        def parts_view(i, s, j):
            dv = D // H[s]
            w = 3 * dv + 1
            return v_parts[i][:, :, 0:H[s] * w].rearrange("p t (h w) -> p t h w", w=w)[:, :, :, j * dv:(j + 1) * dv]

        def sums_view(s, t):
            w = 3 * (D // H[s]) + 1
            return ps[:, 5 + t, 0:H[s] * w].rearrange("p (h w) -> p h w", w=w)

        def rows_at(s, u):
            n, span = H[s], ROW_SLOTS[s]
            i = u - FIRST_ROWS
            return range(i * n // span, (i + 1) * n // span) if 0 <= i < span else range(0)

        def last_rows(s):
            return FIRST_ROWS + ROW_SLOTS[s] - 1

        def low_index(s, u):
            mine = LOW_BY_DVE[s]
            return ("low_by_dve", mine.index(u)) if u in mine else ("low_by_pool", u - sum(i < u for i in mine))

        def slot(s, a, u):
            return (a * H[s] + u) % RING

        def wait_sums(eng, s, a, u):
            g = a * H[s] + u - RING
            if g >= 0:
                wait(eng, "sums_done", s, g // H[s], g % H[s])

        def logits_at(tiles):
            return ps[:, 1 if tiles[0] in GROUPS[0] else SIDE, tiles[0] * E:(tiles[-1] + 1) * E]

        def turn_bank(s, i):
            return (0, 1, 0, 6)[i] if s in MOE else i

        def wt_bank(s, i):
            return (2, 3, SIDE, SIDE)[i] if s == "moe3" else SIDE

        def valid(b):
            return 0 <= b < B

        def wait(eng, name, stage, b, k=None):
            value = done(name, stage, b, k)
            if isinstance(value, int) and value <= 0:
                return
            eng.wait_ge(sem[name], value)

        def before(stage):
            return STAGES[STAGES.index(stage) - 1] if STAGES.index(stage) else None

        def after(stage):
            return STAGES[STAGES.index(stage) + 1]

        def wait_x(eng, stage):
            prev = before(stage)
            if prev:
                eng.wait_ge(sem["x_updated"], done("x_updated", prev, 99))

        def stack_total(s, b):
            total = 0
            for st in ATT:
                for i in range(B):
                    if i % 3 == b % 3 and (ATT.index(st), i) <= (ATT.index(s), b):
                        total += 16 * len(SLOTS[st])
            return total

        def maxrow_total(s, b):
            total = 0
            for st in ATT:
                for i in range(B):
                    if i % 3 == b % 3 and (ATT.index(st), i) <= (ATT.index(s), b):
                        total += 16
            return total

        block = ctx.enter_context(nc.Block())

        @block.sync
        def _(sp):
            xin = args["x"].rearrange("(n p) d -> p n d", p=P)
            cin = args["ctx"].rearrange("(n p) d -> p n d", p=P)
            sp.dma_start(x_sb[:, :, :], xin).then_inc(loaded["x"], 16)
            sp.dma_start(ctx_sb[:, :, :], cin).then_inc(loaded["ctx"], 16)
            for s in ("consts", "att0", "ffn0", "att1"):
                sp.dma_start(pack[s][:, :], args[s]).then_inc(loaded[s], 16)
            sp.dma_start(ctxt_sb[:, :], args["ctxt"]).then_inc(loaded["ctxt"], 16)
            for s in ("moe1", "att2", "att3"):
                sp.dma_start(pack[s][:, 0:cols[s]], args[s]).then_inc(loaded[s], 16)

            for s in ATT:
                nh, dh = H[s], D // H[s]
                if s == "att2":
                    sp.wait_ge(sem["x_updated"], done("x_updated", "moe1", 99))
                    sp.dma_start(pack["moe2"][:, 0:cols["moe2"]], args["moe2"]).then_inc(loaded["moe2"], 16)
                for step in range(B + 1):
                    p, m = step, step - 1
                    if valid(p):
                        if p < 3:
                            sp.wait_ge(rows_padded, 1 + ATT.index(s))
                            sp.wait_ge(maxrow_ones, 3) if s == "att1" else None
                        wait(sp, "cols_psum", s, p - 3)
                        for j, (a, c) in enumerate(SLOTS[s]):
                            if j == 0:
                                wait(sp, "qk0_ready", s, p)
                            if j == 1:
                                wait(sp, "qk1_ready", s, p)
                            if j == 4:
                                wait(sp, "qk2_ready", s, p)
                            sp.dma_start(stack[p % 3][j * dh:(j + 1) * dh, 0:nh, :, :],
                                         qk_parts[:, a:3 + c + 1:3 + c - a, :]).then_inc(stack_in[p % 3], 16)
                    if valid(m):
                        wait(sp, "maxt_ready", s, m)
                        wait(sp, "cols_psum", s, m - 3)
                        sp.dma_start(stack[m % 3][MAXROW:MAXROW + 3, 0:nh, 0, :], maxt[0:3 * nh, :])\
                            .then_inc(maxrow_in[m % 3], 16)
            sp.wait_ge(sem["x_updated"], done("x_updated", "moe2", 99))
            sp.dma_start(pack["moe3"][:, 0:cols["moe3"]], args["moe3"]).then_inc(loaded["moe3"], 16)

            def spread(first, last):
                at = slice(first * BLK, (last + 1) * BLK)
                wait(sp, "wt_ready", "moe3", 0, last)
                sp.dma_start(scratch[:, at], wt[:, at]).then_inc(wt_out, 16)

            spread(0, NBLK - 2)
            sp.wait_ge(wt_out, 16)
            def store(blk):
                wait(sp, "x_updated", "moe3", blk)
                sp.dma_start(out.rearrange("(n p) d -> p n d", p=P)[:, blk * BT:(blk + 1) * BT, :],
                             x_sb[:, blk * BT:(blk + 1) * BT, :]).then_inc(stored, 16)

            for blk in range(NBLK):
                if blk == 1:
                    spread(NBLK - 1, NBLK - 1)
                if blk == NBLK - 1:
                    sp.wait_ge(wt_out, 32)
                for e in range(E):
                    n = blk * E + e
                    if n >= 2:
                        wait(sp, "zs_ready", "moe3", (n - 2) // E, (n - 2) % E)
                    src = scratch[e:e + 1, blk * BLK:(blk + 1) * BLK].broadcast_to([P, BLK])
                    sp.dma_start(scale_sb[:, n % 2, :], src).then_inc(scale_in[n % 2], 16)
                    if e == 1 and blk:
                        store(blk - 1)
            store(NBLK - 1)
            sp.wait_ge(stored, 16 * NBLK)

        @block.vector
        def _(dve):
            dve.memset(zt[:, :, 0:1], 0.0)
            dve.memset(neghalf[:, :, :], -0.5)
            dve.wait_ge(loaded["consts"], 16)
            dve.tensor_copy(ident16[:, :], ident).then_inc(const_ready, 1)
            dve.wait_ge(const_ready, 1)

            def take_stats(s, n, context):
                if n == 0:
                    if s == "att0":
                        dve.wait_ge(loaded["x"], 16)
                        dve.wait_ge(loaded["ctx"], 16)
                    wait_x(dve, s)
                wait(dve, "rstd_ready", s, n - 1)
                for t in range(2):
                    last = dve.bn_stats(stats[:, t, :], x_sb[:, 2 * n + t, :])
                if context:
                    for t in range(2):
                        last = dve.bn_stats(stats[:, 2 + t, :], ctx_sb[:, 2 * n + t, :])
                last.then_inc(sem["stats_taken"], 1)
                wait(dve, "stats_taken", s, n)
                for t in range(4 if context else 2):
                    last = dve.bn_aggr(moments[:, t, :], stats[:, t, :])
                last.then_inc(sem["moments_ready"], 1)

            def apply_norm(s, n, context):
                wait(dve, "rstd_ready", s, n)
                wait(dve, "moments_ready", s, n)
                if n == 0 and before(s):
                    wait(dve, "zt_psum", before(s), 99)
                wait(dve, "zt_psum", s, n - 1)
                for t in range(2):
                    last = dve.tensor_scalar(z[:, t, :], x_sb[:, 2 * n + t, :], moments[:, t, 0:1], rstd[:, 0, t:t + 1],
                                             ALU.subtract, ALU.mult)
                if context:
                    for t in range(2):
                        cn = ctx_sb[:, 2 * n + t, :]
                        last = dve.tensor_scalar(cn, cn, moments[:, 2 + t, 0:1], rstd[:, 0, 2 + t:3 + t],
                                                 ALU.subtract, ALU.mult)
                last.then_inc(sem["z_ready"], 1)

            def stats_all(s, g=0, tiles=range(NT)):
                if tiles[-1] == NT - 1:
                    wait_x(dve, s)
                else:
                    wait(dve, "x_updated", before(s), tiles[-1] // 2)
                wait(dve, "rstd_ready", before(s), 99)
                for t in tiles:
                    last = dve.bn_stats(stats[:, t, :], x_sb[:, t, :])
                last.then_inc(sem["stats_taken"], 1)
                wait(dve, "stats_taken", s, 0, g)
                for t in tiles:
                    last = dve.bn_aggr(moments[:, t, :], stats[:, t, :])
                last.then_inc(sem["moments_ready"], 1)

            def apply_all(s, g=0, tiles=range(NT)):
                wait(dve, "moments_ready", s, 0, g)
                wait(dve, "rstd_ready", s, 0, g)
                wait(dve, "zt_psum", before(s), 99)
                for t in tiles:
                    last = dve.tensor_scalar(z[:, t, :], x_sb[:, t, :], moments[:, t, 0:1], rstd[:, 0, t:t + 1],
                                             ALU.subtract, ALU.mult)
                    if t % 4 == 3:
                        last.then_inc(sem["z_ready"], 1)

            def plus_norm(s, g):
                tiles = GROUPS[g]
                wait(dve, "zt_psum", s, 0, tiles[-1] // BT)
                for t in tiles:
                    last = dve.tensor_scalar(z[:, t, :], x_sb[:, t, :], moments[:, t, 0:1], rstd[:, 1, t:t + 1],
                                             ALU.subtract, ALU.mult)
                last.then_inc(sem["x_plus"], 1)
                wait(dve, "x_plus", s, 0, g)
                for t in range(tiles[0], tiles[-1], BT):
                    last = dve.tensor_tensor(x_sb[:, t:t + BT, :], x_sb[:, t:t + BT, :], z[:, t:t + BT, :], ALU.add)

            def attention(s):
                nh, dh = H[s], D // H[s]
                context = s == "att0"
                bias = s != "att0"
                nxt = after(s)
                dve.wait_ge(loaded[s], 16)
                if s != "att0":
                    prev = ATT[ATT.index(s) - 1]
                    wait(dve, "cols_psum", prev, 99)
                    wait(dve, "sums_done", prev, 99)
                if s == "att1":
                    for i in range(3):
                        dve.memset(stack[i][64:MAXROW, 0:8, 1, :], 0.0)
                w = 3 * dh + 1
                for i in range(3):
                    ones = v_parts[i][:, :, 0:nh * w].rearrange("p t (h w) -> p t h w", w=w)[:, :, :, 3 * dh:w]
                    last = dve.memset(ones, 1.0)
                last.then_inc(rows_padded, 1)

                def finish(d):
                    wait(dve, "sums_done", s, d)
                    for t in range(2):
                        dve.tensor_reduce(osum[:, t, :].rearrange("p (h c) -> p h c", h=nh),
                                          sums_view(s, t)[:, :, 0:3 * dh].rearrange("p h (j c) -> p h c j", j=3),
                                          AX, ALU.add)
                    for t in range(2):
                        last = dve.reciprocal(rden[:, t, 0:nh], sums_view(s, t)[:, :, 3 * dh])
                    last.then_inc(sem["sums_read"], 1)
                    wait(dve, "sums_read", s, d)
                    wait(dve, "ot_psum", s, d - 1)
                    for t in range(2):
                        last = dve.tensor_tensor(o[:, t, :].rearrange("p (h c) -> p h c", h=nh),
                                                 osum[:, t, :].rearrange("p (h c) -> p h c", h=nh),
                                                 rden[:, t, 0:nh].unsqueeze(2).to_broadcast([P, nh, dh]), ALU.mult)
                    last.then_inc(sem["o_ready"], 1)

                def split_max(m):
                    wait(dve, "max_done", s, m)
                    wait(dve, "maxt_psum", s, m - 1)
                    parts = [negmax_parts[:, :, j * nh:(j + 1) * nh] for j in range(3)]
                    whole, rest = negmax[:, :, 0:nh], negmax_rest[:, :, 0:nh]
                    dve.tensor_copy(parts[0], whole).then_inc(sem["max_split"], 1)
                    wait(dve, "max_split", s, m, 0)
                    dve.tensor_tensor(rest, whole, parts[0], ALU.subtract).then_inc(sem["max_split"], 1)
                    wait(dve, "max_split", s, m, 1)
                    dve.tensor_copy(parts[1], rest).then_inc(sem["max_split"], 1)
                    wait(dve, "max_split", s, m, 2)
                    dve.tensor_tensor(parts[2], rest, parts[1], ALU.subtract).then_inc(sem["max_ready"], 1)

                def residual(d):
                    wait(dve, "proj_psum", s, d)
                    if bias:
                        wait(dve, "xb_ready", s, d)
                    base = xb[:, :, :] if bias else x_sb[:, 2 * d:2 * d + 2, :]
                    bank = SIDE if s == "att1" else TURN
                    dve.tensor_tensor(x_sb[:, 2 * d:2 * d + 2, :],
                                      ps[:, bank, 0:2 * D].rearrange("p (t c) -> p t c", t=2), base, ALU.add)\
                        .then_inc(sem["x_updated"], 1)

                by_head = "p t (h c) -> p t h c"
                take_stats(s, 0, context)
                apply_norm(s, 0, context)
                for step in range(B + 3):
                    p, m, a, d, n = step, step - 1, step - 2, step - 3, step + 1
                    for u in range(nh):
                        if u == 0 and valid(n):
                            take_stats(s, n, context)
                        if u == 0 and valid(d):
                            finish(d)
                        if valid(m):
                            for h in rows_at(s, u):
                                wait(dve, "rows_psum", s, m, h)
                                dve.tensor_reduce(negmax[:, :, h:h + 1].rearrange("p t h -> p (t h)"),
                                                  ps[:, h % 2, :].rearrange("p (t k) -> p t k", t=2),
                                                  AX, ALU.max, negate=True).then_inc(sem["max_done"], 1)
                        if valid(a) and u in LOW_BY_DVE[s]:
                            i = slot(s, a, u)
                            wait(dve, "exp_ready", s, a, u)
                            dve.tensor_tensor(low[:, i, :], exps[:, i, :], high[:, i, :], ALU.subtract)\
                                .then_inc(sem["low_by_dve"], 1)
                        if valid(p) and u == 1:
                            wait(dve, "qk_ready", s, p)
                            if p > 0:
                                dve.wait_ge(stack_in[(p - 1) % 3], stack_total(s, p - 1))
                            dve.tensor_copy(qk_parts[:, 0:6:3, :], qk[:, :, :]).then_inc(sem["qk0_ready"], 1)
                        if valid(p) and u == 2:
                            wait(dve, "qkrest_ready", s, p)
                            dve.tensor_copy(qk_parts[:, 1:6:3, :], qk_rest[:, :, :]).then_inc(sem["qk1_ready"], 1)
                        if valid(p) and u == 5:
                            wait(dve, "v_psum", s, p)
                            wait(dve, "vrest_ready", s, p - 1)
                            vp = ps[:, SIDE, 0:2 * D].rearrange("p (t c) -> p t c", t=2)
                            if bias:
                                bv = par(s, "bv").unsqueeze(1).to_broadcast([P, 2, D])
                                dve.tensor_tensor(v[:, :, :], vp, bv, ALU.add).then_inc(sem["v_ready"], 1)
                            else:
                                dve.tensor_copy(v[:, :, :], vp).then_inc(sem["v_ready"], 1)
                            wait(dve, "v_ready", s, p)
                            wait(dve, "sums_done", s, p - 3)
                            dve.tensor_copy(parts_view(p % 3, s, 0), v[:, :, :].rearrange(by_head, h=nh))\
                                .then_inc(sem["v0_ready"], 1)
                        if valid(p) and u == 6:
                            wait(dve, "vrest_ready", s, p)
                            dve.tensor_copy(parts_view(p % 3, s, 1), v_rest[:, :, :].rearrange(by_head, h=nh))\
                                .then_inc(sem["v1_ready"], 1)
                        if valid(m) and u == last_rows(s):
                            split_max(m)
                        if valid(d) and u == (10 if s == "att1" else 6):
                            residual(d)
                        if valid(n) and u == nh - 2:
                            apply_norm(s, n, context)
                        if nxt in MOE and step == B + 1 and u == 1:
                            stats_all(nxt, 0, GROUPS[0])
                        if nxt in MOE and step == B + 1 and u == 4:
                            apply_all(nxt, 0, GROUPS[0])
                        if nxt in MOE and step == B + 2 and u == 1:
                            route_logits(nxt, 0)

            def token_mix():
                s = "ffn0"
                dve.wait_ge(loaded[s], 16)
                stats_all(s)
                apply_all(s)
                for step in range(NBLK + 1):
                    a, m = step, step - 1
                    if a < NBLK:
                        this, prev = zt[:, 2 * a:2 * a + 2, 1:1 + T], zt[:, 2 * a:2 * a + 2, 0:T]
                        wait(dve, "zt_ready", s, 0, a)
                        wait(dve, "mix_ready", s, a - 1)
                        dve.tensor_tensor(mixd[:, :, :], this, prev, ALU.subtract).then_inc(sem["diff_ready"], 1)
                        wait(dve, "diff_ready", s, a)
                        wait(dve, "rk_psum", s, a - 1)
                        for name, mix in (("muk", mixk), ("mur", mixr)):
                            last = dve.scalar_tensor_tensor(out=mix[:, :].rearrange("p (b t) -> p b t", b=2),
                                                            in0=mixd[:, :, :], scalar=par(s, name), in1=prev,
                                                            op0=ALU.mult, op1=ALU.add)
                        last.then_inc(sem["mix_ready"], 1)
                    if m >= 0:
                        wait(dve, "proj_psum", s, m)
                        wait(dve, "x_updated", s, m - 1)
                        dve.tensor_tensor(gv[:, :], ps[:, 6, :], gate[:, :], ALU.mult).then_inc(sem["gated"], 1)
                        wait(dve, "gated", s, m)
                        xm = x_sb[:, BT * m:BT * m + BT, :]
                        dve.tensor_tensor(xm, xm, gv[:, :].rearrange("p (t c) -> p t c", t=BT), ALU.add)\
                            .then_inc(sem["x_updated"], 1)

            def single_head():
                s = "att3"
                dve.wait_ge(loaded[s], 16)
                stats_all(s)
                apply_all(s)
                for step in range(B + 2):
                    p, m, d = step, step - 1, step - 2
                    if valid(m):
                        wait(dve, "s_psum", s, m)
                        dve.tensor_reduce(negmax[:, :, 0:1].rearrange("p t h -> p (t h)"),
                                          ps[:, 2, :].rearrange("p (t k) -> p t k", t=2), AX, ALU.max, negate=True)\
                            .then_inc(sem["smax_ready"], 1)
                    if step == B:
                        stats_all("moe3", 0, GROUPS[0])
                    if step == B + 1:
                        route_logits("moe3", 0)
                    if valid(p):
                        wait(dve, "v_psum", s, p)
                        wait(dve, "pv_psum", s, p - 3)
                        bv = par(s, "bv").unsqueeze(1).to_broadcast([P, 2, D])
                        dve.tensor_tensor(v2[:, p % 3, :, :], ps[:, 1, 0:2 * D].rearrange("p (t c) -> p t c", t=2), bv,
                                          ALU.add).then_inc(sem["v_ready"], 1)
                    if valid(d):
                        wait(dve, "rden_ready", s, d)
                        wait(dve, "pv_psum", s, d)
                        wait(dve, "ot_psum", s, d - 1)
                        for t in range(2):
                            last = dve.tensor_scalar(o[:, t, :], ps[:, 4, t * D:(t + 1) * D], rden3[:, d % 2, t:t + 1], None,
                                                     ALU.mult)
                        last.then_inc(sem["o_ready"], 1)
                    if valid(m):
                        wait(dve, "p_ready", s, m)
                        dve.reciprocal(rden3[:, m % 2, :], den3[:, m % 2, :]).then_inc(sem["rden_ready"], 1)
                    if valid(d):
                        wait(dve, "proj_psum", s, d)
                        wait(dve, "xb_ready", s, d)
                        dve.tensor_tensor(x_sb[:, 2 * d:2 * d + 2, :], ps[:, 6, 0:2 * D].rearrange("p (t c) -> p t c", t=2),
                                          xb[:, :, :], ALU.add).then_inc(sem["x_updated"], 1)
                    if step == B:
                        apply_all("moe3", 0, GROUPS[0])

            steps_taken = {}

            def router_of(s, g):
                ts = slice(GROUPS[g][0], GROUPS[g][-1] + 1)
                n = len(GROUPS[g])

                def chain(ins):
                    k = steps_taken.get(s, 0)
                    ins.then_inc(sem["route_steps"], 1)
                    wait(dve, "route_steps", s, 0, k)
                    steps_taken[s] = k + 1

                def over(a):
                    return a.unsqueeze(2).to_broadcast([P, n, E])

                return (chain, over, index8.unsqueeze(1).to_broadcast([P, n, E]), lg[:, ts, :],
                        [r[:, ts, :] for r in rt], [r[:, ts] for r in rs], weights[:, ts, :])

            def route_logits(s, g):
                chain, over, idx, lgg, rtg, rsg, wg = router_of(s, g)
                lp = logits_at(GROUPS[g]).rearrange("p (n e) -> p n e", e=E)
                wait(dve, "logits_psum", s, 0, g)
                if s == "moe2":
                    rb = par(s, "rb").unsqueeze(1).to_broadcast([P, len(GROUPS[g]), E])
                    chain(dve.tensor_tensor(lgg, lp, rb, ALU.add))
                else:
                    chain(dve.tensor_copy(lgg, lp))
                chain(dve.tensor_reduce(rsg[0], lgg, AX, ALU.max))
                dve.tensor_tensor(rtg[0], lgg, over(rsg[0]), ALU.subtract).then_inc(sem["route_exp_in"], 1)

            def route_pick(s, g):
                chain, over, idx, e_all, rtg, rsg, wg = router_of(s, g)
                wait(dve, "route_exp", s, 0, g)
                chain(dve.tensor_reduce(rsg[0], e_all, AX, ALU.add))
                chain(dve.reciprocal(rsg[3], rsg[0]))
                src = e_all
                for r in range(2):
                    chain(dve.tensor_reduce(rsg[1], src, AX, ALU.max))
                    chain(dve.tensor_tensor(rtg[1], src, over(rsg[1]), ALU.is_equal))
                    chain(dve.tensor_tensor(rtg[1], rtg[1], idx, ALU.mult))
                    chain(dve.tensor_reduce(rsg[2], rtg[1], AX, ALU.min))
                    chain(dve.tensor_tensor(rtg[2 - r], over(rsg[2]), idx, ALU.is_equal))
                    if r == 0:
                        chain(dve.scalar_tensor_tensor(out=rtg[0], in0=rtg[2], scalar=-2.0, in1=e_all,
                                                       op0=ALU.mult, op1=ALU.add))
                        src = rtg[0]

            def route_weights(s, g):
                chain, over, idx, e_all, rtg, rsg, wg = router_of(s, g)
                chain(dve.tensor_tensor(rtg[2], rtg[2], rtg[1], ALU.add))
                chain(dve.tensor_tensor(rtg[2], rtg[2], e_all, ALU.mult))
                if s == "moe3":
                    dve.tensor_tensor(wg, rtg[2], over(rsg[3]), ALU.mult).then_inc(sem["weights_ready"], 1)
                else:
                    chain(dve.tensor_tensor(rtg[2], rtg[2], over(rsg[3]), ALU.mult))
                    chain(dve.tensor_reduce(rsg[0], rtg[2], AX, ALU.add))
                    if s == "moe2":
                        chain(dve.tensor_scalar(rsg[0], rsg[0], 1e-8, None, ALU.max))
                    chain(dve.reciprocal(rsg[1], rsg[0]))
                    dve.tensor_tensor(wg, rtg[2], over(rsg[1]), ALU.mult).then_inc(sem["weights_ready"], 1)
                assert steps_taken[s] == (g + 1) * ROUTE_STEPS[s]
                wait(dve, "weights_ready", s, 0, g)

            def add_bias_of_block(i):
                s = "moe2"
                wait(dve, "bias_psum", s, 0, i)
                wait(dve, "x_updated", s, 0, i + 2)
                xs = x_sb[:, i * BT:(i + 1) * BT, :]
                dve.tensor_tensor(xs, xs, ps[:, 6, :].rearrange("p (t c) -> p t c", t=BT), ALU.add)\
                    .then_inc(sem["bias_added"], 1)
                wait(dve, "bias_added", s, 0, i)

            def beside_first_block(s, e):
                if e == 1:
                    if s == "moe2":
                        plus_norm(s, 1)
                    route_logits(s, 1)
                if e == 3:
                    route_pick(s, 1)
                if e == 4:
                    route_weights(s, 1)
                if s == "moe2" and e >= 4:
                    add_bias_of_block(e - 4)

            def mul_h(s, blk, i):
                wait(dve, "gate_done", s, blk, i)
                wait(dve, "y_psum", s, blk, i - 2)
                dve.tensor_tensor(ht[:, i % 2, 0, :], ps[:, 2 * (i % 2) + 1, :], gated[:, i % 2, :], ALU.mult)\
                    .then_inc(sem["h_ready"], 1)

            def add_y(s, blk, e):
                wait(dve, "y_psum", s, blk, e)
                wait(dve, "x_updated", s, blk, e - 1)
                for t in range(BT):
                    xt = x_sb[:, bass.ds(blk * BT + t, 1), :].rearrange("p a d -> p (a d)")
                    w = weights[:, bass.ds(blk * BT + t, 1), e:e + 1].rearrange("p a d -> p (a d)")
                    last = dve.scalar_tensor_tensor(out=xt, in0=ps[:, 4 + e % 2, t * D:(t + 1) * D],
                                                    scalar=w, in1=xt, op0=ALU.mult, op1=ALU.add)
                last.then_inc(sem["x_updated"], 1)

            def block_of(s, blk, first):
                for e in range(E):
                    if s == "moe1":
                        for c in range(2):
                            wait(dve, "gate_done", s, blk, 2 * e + c)
                            wait(dve, "y_psum", s, blk, e - 2)
                            dve.tensor_tensor(ht[:, e % 2, c, :], ps[:, 2 * c + 1, :], gated[:, c, :], ALU.mult)\
                                .then_inc(sem["h_ready"], 1)
                    if first and e == 0:
                        route_pick(s, 0)
                        route_weights(s, 0)
                    if e >= 1:
                        add_y(s, blk, e - 1)
                    elif not first:
                        add_y(s, blk - 1, E - 1)
                    if first:
                        beside_first_block(s, e)

            def experts(s):
                dve.wait_ge(loaded[s], 16)
                if s == "moe3":
                    route_pick(s, 0)
                    route_weights(s, 0)
                stats_all(s, 1, GROUPS[1])
                apply_all(s, 1, GROUPS[1])
                if s == "moe2":
                    plus_norm(s, 0)
                if s == "moe3":
                    for blk in range(NBLK):
                        for i in range(E + 1):
                            if i >= 1:
                                mul_h(s, blk, i - 1)
                            if i < E:
                                n = blk * E + i
                                dve.wait_ge(scale_in[n % 2], 16 * (n // 2 + 1))
                                wait(dve, "up_psum", s, blk, i - 1) if i >= 2 else \
                                    wait(dve, "up_psum", s, blk - 1, E - 1 + i)
                                dve.tensor_tensor(zs[:, i % 2, :].rearrange("p (b t) -> p b t", b=2),
                                                  zt[:, 2 * blk:2 * blk + 2, 1:1 + T],
                                                  scale_sb[:, n % 2, :].rearrange("p (b t) -> p b t", b=2), ALU.mult)\
                                    .then_inc(sem["zs_ready"], 1)
                            if blk == 0:
                                beside_first_block(s, i)
                        mul_h(s, blk, E)
                        wait(dve, "y_psum", s, blk)
                        xs = x_sb[:, blk * BT:(blk + 1) * BT, :]
                        dve.tensor_tensor(xs, xs, ps[:, 4 + blk % 2, :].rearrange("p (t c) -> p t c", t=BT), ALU.add)\
                            .then_inc(sem["x_updated"], 1)
                    return
                block_of(s, 0, True)
                with dve.Fori(1, NBLK) as blk:
                    block_of(s, blk, False)
                add_y(s, NBLK - 1, E - 1)

            for s in STAGES:
                if s in ATT:
                    attention(s)
                elif s == "ffn0":
                    token_mix()
                elif s == "att3":
                    single_head()
                else:
                    experts(s)

        @block.gpsimd
        def _(pool):
            pool.wait_ge(const_ready, 1)

            def make_rstd_all(s, g=0, tiles=range(NT)):
                wait(pool, "moments_ready", s, 0, g)
                wait(pool, "z_ready", before(s), 99)
                wait(pool, "x_plus", "moe2", 99) if s == "att3" else None
                ts = slice(tiles[0], tiles[-1] + 1)
                a, b = (1.0 + EPS, EPS * EPS) if s in ("moe2", "att3") else (1.0, EPS)
                last = pool.tensor_scalar(var_eps[:, 0, ts], moments[:, ts, 1], a, b, ALU.mult, ALU.add)
                rows = 1
                if s == "moe2":
                    last = pool.tensor_scalar(var_eps[:, 1, ts], moments[:, ts, 1], 1.0, EPS, ALU.mult, ALU.add)
                    rows = 2
                last.then_inc(sem["var_ready"], 1)
                wait(pool, "var_ready", s, 0, g)
                pool.tensor_tensor(rstd[:, 0:rows, ts], var_eps[:, 0:rows, ts], neghalf[:, 0:rows, ts], ALU.pow)\
                    .then_inc(sem["rstd_ready"], 1)

            def make_rstd(s, n, context):
                wait(pool, "moments_ready", s, n)
                wait(pool, "z_ready", s, n - 1)
                if n == 0 and before(s):
                    wait(pool, "z_ready", before(s), 99)
                c = 2
                a, b = (1.0 + EPS, EPS * EPS) if s == "att0" else (1.0, EPS)
                last = pool.tensor_scalar(var_eps[:, 0, 0:c], moments[:, 0:c, 1], a, b, ALU.mult, ALU.add)
                if context:
                    last = pool.tensor_scalar(var_eps[:, 0, 2:4], moments[:, 2:4, 1], 1.0, EPS, ALU.mult, ALU.add)
                    c = 4
                last.then_inc(sem["var_ready"], 1)
                wait(pool, "var_ready", s, n)
                pool.tensor_tensor(rstd[:, 0, 0:c], var_eps[:, 0, 0:c], neghalf[:, 0, 0:c], ALU.pow)\
                    .then_inc(sem["rstd_ready"], 1)

            def add_bias(s, d):
                wait_x(pool, s)
                wait(pool, "x_updated", s, d - 1)
                bo = par(s, "bo").unsqueeze(1).to_broadcast([P, 2, D])
                pool.tensor_tensor(xb[:, :, :], x_sb[:, 2 * d:2 * d + 2, :], bo, ALU.add).then_inc(sem["xb_ready"], 1)

            def make_low(s, a, u):
                i = slot(s, a, u)
                wait(pool, "exp_ready", s, a, u)
                pool.tensor_tensor(low[:, i, :], exps[:, i, :], high[:, i, :], ALU.subtract)\
                    .then_inc(sem["low_by_pool"], 1)

            by_head = "p t (h c) -> p t h c"
            for s in STAGES:
                pool.wait_ge(loaded[s], 16)
                if s in ATT:
                    nh = H[s]
                    context = s == "att0"
                    make_rstd(s, 0, context)
                    if s == "att0":
                        wait(pool, "rstd_ready", s, 0)
                        for i in range(3):
                            last = pool.memset(stack[i][MAXROW:MAXROW + 3, 0:8, 1, :], 1.0)
                        last.then_inc(maxrow_ones, 1)
                        pool.wait_ge(maxrow_ones, 1)
                    for step in range(B + 3):
                        p, m, a, d, n = step, step - 1, step - 2, step - 3, step + 1
                        for u in range(nh):
                            if u == 0 and valid(n):
                                make_rstd(s, n, context)
                            if valid(a) and u not in LOW_BY_DVE[s]:
                                make_low(s, a, u)
                            if u == 1 and valid(p):
                                wait(pool, "qk0_ready", s, p)
                                pool.tensor_tensor(qk_rest[:, :, :], qk[:, :, :], qk_parts[:, 0:6:3, :], ALU.subtract)\
                                    .then_inc(sem["qkrest_ready"], 1)
                            if u == 2 and valid(p):
                                wait(pool, "qk1_ready", s, p)
                                wait(pool, "qkrest_ready", s, p)
                                pool.tensor_tensor(qk_parts[:, 2:6:3, :], qk_rest[:, :, :], qk_parts[:, 1:6:3, :],
                                                   ALU.subtract).then_inc(sem["qk2_ready"], 1)
                            if u == 3 and after(s) in MOE and step == B + 1:
                                make_rstd_all(after(s), 0, GROUPS[0])
                            if u == 3 and valid(d) and s != "att0":
                                add_bias(s, d)
                            if u == 5 and valid(p):
                                wait(pool, "v0_ready", s, p)
                                pool.tensor_tensor(v_rest[:, :, :].rearrange(by_head, h=nh),
                                                   v[:, :, :].rearrange(by_head, h=nh), parts_view(p % 3, s, 0),
                                                   ALU.subtract).then_inc(sem["vrest_ready"], 1)
                            if u == 6 and valid(p):
                                wait(pool, "v1_ready", s, p)
                                wait(pool, "vrest_ready", s, p)
                                pool.tensor_tensor(parts_view(p % 3, s, 2), v_rest[:, :, :].rearrange(by_head, h=nh),
                                                   parts_view(p % 3, s, 1), ALU.subtract).then_inc(sem["v2_ready"], 1)
                    continue
                if s == "ffn0":
                    wait(pool, "low_by_pool", "att0", 99)
                    for i in range(3):
                        last = pool.memset(stack[i][64:MAXROW, 8:16, :, :], 0.0)
                    last.then_inc(maxrow_ones, 1)
                    pool.wait_ge(maxrow_ones, 2)
                    for i in range(3):
                        last = pool.memset(stack[i][MAXROW:MAXROW + 3, 8:16, 1, :], 1.0)
                    last.then_inc(maxrow_ones, 1)
                    pool.wait_ge(maxrow_ones, 3)
                if s in MOE:
                    make_rstd_all(s, 1, GROUPS[1])
                else:
                    make_rstd_all(s)
                if s == "ffn0":
                    for a in range(NBLK):
                        wait(pool, "gate_ready", s, a)
                        wait(pool, "proj_psum", s, a - 1)
                        pool.tensor_tensor(kact[:, :], krelu[:, :], krelu[:, :], ALU.mult).then_inc(sem["kact_ready"], 1)
                if s == "att3":
                    for d in range(B):
                        if d == B - 2:
                            make_rstd_all("moe3", 0, GROUPS[0])
                        add_bias(s, d)

        @block.scalar
        def _(act):
            act.wait_ge(const_ready, 1)

            def copy_turned(s, p):
                wait(act, "zt_psum", s, p)
                wait(act, "qk_psum", s, p - 1)
                dst = zt[:, 0, 1:1 + T]
                if s == "att0":
                    wait(act, "v_psum", s, p - 1)
                    nc.scalar.activation(dst, ps[:, TURN, 0:T], ACT.Identity, bias=par(s, "xb"), scale=par(s, "xg"))
                    last = nc.scalar.activation(ct[:, 0, :], ps[0:C, TURN, T:2 * T], ACT.Identity, bias=par(s, "cb", C),
                                                scale=par(s, "cg", C))
                else:
                    last = nc.scalar.activation(dst, ps[:, TURN, 0:T], ACT.Copy)
                last.then_inc(sem["zt_ready"], 1)

            def copy_all(s, chunks=range(4)):
                if s in MOE and chunks[0] == 0:
                    act.wait_ge(loaded[s], 16)
                for i in chunks:
                    wait(act, "zt_psum", s, 0, i)
                    wait(act, "qk_psum", before(s), 99) if s in MOE else None
                    dst = zt[:, 2 * i:2 * i + 2, 1:1 + T]
                    src = ps[:, turn_bank(s, i), :].rearrange("p (b t) -> p b t", b=2)
                    if s in ("moe2", "att3"):
                        last = nc.scalar.activation(dst, src, ACT.Identity, bias=par(s, "xb"), scale=par(s, "xg"))
                    else:
                        last = nc.scalar.activation(dst, src, ACT.Copy)
                    last.then_inc(sem["zt_ready"], 1)

            def attention(s):
                nh = H[s]
                scale = float(D // nh) ** -0.5
                copy_turned(s, 0)
                for step in range(B + 3):
                    p, m, a, d, n = step, step - 1, step - 2, step - 3, step + 1
                    for u in range(nh):
                        if u == 3 and valid(d):
                            wait(act, "ot_psum", s, d)
                            wait(act, "hid_psum" if s == "att1" else "proj_psum", s, d - 1)
                            nc.scalar.activation(ot[:, :], ps[:, SIDE, 0:T], ACT.Copy).then_inc(sem["ot_ready"], 1)
                        if u == 6 and valid(d) and s == "att1":
                            wait(act, "hid_psum", s, d)
                            wait(act, "proj_psum", s, d - 1)
                            for c in range(2):
                                last = nc.scalar.activation(hid[:, c, :], ps[:, TURN, c * T:(c + 1) * T], ACT.Relu,
                                                            bias=par(s, "b1")[:, c:c + 1])
                            last.then_inc(sem["hid_ready"], 1)
                        if valid(a):
                            i = slot(s, a, u)
                            wait(act, "cols_psum", s, a, u)
                            wait_sums(act, s, a, u)
                            nc.scalar.activation(exps[:, i, :], ps[:, 2 + u % 2, :], ACT.Exp, scale=scale)
                            nc.scalar.activation(high[:, i, :], ps[:, 2 + u % 2, :], ACT.Exp, scale=scale)\
                                .then_inc(sem["exp_ready"], 1)
                        if u == 0 and valid(p):
                            wait(act, "qk_psum", s, p)
                            wait(act, "qkrest_ready", s, p - 1)
                            if s == "att0":
                                nc.scalar.activation(qk[:, :, :], ps[:, TURN, :].rearrange("p (a t) -> p a t", a=2),
                                                     ACT.Copy).then_inc(sem["qk_ready"], 1)
                            else:
                                nc.scalar.activation(qk[:, 0, :], ps[:, TURN, 0:T], ACT.Identity, bias=par(s, "bq"))
                                nc.scalar.activation(qk[:, 1, :], ps[:, TURN, T:2 * T], ACT.Identity, bias=par(s, "bk"))\
                                    .then_inc(sem["qk_ready"], 1)
                    if valid(m):
                        wait(act, "maxt_psum", s, m)
                        if m > 0:
                            act.wait_ge(maxrow_in[(m - 1) % 3], maxrow_total(s, m - 1))
                        nc.scalar.activation(maxt[0:3 * nh, :], ps[0:3 * nh, SIDE, 0:T // 2].bitcast(BF16), ACT.Copy)\
                            .then_inc(sem["maxt_ready"], 1)
                    if valid(n):
                        copy_turned(s, n)
                    if after(s) in MOE and step == B + 1:
                        copy_all(after(s), range(3))
                    if after(s) in MOE and step == B + 2:
                        route_exp(after(s), 0)

            def route_exp(s, g):
                ts = slice(GROUPS[g][0], GROUPS[g][-1] + 1)
                wait(act, "route_exp_in", s, 0, g)
                nc.scalar.activation(lg[:, ts, :], rt[0][:, ts, :], ACT.Exp).then_inc(sem["route_exp"], 1)

            def copy_weights(s, i):
                wait(act, "wt_psum", s, 0, i)
                nc.scalar.activation(wt[:, i * BLK:(i + 1) * BLK], ps[0:E, wt_bank(s, i), :], ACT.Copy)\
                    .then_inc(sem["wt_ready"], 1)

            def beside_first_block(s, e):
                if e == 0 and s == "moe3":
                    for i in range(NBLK - 1):
                        copy_weights(s, i)
                if e == 0:
                    copy_all(s, range(3, 4))
                if e == 2:
                    route_exp(s, 1)
                if s == "moe2" and 3 <= e < 3 + NBLK:
                    copy_weights(s, e - 3)
                if s == "moe3" and e == 5:
                    copy_weights(s, NBLK - 1)

            def token_mix():
                s = "ffn0"
                copy_all(s)
                for a in range(NBLK):
                    wait(act, "rk_psum", s, a)
                    wait(act, "gated", s, a - 1)
                    wait(act, "kact_ready", s, a - 1)
                    nc.scalar.activation(krelu[:, :], ps[:, 5, :], ACT.Relu)
                    nc.scalar.activation(gate[:, :], ps[:, 4, :], ACT.Sigmoid).then_inc(sem["gate_ready"], 1)

            def single_head():
                s = "att3"
                scale = float(D) ** -0.5
                copy_all(s)
                for step in range(B + 2):
                    p, m, d = step, step - 1, step - 2
                    if valid(p):
                        if p % 2 == 0:
                            wait(act, "zt_psum", s, 0, 4 + p // 2)
                            wait(act, "v_psum", s, p - 1)
                            nc.scalar.activation(ct[:, :, :], ps[0:C, 7, :].rearrange("p (b t) -> p b t", b=2),
                                                 ACT.Identity, bias=par(s, "cb", C), scale=par(s, "cg", C))\
                                .then_inc(sem["zt_ready"], 1)
                        wait(act, "qk_psum", s, p)
                        wait(act, "s_psum", s, p - 1)
                        nc.scalar.activation(qk[:, 0, :], ps[:, 0, 0:T], ACT.Identity, bias=par(s, "bq"))
                        nc.scalar.activation(qk[:, 1, :], ps[:, 0, T:2 * T], ACT.Identity, bias=par(s, "bk"))\
                            .then_inc(sem["qk_ready"], 1)
                    if valid(d):
                        wait(act, "pt_psum", s, d)
                        wait(act, "pv_psum", s, d - 1)
                        nc.scalar.activation(pt[:, :], ps[:, 3, :], ACT.Copy).then_inc(sem["pt_ready"], 1)
                    if valid(m):
                        wait(act, "smax_ready", s, m)
                        nc.scalar.activation(nbias[:, :], negmax[:, :, 0:1].rearrange("p t h -> p (t h)"), ACT.Copy,
                                             scale=scale).then_inc(sem["nbias_ready"], 1)
                        wait(act, "nbias_ready", s, m)
                        wait(act, "pt_psum", s, m - 1)
                        for t in range(2):
                            last = nc.scalar.activation(prob[:, t, :], ps[:, 2, t * T:(t + 1) * T], ACT.Exp,
                                                        bias=nbias[:, t:t + 1], scale=scale,
                                                        accum_out=den3[:, m % 2, t:t + 1])
                        last.then_inc(sem["p_ready"], 1)
                    if valid(d):
                        wait(act, "ot_psum", s, d)
                        wait(act, "proj_psum", s, d - 1)
                        nc.scalar.activation(ot[:, :], ps[:, 5, 0:T], ACT.Copy).then_inc(sem["ot_ready"], 1)
                    if step == B:
                        copy_all("moe3", range(3))
                    if step == B + 1:
                        route_exp("moe3", 0)

            def block_of(s, blk, first=False):
                for e in range(E):
                    for c in range(2):
                        k = 2 * e + c
                        wait(act, "up_psum", s, blk, k)
                        if s == "moe1":
                            wait(act, "h_ready", s, blk, k - 2)
                            nc.scalar.activation(gated[:, c, :], ps[:, 2 * c, :], ACT.Silu).then_inc(sem["gate_done"], 1)
                        else:
                            wait(act, "y_psum", s, blk, e - 2)
                            nc.scalar.activation(ht[:, e % 2, c, :], ps[:, 2 * (e % 2) + c, :], ACT.Gelu,
                                                 bias=par(s, "b1")[:, k:k + 1]).then_inc(sem["h_ready"], 1)
                    if first:
                        beside_first_block(s, e)

            def experts(s):
                if s == "moe3":
                    for blk in range(NBLK):
                        for i in range(E + 1):
                            wait(act, "up_psum", s, blk, i)
                            wait(act, "h_ready", s, blk, i - 2) if i >= 2 else wait(act, "h_ready", s, blk - 1)
                            nc.scalar.activation(gated[:, i % 2, :], ps[:, 2 * (i % 2), :], ACT.Silu)\
                                .then_inc(sem["gate_done"], 1)
                            if blk == 0 and i < E:
                                beside_first_block(s, i)
                    return
                block_of(s, 0, True)
                with act.Fori(1, NBLK) as blk:
                    block_of(s, blk)

            for s in STAGES:
                act.wait_ge(loaded[s], 16)
                if s in ATT:
                    attention(s)
                elif s == "ffn0":
                    token_mix()
                elif s == "att3":
                    single_head()
                else:
                    experts(s)

        @block.tensor
        def _(pe):
            pe.wait_ge(const_ready, 1)

            def turn(s, p):
                wait(pe, "z_ready", s, p)
                for t in range(2):
                    last = pe.transpose(ps[:, TURN, t * P:(t + 1) * P], z[:, t, :], ident)
                if s == "att0":
                    for t in range(2):
                        last = pe.transpose(ps[0:C, TURN, T + t * P:T + (t + 1) * P], ctx_sb[:, 2 * p + t, :], ident)
                last.then_inc(sem["zt_psum"], 1)

            def turn_all(s, chunks=range(4)):
                for i in chunks:
                    wait(pe, "z_ready", s, 0, i)
                    if s in MOE and i == 2:
                        wait(pe, "zt_ready", s, 0, 0)
                    for t in range(4):
                        last = pe.transpose(ps[:, turn_bank(s, i), t * P:(t + 1) * P], z[:, 4 * i + t, :], ident)
                    last.then_inc(sem["zt_psum"], 1)

            def logits(s, g):
                pe.wait_ge(loaded[s], 16)
                wait(pe, "zt_ready", s, 0, GROUPS[g][-1] // 4)
                for t in GROUPS[g]:
                    last = pe.matmul(logits_at([t]), zt[:, t // 2, 1 + (t % 2) * P:1 + (t % 2 + 1) * P],
                                     par(s, "router"), start=True, stop=True)
                last.then_inc(sem["logits_psum"], 1)

            def turn_weights(s, i):
                wait(pe, "weights_ready", s, 0, 0 if i < NBLK - 1 else 1)
                if i and wt_bank(s, i) == wt_bank(s, i - 1):
                    wait(pe, "wt_ready", s, 0, i - 1)
                for t in range(BT):
                    last = pe.transpose(ps[0:E, wt_bank(s, i), t * P:(t + 1) * P], weights[:, i * BT + t, :], ident)
                last.then_inc(sem["wt_psum"], 1)

            def biases(s, i):
                wait(pe, "wt_ready", s, 0, i)
                wait(pe, "bias_added", s, 0, i - 1) if i else wait(pe, "zt_ready", s, 0)
                for t in range(BT):
                    last = pe.matmul(ps[:, 6, t * D:(t + 1) * D], wt[:, (i * BT + t) * P:(i * BT + t + 1) * P],
                                     par(s, "b2", E), start=True, stop=True)
                last.then_inc(sem["bias_psum"], 1)

            def beside_first_block(s, e):
                if e == 0 and s == "moe3":
                    for i in range(NBLK - 1):
                        turn_weights(s, i)
                if e == 0:
                    turn_all(s, range(3, 4))
                if e == 1:
                    if s == "moe3":
                        wait(pe, "wt_ready", s, 0, NBLK - 2)
                    logits(s, 1)
                if s == "moe2" and 3 <= e < 3 + NBLK:
                    wait(pe, "route_exp_in", s, 0, 1)
                    turn_weights(s, e - 3)
                if s == "moe2" and e >= 4:
                    biases(s, e - 4)
                if s == "moe3" and e == 5:
                    turn_weights(s, NBLK - 1)

            def turn_o(s, d, bank):
                wait(pe, "o_ready", s, d)
                for t in range(2):
                    last = pe.transpose(ps[:, bank, t * P:(t + 1) * P], o[:, t, :], ident)
                last.then_inc(sem["ot_psum"], 1)

            def project_o(s, d, bank):
                wait(pe, "ot_ready", s, d)
                for t in range(2):
                    last = pe.matmul(ps[:, bank, t * D:(t + 1) * D], ot[:, t * P:(t + 1) * P], par(s, "wo"),
                                     start=True, stop=True)
                last.then_inc(sem["proj_psum"], 1)

            def attention(s):
                nh, dh = H[s], D // H[s]
                w = 3 * dh + 1

                def rows(m, h):
                    st = stack[m % 3]
                    if h == 0:
                        pe.wait_ge(stack_in[m % 3], stack_total(s, m))
                    wait(pe, "max_done", s, m, h - 2) if h >= 2 else wait(pe, "max_done", s, m - 1, nh + h - 2)
                    for t in range(2):
                        last = pe.matmul(ps[:, h % 2, t * T:(t + 1) * T], st[0:MAXROW, h, 0, t * P:(t + 1) * P],
                                         st[0:MAXROW, h, 1, :], start=True, stop=True)
                    last.then_inc(sem["rows_psum"], 1)

                def columns(a, h):
                    st = stack[a % 3]
                    if h == 0:
                        pe.wait_ge(maxrow_in[a % 3], maxrow_total(s, a))
                        pe.wait_ge(maxrow_ones, 1 if s == "att0" else 3)
                    wait(pe, "exp_ready", s, a, h - 2) if h >= 2 else wait(pe, "exp_ready", s, a - 1, nh + h - 2)
                    for t in range(2):
                        last = pe.matmul(ps[:, 2 + h % 2, t * T:(t + 1) * T], st[0:MAXROW + 3, h, 1, t * P:(t + 1) * P],
                                         st[0:MAXROW + 3, h, 0, :], start=True, stop=True)
                    last.then_inc(sem["cols_psum"], 1)

                def sums(a, h):
                    name, k = low_index(s, h)
                    if h == 0:
                        wait(pe, "sums_read", s, a - 1)
                        wait(pe, "v2_ready", s, a)
                    wait(pe, "exp_ready", s, a, h)
                    wait(pe, name, s, a, k)
                    i = slot(s, a, h)
                    for t in range(2):
                        n = 0
                        for kt in range(2):
                            for part in (high, low):
                                last = pe.matmul(ps[:, 5 + t, h * w:(h + 1) * w],
                                                 part[:, i, kt * T + t * P:kt * T + (t + 1) * P],
                                                 v_parts[a % 3][:, kt, h * w:(h + 1) * w],
                                                 start=(n == 0), stop=(n == 3), skip_group_check=True)
                                n += 1
                    last.then_inc(sem["sums_done"], 1)

                turn(s, 0)
                for step in range(B + 3):
                    p, m, a, d, n = step, step - 1, step - 2, step - 3, step + 1
                    for u in range(nh):
                        if valid(a):
                            columns(a, u)
                        if u == 0 and valid(p):
                            wait(pe, "zt_ready", s, p)
                            kv = ct[:, 0, :] if s == "att0" else ctxt_sb[:, p * T:(p + 1) * T]
                            pe.matmul(ps[:, TURN, 0:T], par(s, "wq"), zt[:, 0, 1:1 + T], start=True, stop=True)
                            pe.matmul(ps[:, TURN, T:2 * T], par(s, "wk", C), kv, start=True, stop=True)\
                                .then_inc(sem["qk_psum"], 1)
                        if u == 2 and valid(d):
                            wait(pe, "maxt_ready", s, m - 1)
                            turn_o(s, d, SIDE)
                        if u == 4 and valid(d):
                            wait(pe, "qk_ready", s, p)
                            if s == "att1":
                                wait(pe, "ot_ready", s, d)
                                for c in range(2):
                                    last = pe.matmul(ps[:, TURN, c * T:(c + 1) * T], par(s, "w1")[:, c * P:(c + 1) * P],
                                                     ot[:, :], start=True, stop=True)
                                last.then_inc(sem["hid_psum"], 1)
                            else:
                                project_o(s, d, TURN)
                        if u == 4 and valid(p):
                            wait(pe, "ot_ready", s, d)
                            wait(pe, "maxt_ready", s, m - 1)
                            kv = ct[:, 0, :] if s == "att0" else ctxt_sb[:, p * T:(p + 1) * T]
                            for t in range(2):
                                last = pe.matmul(ps[:, SIDE, t * D:(t + 1) * D], kv[:, t * P:(t + 1) * P],
                                                 par(s, "wv", C), start=True, stop=True)
                            last.then_inc(sem["v_psum"], 1)
                        if u == 8 and valid(d) and s == "att1":
                            wait(pe, "hid_ready", s, d)
                            wait(pe, "v_ready", s, p)
                            for t in range(2):
                                for c in range(2):
                                    last = pe.matmul(ps[:, SIDE, t * D:(t + 1) * D], hid[:, c, t * P:(t + 1) * P],
                                                     par(s, "w2")[:, c * P:(c + 1) * P], start=(c == 0), stop=(c == 1))
                            last.then_inc(sem["proj_psum"], 1)
                        if valid(m):
                            for h in rows_at(s, u):
                                rows(m, h)
                        if valid(a) and u >= LAG:
                            sums(a, u - LAG)
                    if valid(m):
                        wait(pe, "max_ready", s, m)
                        wait(pe, "v_ready", s, p)
                        wait(pe, "x_updated", s, d) if s == "att1" else None
                        for t in range(2):
                            last = pe.transpose(ps[0:3 * nh, SIDE, t * 64:(t + 1) * 64].bitcast(BF16),
                                                negmax_parts[:, t, 0:3 * nh], ident16[:, :])
                        last.then_inc(sem["maxt_psum"], 1)
                    if valid(n):
                        wait(pe, "qk_ready", s, p)
                        wait(pe, "hid_ready", s, d) if s == "att1" else wait(pe, "x_updated", s, d)
                        turn(s, n)
                    if valid(a):
                        for h in range(nh - LAG, nh):
                            sums(a, h)
                    if after(s) in MOE and step == B + 1:
                        wait(pe, "max_done", s, 99)
                        turn_all(after(s), range(3))
                        logits(after(s), 0)

            def token_mix():
                s = "ffn0"
                turn_all(s)
                for a in range(NBLK):
                    wait(pe, "mix_ready", s, a)
                    wait(pe, "gate_ready", s, a - 1)
                    pe.matmul(ps[:, 5, :], par(s, "wk"), mixk[:, :], start=True, stop=True)
                    for t in range(BT):
                        last = pe.matmul(ps[:, 4, t * D:(t + 1) * D], mixr[:, t * P:(t + 1) * P], par(s, "wr"),
                                         start=True, stop=True)
                    last.then_inc(sem["rk_psum"], 1)
                    wait(pe, "kact_ready", s, a)
                    wait(pe, "gated", s, a - 1)
                    for t in range(BT):
                        last = pe.matmul(ps[:, 6, t * D:(t + 1) * D], kact[:, t * P:(t + 1) * P], par(s, "wv"),
                                         start=True, stop=True)
                    last.then_inc(sem["proj_psum"], 1)

            def single_head():
                s = "att3"
                turn_all(s)

                def turn_context(i):
                    wait(pe, "zt_ready", s, 0, 4 + i - 1)
                    for t in range(4):
                        last = pe.transpose(ps[0:C, 7, t * P:(t + 1) * P], ctx_sb[:, 4 * i + t, :], ident)
                    last.then_inc(sem["zt_psum"], 1)

                turn_context(0)
                for step in range(B + 2):
                    p, m, d = step, step - 1, step - 2
                    if valid(p):
                        wait(pe, "zt_ready", s, 0, 4 + p // 2)
                        wait(pe, "qk_ready", s, p - 1)
                        pe.matmul(ps[:, 0, 0:T], par(s, "wq"), zt[:, p, 1:1 + T], start=True, stop=True)
                        pe.matmul(ps[:, 0, T:2 * T], par(s, "wk", C), ct[:, p % 2, :], start=True, stop=True)\
                            .then_inc(sem["qk_psum"], 1)
                    if valid(d):
                        wait(pe, "p_ready", s, d)
                        wait(pe, "pt_ready", s, d - 1)
                        for kt in range(2):
                            for t in range(2):
                                last = pe.transpose(ps[:, 3, kt * T + t * P:kt * T + (t + 1) * P],
                                                    prob[:, t, kt * P:(kt + 1) * P], ident)
                        last.then_inc(sem["pt_psum"], 1)
                    if valid(p):
                        wait(pe, "v_ready", s, p - 1)
                        for t in range(2):
                            last = pe.matmul(ps[:, 1, t * D:(t + 1) * D], ct[:, p % 2, t * P:(t + 1) * P],
                                             par(s, "wv", C), start=True, stop=True)
                        last.then_inc(sem["v_psum"], 1)
                        if p % 2 == 1 and p < B - 1:
                            turn_context(p // 2 + 1)
                    if valid(d):
                        wait(pe, "pt_ready", s, d)
                        wait(pe, "v_ready", s, d)
                        wait(pe, "o_ready", s, d - 1)
                        for t in range(2):
                            for kt in range(2):
                                last = pe.matmul(ps[:, 4, t * D:(t + 1) * D], pt[:, kt * T + t * P:kt * T + (t + 1) * P],
                                                 v2[:, d % 3, kt, :], start=(kt == 0), stop=(kt == 1))
                        last.then_inc(sem["pv_psum"], 1)
                    if valid(p):
                        wait(pe, "qk_ready", s, p)
                        wait(pe, "p_ready", s, p - 1)
                        for t in range(2):
                            last = pe.matmul(ps[:, 2, t * T:(t + 1) * T], qk[:, 0, t * P:(t + 1) * P], qk[:, 1, :],
                                             start=True, stop=True)
                        last.then_inc(sem["s_psum"], 1)
                    if valid(d):
                        wait(pe, "ot_ready", s, d - 1)
                        turn_o(s, d, 5)
                        wait(pe, "x_updated", s, d - 1)
                        project_o(s, d, 6)
                    if step == B:
                        turn_all("moe3", range(3))
                        logits("moe3", 0)

            def down(s, blk, e):
                wait(pe, "h_ready", s, blk, 2 * e + 1)
                if isinstance(blk, int) and blk == 0 and e == 0:
                    wait_x(pe, s)
                wait(pe, "x_updated", s, blk, e - 2)
                for t in range(BT):
                    for c in range(2):
                        k = 2 * e + c
                        last = pe.matmul(ps[:, 4 + e % 2, t * D:(t + 1) * D], ht[:, e % 2, c, t * P:(t + 1) * P],
                                         par(s, "wd" if s == "moe1" else "w2")[:, k * P:(k + 1) * P],
                                         start=(c == 0), stop=(c == 1))
                last.then_inc(sem["y_psum"], 1)

            def block_of(s, blk, first):
                for e in range(E):
                    for c in range(2):
                        k = 2 * e + c
                        if s == "moe1":
                            wait(pe, "h_ready", s, blk, k - 2)
                            if first and k == 0:
                                wait(pe, "route_exp_in", s, 0, 0)
                            products = (("wg", 2 * c), ("wu", 2 * c + 1))
                        else:
                            wait(pe, "h_ready", s, blk, k - 4)
                            if first and k == 0:
                                wait(pe, "route_exp_in", s, 0, 0)
                            products = (("w1", 2 * (e % 2) + c),)
                        for name, bank in products:
                            last = pe.matmul(ps[:, bank, :], par(s, name)[:, k * P:(k + 1) * P],
                                             zt[:, bass.ds(2 * blk, 2), 1:1 + T], start=True, stop=True)
                        last.then_inc(sem["up_psum"], 1)
                    if e >= 1:
                        down(s, blk, e - 1)
                    elif not first:
                        down(s, blk - 1, E - 1)
                    if first:
                        beside_first_block(s, e)

            def experts(s):
                if s == "moe3":
                    for blk in range(NBLK):
                        for i in range(E + 2):
                            if i <= E:
                                w = E if i == 0 else i - 1
                                if blk == 0 and i == 0:
                                    wait(pe, "route_exp_in", s, 0, 0)
                                if blk == 0 and i == 1:
                                    wait(pe, "wt_ready", s, 0, 1)
                                wait(pe, "h_ready", s, blk, i - 2) if i >= 2 else wait(pe, "h_ready", s, blk - 1)
                                if i:
                                    wait(pe, "zs_ready", s, blk, i - 1)
                                rhs = zs[:, (i - 1) % 2, :] if i else zt[:, 2 * blk:2 * blk + 2, 1:1 + T]
                                pe.matmul(ps[:, 2 * (i % 2), :], par(s, "w1")[:, w * P:(w + 1) * P], rhs,
                                          start=True, stop=True)
                                pe.matmul(ps[:, 2 * (i % 2) + 1, :], par(s, "w3")[:, w * P:(w + 1) * P], rhs,
                                          start=True, stop=True).then_inc(sem["up_psum"], 1)
                            if i >= 1:
                                q = i - 1
                                w = E if q == 0 else q - 1
                                wait(pe, "h_ready", s, blk, q)
                                if q == 0:
                                    wait_x(pe, s) if blk == 0 else None
                                    wait(pe, "x_updated", s, blk - 2)
                                for t in range(BT):
                                    last = pe.matmul(ps[:, 4 + blk % 2, t * D:(t + 1) * D],
                                                     ht[:, q % 2, 0, t * P:(t + 1) * P],
                                                     par(s, "w2")[:, w * P:(w + 1) * P], start=(q == 0 and t == 0),
                                                     stop=(q == E), skip_group_check=True)
                                last.then_inc(sem["y_psum"], 1)
                            if blk == 0 and i < E:
                                beside_first_block(s, i)
                    return
                block_of(s, 0, True)
                with pe.Fori(1, NBLK) as blk:
                    block_of(s, blk, False)
                down(s, NBLK - 1, E - 1)

            for s in STAGES:
                pe.wait_ge(loaded[s], 16)
                if s not in MOE:
                    wait_x(pe, s)
                if s == "att1":
                    pe.wait_ge(loaded["ctxt"], 16)
                if s in ATT:
                    attention(s)
                elif s == "ffn0":
                    token_mix()
                elif s == "att3":
                    single_head()
                else:
                    experts(s)


def columns(inputs):
    f = {k: np.asarray(a) for k, a in inputs.items()}

    def col(v):
        return v[:, None]

    def row(v):
        return np.broadcast_to(v[None, :], (P, v.shape[0]))

    def heads_last(w, s):
        return w.reshape(w.shape[0], H[s], D // H[s]).transpose(0, 2, 1).reshape(w.shape[0], D)

    def att(s, name, bias=True):
        q, k = f[name + "Wq"], f[name + "Wk"]
        one = {"wq": q, "wk": k, "wv": f[name + "Wv"]}
        if s in H:
            one["wq"], one["wk"] = heads_last(q, s), heads_last(k, s)
        bq, bk = f[name + "bq"], f[name + "bk"]
        if s in H:
            bq, bk = heads_last(bq[None], s)[0], heads_last(bk[None], s)[0]
        one.update(bq=col(bq), bk=col(bk), bv=row(f[name + "bv"]))
        return one

    got = {}
    got["consts"] = {"ident": np.eye(P, dtype=np.float32), "index": row(np.arange(E, dtype=np.float32) - E)}
    n = "L0_xattn_"
    got["att0"] = {"wq": heads_last(f[n + "W_Q"], "att0"), "wk": heads_last(f[n + "W_K"], "att0"), "wv": f[n + "W_V"],
                   "xg": col(f[n + "ln_lat_g"]), "xb": col(f[n + "ln_lat_b"]),
                   "cg": col(f[n + "ln_in_g"]), "cb": col(f[n + "ln_in_b"]), "wo": f[n + "W_O"]}
    n = "L0_ffn_"
    got["ffn0"] = {"wr": f[n + "W_r"].T, "wk": f[n + "W_k"].T, "wv": f[n + "W_v"].T,
                   "mur": col(f[n + "mu_r"]), "muk": col(f[n + "mu_k"])}
    n = "L1_xattn_"
    got["att1"] = {**att("att1", n), "w1": f[n + "W1"], "b1": f[n + "b1"].reshape(2, P).T,
                   "w2": f[n + "W2"].reshape(2, P, D).transpose(1, 0, 2).reshape(P, 2 * D), "bo": row(f[n + "b2"])}
    n = "L1_ffn_"
    got["moe1"] = {"router": f[n + "router_w"].T, "wg": f[n + "w_gate"].transpose(2, 0, 1).reshape(P, -1),
                   "wu": f[n + "w_up"].transpose(2, 0, 1).reshape(P, -1),
                   "wd": f[n + "w_down"].reshape(E, D, 2, P).transpose(3, 0, 2, 1).reshape(P, -1)}
    n = "L2_xattn_"
    got["att2"] = {**att("att2", n), "wo": f[n + "Wo"], "bo": row(f[n + "bo"])}
    n = "L2_ffn_"
    got["moe2"] = {"router": f[n + "rW"], "rb": row(f[n + "rb"]), "xg": col(f[n + "ln_g"]), "xb": col(f[n + "ln_b"]),
                   "w1": f[n + "W1"].transpose(1, 0, 2).reshape(P, -1), "b1": f[n + "b1"].reshape(2 * E, P).T,
                   "w2": f[n + "W2"].reshape(E, 2, P, D).transpose(2, 0, 1, 3).reshape(P, -1), "b2": f[n + "b2"]}
    n = "L3_xattn_"
    got["att3"] = {**att("att3", n), "wo": f[n + "Wo"], "bo": row(f[n + "bo"]),
                   "xg": col(f[n + "ln1_g"]), "xb": col(f[n + "ln1_b"]),
                   "cg": col(f[n + "ln2_g"]), "cb": col(f[n + "ln2_b"])}
    n = "L3_ffn_"
    both = {w: np.concatenate([f[n + w], f[n + w + "s"]]).transpose(1, 0, 2).reshape(P, -1) for w in ("w1", "w2", "w3")}
    got["moe3"] = {"router": f[n + "gate_w"].T, **both}

    packed = {}
    for s, names in PACKS.items():
        a = np.zeros((P, sum(w for _, w in names)), np.float32)
        at = 0
        for name, w in names:
            part = got[s][name]
            a[0:part.shape[0], at:at + w] = part
            at += w
        packed[s] = a
    return packed


def kernel(**inputs):
    import concourse.bacc as bacc
    from concourse.bass_utils import run_bass_kernel_spmd

    x = np.asarray(inputs["x"])
    ctx = np.asarray(inputs["ctx_768"]).reshape(B * T, C)
    arrays = {"x": x.reshape(B * T, D), "ctx": ctx, "ctxt": ctx.T, **columns(inputs)}
    arrays = {f"in_{k}": np.ascontiguousarray(a) for k, a in arrays.items()}
    nc = bacc.Bacc("TRN2", target_bir_lowering=False, num_devices=1)
    args = {k[3:]: nc.dram_tensor(k, a.shape, mybir.dt.from_np(a.dtype), kind="ExternalInput").ap()
            for k, a in arrays.items()}
    out = nc.dram_tensor("out", (B * T, D), F32, kind="ExternalOutput").ap()
    build(nc, args, out)
    r = run_bass_kernel_spmd(nc, [arrays], core_ids=[0])
    return r.results[0]["out"].reshape(x.shape)
```

```python
from contextlib import ExitStack

import concourse.bass as bass
from concourse import mybir
import numpy as np

F32 = mybir.dt.float32
BF16 = mybir.dt.bfloat16
F16 = mybir.dt.float16
ALU = mybir.AluOpType
ACT = mybir.ActivationFunctionType
AX = mybir.AxisListType.X

P = 128
B = 8
T = 256
D = 128
C = 96
NT = B * T // P
EPS = 1e-5
NBLK = 4
BLK = B * T // NBLK
BT = BLK // P
E = 8

HEADS = {"att0": 8, "att1": 16, "att2": 8}
SLOTS = {
    "att0": [(0, 0), (0, 1), (1, 0), (1, 1), (0, 2), (2, 0)],
    "att1": [(0, 0), (0, 1), (1, 0), (1, 1), (0, 2), (2, 0), (1, 2), (2, 1), (2, 2)],
    "att2": [(0, 0), (0, 1), (1, 0), (1, 1), (0, 2), (2, 0)],
}
TWO_ONES = float(np.array([0x3F803F80], np.uint32).view(np.float32)[0])
MAXROW = 96

PACKS = {
    "consts": [("ident", 128), ("index", 8)],
    "att0": [("wq", 128), ("wk", 128), ("wv", 128), ("xg", 1), ("xb", 1), ("cg", 1), ("cb", 1), ("wo", 128)],
    "ffn0": [("wr", 128), ("wk", 128), ("wv", 128), ("mur", 1), ("muk", 1)],
    "att1": [("wq", 128), ("wk", 128), ("wv", 128), ("bq", 1), ("bk", 1), ("bv", 128),
             ("w1", 256), ("b1", 2), ("w2", 256), ("bo", 128)],
    "moe1": [("router", 8), ("wg", 2048), ("wu", 2048), ("wd", 2048)],
    "att2": [("wq", 128), ("wk", 128), ("wv", 128), ("bq", 1), ("bk", 1), ("bv", 128), ("wo", 128), ("bo", 128)],
    "moe2": [("router", 8), ("rb", 8), ("xg", 1), ("xb", 1), ("w1", 2048), ("b1", 16), ("w2", 2048), ("b2", 128)],
    "att3": [("wq", 128), ("wk", 128), ("wv", 128), ("bq", 1), ("bk", 1), ("bv", 128), ("wo", 128), ("bo", 128),
             ("xg", 1), ("xb", 1), ("cg", 1), ("cb", 1)],
    "moe3": [("router", 8), ("w1", 9 * 128), ("w3", 9 * 128), ("w2", 9 * 128)],
}
STAGES = [s for s in PACKS if s != "consts"]
ATT = ("att0", "att1", "att2")
FLOWS = {"att0": ("att0", "att1"), "att2": ("att2",)}
EARLY = ("att2", 0)
EARLY_BEATS = [(), (), (), (0, 1), (2, 3), (4, 5), (6,), (7,)]
MOE = ("moe1", "moe2", "moe3")

FIRST_ROWS = 1
ROW_SLOTS = {"att0": 5, "att1": 11, "att2": 5}
LOW_BY_DVE = {"att0": (3, 6, 7), "att1": (6, 12, 13, 14, 15), "att2": (3, 6, 7)}
LOW_BY_DVE_LAST = {"att1": (3, 5, 7, 9, 11, 13, 15), "att2": (1, 3, 5, 7)}
RING = 6
LAG = 3

H = HEADS
PER_BATCH = {s: (1, 8) for s in ATT}
PER_MIX = {"ffn0": (1, 8)}
ALL_ATT = {s: (1, 8) for s in (*ATT, "att3")}
AT_ONCE = ("moe1", "moe2", "att3", "moe3")
GROUPS = (range(0, NT - BT), range(NT - BT, NT))
ROUTE_STEPS = {"moe1": 20, "moe2": 21, "moe3": 17}
NORM_GROUPS = {s: (2, 1) for s in AT_ONCE}
EVENTS = {
    "stats_taken": {**PER_BATCH, **NORM_GROUPS},
    "moments_ready": {**PER_BATCH, **NORM_GROUPS},
    "var_ready": {**PER_BATCH, **NORM_GROUPS},
    "rstd_ready": {**PER_BATCH, **NORM_GROUPS},
    "z_ready": {**PER_BATCH, **{s: (4, 1) for s in AT_ONCE}},
    "zt_psum": {**PER_BATCH, **{s: (4, 1) for s in AT_ONCE}, "att3": (8, 1)},
    "zt_ready": {**PER_BATCH, **{s: (4, 1) for s in AT_ONCE}, "att3": (8, 1)},
    "x_plus": {"moe2": (2, 1)},
    "x_updated": {**ALL_ATT, "moe1": (8, 4), "moe2": (8, 4), "moe3": (1, 4)},
    "qk_psum": ALL_ATT,
    "v_psum": ALL_ATT,
    "qk_ready": ALL_ATT,
    "v_ready": ALL_ATT,
    "o_ready": ALL_ATT,
    "ot_psum": ALL_ATT,
    "ot_ready": ALL_ATT,
    "proj_psum": ALL_ATT,
    "xb_ready": {s: (1, 8) for s in ("att1", "att2", "att3")},
    "qk0_ready": PER_BATCH, "qkrest_ready": PER_BATCH, "qk1_ready": PER_BATCH, "qk2_ready": PER_BATCH,
    "v0_ready": PER_BATCH, "vrest_ready": PER_BATCH, "v1_ready": PER_BATCH, "v2_ready": PER_BATCH,
    "rows_psum": {s: (H[s], 8) for s in ATT},
    "max_done": {s: (H[s], 8) for s in ATT},
    "max_split": {s: (3, 8) for s in ATT},
    "max_ready": PER_BATCH,
    "maxt_psum": PER_BATCH,
    "maxt_ready": PER_BATCH,
    "cols_psum": {s: (H[s], 8) for s in ATT},
    "exp_ready": {s: (H[s], 8) for s in ATT},
    "low_by_dve": {},
    "low_by_pool": {},
    "sums_done": {s: (H[s], 8) for s in ATT},
    "sums_read": PER_BATCH,
    "hid_psum": {"att1": (1, 8)},
    "hid_ready": {"att1": (1, 8)},
    "mix_stats_taken": PER_MIX,
    "mix_moments_ready": PER_MIX,
    "mix_var_ready": PER_MIX,
    "mix_rstd_ready": PER_MIX,
    "mix_z_ready": PER_MIX,
    "mix_zt_psum": PER_MIX,
    "mix_zt_ready": PER_MIX,
    "diff_ready": PER_MIX,
    "mix_ready": PER_MIX,
    "rk_psum": PER_MIX,
    "gate_ready": PER_MIX,
    "kact_ready": PER_MIX,
    "sigmoid_step": PER_MIX,
    "sigmoid_ready": PER_MIX,
    "val_psum": PER_MIX,
    "val_ready": PER_MIX,
    "gated": PER_MIX,
    "mixed": PER_MIX,
    "s_psum": {"att3": (1, 8)},
    "smax_ready": {"att3": (1, 8)},
    "nbias_ready": {"att3": (1, 8)},
    "p_ready": {"att3": (1, 8)},
    "rden_ready": {"att3": (1, 8)},
    "pt_psum": {"att3": (1, 8)},
    "pt_ready": {"att3": (1, 8)},
    "pv_psum": {"att3": (1, 8)},
    "logits_psum": {s: (2, 1) for s in MOE},
    "route_steps": {s: (2 * n, 1) for s, n in ROUTE_STEPS.items()},
    "route_exp_in": {s: (2, 1) for s in MOE},
    "route_exp": {s: (2, 1) for s in MOE},
    "weights_ready": {s: (2, 1) for s in MOE},
    "wt_psum": {s: (4, 1) for s in ("moe2", "moe3")},
    "wt_ready": {s: (4, 1) for s in ("moe2", "moe3")},
    "bias_psum": {"moe2": (4, 1)},
    "bias_added": {"moe2": (4, 1)},
    "up_psum": {"moe1": (16, 4), "moe2": (16, 4), "moe3": (9, 4)},
    "gate_done": {"moe1": (16, 4), "moe3": (9, 4)},
    "h_ready": {"moe1": (16, 4), "moe2": (16, 4), "moe3": (9, 4)},
    "y_psum": {"moe1": (8, 4), "moe2": (8, 4), "moe3": (9, 4)},
    "zs_ready": {"moe3": (8, 4)},
}


class Counts:

    def __init__(self):
        self.base = {}
        for name, stages in EVENTS.items():
            total = 0
            for s in STAGES:
                self.base[name, s] = total
                per, steps = stages.get(s, (0, 0))
                total += per * steps

    def done(self, name, stage, b, k=None):
        if stage == "att1" and isinstance(b, int) and b < 0:
            stage, b = "att0", b + B
        per, steps = EVENTS[name][stage]
        base = self.base[name, stage]
        k = per - 1 if k is None else k
        if isinstance(b, int):
            if b < 0 or (b == 0 and k < 0 and stage != "att1"):
                return base
            if b >= steps:
                return base + per * steps
        return b * per + (base + k + 1)


def build(nc, args, out):
    counts = Counts()
    done = counts.done

    with ExitStack() as ctx:
        def sb(name, shape, dt=F32):
            return ctx.enter_context(nc.sbuf_tensor(name, shape, dt))

        sem = {name: ctx.enter_context(nc.semaphore(name)) for name in EVENTS}
        loaded = {name: ctx.enter_context(nc.semaphore(f"loaded_{name}"))
                  for name in (*PACKS, "x0", "ctx0", "x", "ctx", "ctxt")}
        stack_in = [ctx.enter_context(nc.semaphore(f"stack_in{i}")) for i in range(3)]
        maxrow_in = [ctx.enter_context(nc.semaphore(f"maxrow_in{i}")) for i in range(3)]
        const_ready = ctx.enter_context(nc.semaphore("const_ready"))
        maxrow_ones = ctx.enter_context(nc.semaphore("maxrow_ones"))
        rows_padded = ctx.enter_context(nc.semaphore("rows_padded"))
        wt_out = ctx.enter_context(nc.semaphore("wt_out"))
        scale_in = [ctx.enter_context(nc.semaphore(f"scale_in{i}")) for i in range(2)]
        stored = ctx.enter_context(nc.semaphore("stored"))

        x_sb = sb("x_sb", [P, NT, D])
        ctx_sb = sb("ctx_sb", [P, NT, C])
        ctxt_sb = sb("ctxt_sb", [C, B * T])
        cols = {s: sum(n for _, n in PACKS[s]) for s in PACKS}
        pack = {s: sb(f"pack_{s}", [P, cols[s]]) for s in PACKS if s not in MOE}
        moe_pack = sb("pack_moe", [P, max(cols[s] for s in MOE)])
        for s in MOE:
            pack[s] = moe_pack

        def par(stage, name, rows=P):
            at = 0
            for n, w in PACKS[stage]:
                if n == name:
                    return pack[stage][0:rows, at:at + w]
                at += w
            raise KeyError(name)

        ident = par("consts", "ident")
        ident16 = sb("ident16", [P, P], BF16)
        index8 = par("consts", "index")

        stats = sb("stats", [P, NT, 6])
        moments = sb("moments", [P, NT, 2])
        var_eps = sb("var_eps", [P, 2, NT])
        rstd = sb("rstd", [P, 2, NT])
        neghalf = sb("neghalf", [P, 2, NT])
        z = sb("z", [P, NT, D])
        zt = sb("zt", [P, B, 1 + T])
        ct = sb("ct", [C, 2, T])

        qk = sb("qk", [P, 2, T])
        qk_rest = sb("qk_rest", [P, 2, T])
        qk_parts = sb("qk_parts", [P, 6, T], BF16)
        v = sb("v", [P, 2, D])
        v_rest = sb("v_rest", [P, 2, D])
        v_parts = [sb(f"v_parts{i}", [P, 2, 400], BF16) for i in range(3)]
        stack = [sb(f"stack{i}", [P, 16, 2, T], BF16) for i in range(3)]
        negmax = sb("negmax", [P, 2, 16])
        negmax_rest = sb("negmax_rest", [P, 2, 16])
        negmax_parts = sb("negmax_parts", [P, 2, 48], BF16)
        maxt = sb("maxt", [48, T], BF16)
        exps = sb("exps", [P, RING, 2 * T])
        high = sb("high", [P, RING, 2 * T], F16)
        low = sb("low", [P, RING, 2 * T], F16)
        osum = sb("osum", [P, 2, D])
        rden = sb("rden", [P, 2, 16])
        o = sb("o", [P, 2, D])
        ot = sb("ot", [P, T])
        hid = sb("hid", [P, 2, T])
        xb = sb("xb", [P, 2, D])

        lg = sb("lg", [P, NT, E])
        rt = [sb(f"rt{i}", [P, NT, E]) for i in range(3)]
        rs = [sb(f"rs{i}", [P, NT]) for i in range(4)]
        weights = sb("weights", [P, NT, E])
        wt = sb("wt", [E, B * T])
        gated = sb("gated", [P, 2, BLK])
        ht = sb("ht", [P, 2, 2, BLK])
        scale_sb = sb("scale_sb", [P, 2, BLK])
        zs = sb("zs", [P, 2, BLK])

        mixd, mixr, mixk, sig, krelu, kact, val, gv = (ht[:, i // 4, (i // 2) % 2, (i % 2) * T:(i % 2 + 1) * T]
                                                       for i in range(8))
        mix_stats = sb("mix_stats", [P, 2, 6])
        mix_moments = sb("mix_moments", [P, 2, 2])
        mix_var = sb("mix_var", [P, 2])
        mix_rstd = sb("mix_rstd", [P, 2])

        v2 = exps[:, 0:2, :].rearrange("p r c -> p (r c)")[:, 0:3 * 2 * D].rearrange("p (i t c) -> p i t c", i=3, t=2)
        prob = exps[:, 2, :].rearrange("p (t k) -> p t k", t=2)
        pt = exps[:, 3, :]
        nbias = sb("nbias", [P, 2])
        den3 = sb("den3", [P, 2, 2])
        rden3 = sb("rden3", [P, 2, 2])

        scratch = nc.dram_tensor("weights_t", (E, B * T), F32, kind="Internal").ap()

        ps = ctx.enter_context(nc.psum_tensor("ps", [P, 8, 512], F32))
        TURN, SIDE = 4, 7

        def parts_view(i, s, j):
            dv = D // H[s]
            w = 3 * dv + 1
            return v_parts[i][:, :, 0:H[s] * w].rearrange("p t (h w) -> p t h w", w=w)[:, :, :, j * dv:(j + 1) * dv]

        def sums_view(s, t):
            w = 3 * (D // H[s]) + 1
            return ps[:, 5 + t, 0:H[s] * w].rearrange("p (h w) -> p h w", w=w)

        def rows_at(s, u):
            n, span = H[s], ROW_SLOTS[s]
            i = u - FIRST_ROWS
            return range(i * n // span, (i + 1) * n // span) if 0 <= i < span else range(0)

        def last_rows(s):
            return FIRST_ROWS + ROW_SLOTS[s] - 1

        def low_by_dve(s, a, u):
            table = LOW_BY_DVE_LAST if a == B - 1 and s in LOW_BY_DVE_LAST else LOW_BY_DVE
            return u in table[s]

        def lows_done(s, a, u):
            who = low_by_dve(s, a, u)
            heads = [(t, b, h) for t in ATT for b in range(B) for h in range(H[t])]
            upto = heads[:heads.index((s, a, u)) + 1]
            return "low_by_dve" if who else "low_by_pool", sum(low_by_dve(*h) == who for h in upto)

        def head_number(s, a, u):
            return B * sum(H[t] for t in ATT[:ATT.index(s)]) + a * H[s] + u

        def slot(s, a, u):
            return head_number(s, a, u) % RING

        def wait_sums(eng, s, a, u):
            g = head_number(s, a, u) - RING
            if g >= 0:
                eng.wait_ge(sem["sums_done"], g + 1)

        def buf(s, b):
            return (B * ATT.index(s) + b) % 3

        def steps_of(flow):
            stages = FLOWS[flow]
            last = B * len(stages)

            def at(g):
                if g < 0:
                    return stages[0], g
                return (stages[g // B], g % B) if g < last else (stages[-1], B + g - last)

            for g in range(last + 3):
                p, m, a, d, n = (at(g - lag) for lag in (0, 1, 2, 3, -1))
                heads = max(H[s] for s, b in (m, a, d) if valid(b)) if g else H[p[0]]
                yield g - last, heads, p, m, a, d, n

        def mix_step(flow, g):
            return [b if flow == "att0" and valid(b) else None for b in (g - 4, g - 5, g - 6)]

        def logits_at(s, tiles):
            bank = SIDE if tiles[0] in GROUPS[1] else 1 if s == "moe3" else 5
            return ps[:, bank, tiles[0] * E:(tiles[-1] + 1) * E]

        def turn_bank(s, i):
            return (0, 1, 0, 6)[i] if s in MOE else (6, SIDE, 6, 6)[i]

        def qk_bank(s, p):
            return 6 if s == EARLY[0] and p <= 1 else TURN

        def turn_event(s, i):
            return 4 if s == "att3" and i == 3 else i

        def context_event(i):
            return 4 + i if i else 3

        def wt_bank(s, i):
            return (2, 3, SIDE, SIDE)[i] if s == "moe3" else SIDE

        def valid(b):
            return 0 <= b < B

        def wait(eng, name, stage, b, k=None):
            value = done(name, stage, b, k)
            if isinstance(value, int) and value <= 0:
                return
            eng.wait_ge(sem[name], value)

        def before(stage):
            names = [s for s in STAGES if s != "ffn0"]
            return names[names.index(stage) - 1] if names.index(stage) else None

        def after(stage):
            return STAGES[STAGES.index(stage) + 1]

        def wait_x(eng, stage):
            prev = before(stage)
            if prev:
                eng.wait_ge(sem["x_updated"], done("x_updated", prev, 99))

        def uses(s, b):
            return [st for st in ATT for i in range(B)
                    if buf(st, i) == buf(s, b) and (ATT.index(st), i) <= (ATT.index(s), b)]

        def stack_total(s, b):
            return sum(16 * len(SLOTS[st]) for st in uses(s, b))

        def maxrow_total(s, b):
            return 16 * len(uses(s, b))

        block = ctx.enter_context(nc.Block())

        @block.sync
        def _(sp):
            xin = args["x"].rearrange("(n p) d -> p n d", p=P)
            cin = args["ctx"].rearrange("(n p) d -> p n d", p=P)
            sp.dma_start(x_sb[:, 0:2, :], xin[:, 0:2, :]).then_inc(loaded["x0"], 16)
            sp.dma_start(ctx_sb[:, 0:2, :], cin[:, 0:2, :]).then_inc(loaded["ctx0"], 16)
            for s in ("consts", "att0"):
                sp.dma_start(pack[s][:, :], args[s]).then_inc(loaded[s], 16)
            sp.dma_start(x_sb[:, 2:, :], xin[:, 2:, :]).then_inc(loaded["x"], 16)
            sp.dma_start(ctx_sb[:, 2:, :], cin[:, 2:, :]).then_inc(loaded["ctx"], 16)
            for s in ("ffn0", "att1"):
                sp.dma_start(pack[s][:, :], args[s]).then_inc(loaded[s], 16)
            sp.dma_start(ctxt_sb[:, :], args["ctxt"]).then_inc(loaded["ctxt"], 16)
            for s in ("moe1", "att2", "att3"):
                sp.dma_start(pack[s][:, 0:cols[s]], args[s]).then_inc(loaded[s], 16)

            for flow in FLOWS:
                for g, heads, (s, p), (sm, m), (sa, a), (sd, d), (sn, n) in steps_of(flow):
                    if valid(p):
                        nh, dh, i = H[s], D // H[s], buf(s, p)
                        if s == "att1" and p < 3:
                            sp.wait_ge(rows_padded, p + 1)
                        wait(sp, "cols_psum", s, p - 3)
                        for j, (qa, kc) in enumerate(SLOTS[s]):
                            if j == 0:
                                wait(sp, "qk0_ready", s, p)
                            if j == 1:
                                wait(sp, "qk1_ready", s, p)
                            if j == 4:
                                wait(sp, "qk2_ready", s, p)
                            sp.dma_start(stack[i][j * dh:(j + 1) * dh, 0:nh, :, :],
                                         qk_parts[:, qa:3 + kc + 1:3 + kc - qa, :]).then_inc(stack_in[i], 16)
                    if (s, p) == EARLY:
                        sp.wait_ge(sem["x_updated"], done("x_updated", "moe1", 99))
                        sp.dma_start(pack["moe2"][:, 0:cols["moe2"]], args["moe2"]).then_inc(loaded["moe2"], 16)
                    if valid(m):
                        wait(sp, "maxt_ready", sm, m)
                        wait(sp, "cols_psum", sm, m - 3)
                        i = buf(sm, m)
                        sp.dma_start(stack[i][MAXROW:MAXROW + 3, 0:H[sm], 0, :], maxt[0:3 * H[sm], :])\
                            .then_inc(maxrow_in[i], 16)
            sp.wait_ge(sem["x_updated"], done("x_updated", "moe2", 99))
            sp.dma_start(pack["moe3"][:, 0:cols["moe3"]], args["moe3"]).then_inc(loaded["moe3"], 16)

            def spread(first, last):
                at = slice(first * BLK, (last + 1) * BLK)
                wait(sp, "wt_ready", "moe3", 0, last)
                sp.dma_start(scratch[:, at], wt[:, at]).then_inc(wt_out, 16)

            spread(0, NBLK - 2)
            sp.wait_ge(wt_out, 16)
            def store(blk):
                wait(sp, "x_updated", "moe3", blk)
                sp.dma_start(out.rearrange("(n p) d -> p n d", p=P)[:, blk * BT:(blk + 1) * BT, :],
                             x_sb[:, blk * BT:(blk + 1) * BT, :]).then_inc(stored, 16)

            for blk in range(NBLK):
                if blk == 1:
                    spread(NBLK - 1, NBLK - 1)
                if blk == NBLK - 1:
                    sp.wait_ge(wt_out, 32)
                for e in range(E):
                    n = blk * E + e
                    if n >= 2:
                        wait(sp, "zs_ready", "moe3", (n - 2) // E, (n - 2) % E)
                    src = scratch[e:e + 1, blk * BLK:(blk + 1) * BLK].broadcast_to([P, BLK])
                    sp.dma_start(scale_sb[:, n % 2, :], src).then_inc(scale_in[n % 2], 16)
                    if e == 1 and blk:
                        store(blk - 1)
            store(NBLK - 1)
            sp.wait_ge(stored, 16 * NBLK)

        @block.vector
        def _(dve):
            dve.memset(zt[:, :, 0:1], 0.0)
            dve.memset(neghalf[:, :, :], -0.5)
            dve.wait_ge(loaded["consts"], 16)
            dve.tensor_copy(ident16[:, :], ident).then_inc(const_ready, 1)
            dve.wait_ge(const_ready, 1)

            def take_stats(s, n, context):
                if n < 2 and s == "att0":
                    dve.wait_ge(loaded["x" if n else "x0"], 16)
                    dve.wait_ge(loaded["ctx" if n else "ctx0"], 16)
                if n == 0 and s == "att2":
                    wait(dve, "x_updated", before(s), NBLK - 2, E - 1)
                if s == "att1":
                    wait(dve, "mixed", "ffn0", n)
                wait(dve, "rstd_ready", s, n - 1)
                for t in range(2):
                    last = dve.bn_stats(stats[:, t, :], x_sb[:, 2 * n + t, :])
                if context:
                    for t in range(2):
                        last = dve.bn_stats(stats[:, 2 + t, :], ctx_sb[:, 2 * n + t, :])
                last.then_inc(sem["stats_taken"], 1)
                wait(dve, "stats_taken", s, n)
                for t in range(4 if context else 2):
                    last = dve.bn_aggr(moments[:, t, :], stats[:, t, :])
                last.then_inc(sem["moments_ready"], 1)

            def apply_norm(s, n, context):
                wait(dve, "rstd_ready", s, n)
                wait(dve, "moments_ready", s, n)
                wait(dve, "zt_psum", s, n - 1)
                for t in range(2):
                    last = dve.tensor_scalar(z[:, t, :], x_sb[:, 2 * n + t, :], moments[:, t, 0:1], rstd[:, 0, t:t + 1],
                                             ALU.subtract, ALU.mult)
                if context:
                    for t in range(2):
                        cn = ctx_sb[:, 2 * n + t, :]
                        last = dve.tensor_scalar(cn, cn, moments[:, 2 + t, 0:1], rstd[:, 0, 2 + t:3 + t],
                                                 ALU.subtract, ALU.mult)
                last.then_inc(sem["z_ready"], 1)

            def stats_all(s, g, tiles):
                if tiles[-1] == NT - 1:
                    wait_x(dve, s)
                elif before(s) in MOE:
                    wait(dve, "x_updated", before(s), tiles[-1] // BT, E - 1)
                else:
                    wait(dve, "x_updated", before(s), tiles[-1] // 2)
                wait(dve, "rstd_ready", before(s), 99)
                for t in tiles:
                    last = dve.bn_stats(stats[:, t, :], x_sb[:, t, :])
                last.then_inc(sem["stats_taken"], 1)
                moments_all(s, g, tiles)

            def moments_all(s, g, tiles):
                wait(dve, "stats_taken", s, 0, g)
                for t in tiles:
                    last = dve.bn_aggr(moments[:, t, :], stats[:, t, :])
                last.then_inc(sem["moments_ready"], 1)

            def apply_all(s, g, tiles):
                wait(dve, "moments_ready", s, 0, g)
                wait(dve, "rstd_ready", s, 0, g)
                wait(dve, "zt_psum", before(s), 99)
                for t in tiles:
                    last = dve.tensor_scalar(z[:, t, :], x_sb[:, t, :], moments[:, t, 0:1], rstd[:, 0, t:t + 1],
                                             ALU.subtract, ALU.mult)
                    if t % 4 == 3:
                        last.then_inc(sem["z_ready"], 1)

            def plus_norm(s, g):
                tiles = GROUPS[g]
                wait(dve, "zt_psum", s, 0, tiles[-1] // BT)
                for t in tiles:
                    last = dve.tensor_scalar(z[:, t, :], x_sb[:, t, :], moments[:, t, 0:1], rstd[:, 1, t:t + 1],
                                             ALU.subtract, ALU.mult)
                last.then_inc(sem["x_plus"], 1)
                wait(dve, "x_plus", s, 0, g)
                for t in range(tiles[0], tiles[-1], BT):
                    last = dve.tensor_tensor(x_sb[:, t:t + BT, :], x_sb[:, t:t + BT, :], z[:, t:t + BT, :], ALU.add)

            def finish(s, d):
                nh, dh = H[s], D // H[s]
                wait(dve, "sums_done", s, d)
                for t in range(2):
                    dve.tensor_reduce(osum[:, t, :].rearrange("p (h c) -> p h c", h=nh),
                                      sums_view(s, t)[:, :, 0:3 * dh].rearrange("p h (j c) -> p h c j", j=3),
                                      AX, ALU.add)
                for t in range(2):
                    last = dve.reciprocal(rden[:, t, 0:nh], sums_view(s, t)[:, :, 3 * dh])
                last.then_inc(sem["sums_read"], 1)
                wait(dve, "sums_read", s, d)
                wait(dve, "ot_psum", s, d - 1)
                for t in range(2):
                    last = dve.tensor_tensor(o[:, t, :].rearrange("p (h c) -> p h c", h=nh),
                                             osum[:, t, :].rearrange("p (h c) -> p h c", h=nh),
                                             rden[:, t, 0:nh].unsqueeze(2).to_broadcast([P, nh, dh]), ALU.mult)
                last.then_inc(sem["o_ready"], 1)

            def split_max(s, m):
                nh = H[s]
                wait(dve, "max_done", s, m)
                wait(dve, "maxt_psum", s, m - 1)
                parts = [negmax_parts[:, :, j * nh:(j + 1) * nh] for j in range(3)]
                whole, rest = negmax[:, :, 0:nh], negmax_rest[:, :, 0:nh]
                dve.tensor_copy(parts[0], whole).then_inc(sem["max_split"], 1)
                wait(dve, "max_split", s, m, 0)
                dve.tensor_tensor(rest, whole, parts[0], ALU.subtract).then_inc(sem["max_split"], 1)
                wait(dve, "max_split", s, m, 1)
                dve.tensor_copy(parts[1], rest).then_inc(sem["max_split"], 1)
                wait(dve, "max_split", s, m, 2)
                dve.tensor_tensor(parts[2], rest, parts[1], ALU.subtract).then_inc(sem["max_ready"], 1)

            def residual(s, d):
                bias = s != "att0"
                wait(dve, "proj_psum", s, d)
                if bias:
                    wait(dve, "xb_ready", s, d)
                base = xb[:, :, :] if bias else x_sb[:, 2 * d:2 * d + 2, :]
                bank = SIDE if s == "att1" else TURN
                dve.tensor_tensor(x_sb[:, 2 * d:2 * d + 2, :],
                                  ps[:, bank, 0:2 * D].rearrange("p (t c) -> p t c", t=2), base, ALU.add)\
                    .then_inc(sem["x_updated"], 1)

            def make_value_parts(s, p):
                nh, dh = H[s], D // H[s]
                w = 3 * dh + 1
                wait(dve, "v_psum", s, p)
                wait(dve, "vrest_ready", s, p - 1)
                vp = ps[:, SIDE, 0:2 * D].rearrange("p (t c) -> p t c", t=2)
                if s != "att0":
                    bv = par(s, "bv").unsqueeze(1).to_broadcast([P, 2, D])
                    dve.tensor_tensor(v[:, :, :], vp, bv, ALU.add).then_inc(sem["v_ready"], 1)
                else:
                    dve.tensor_copy(v[:, :, :], vp).then_inc(sem["v_ready"], 1)
                wait(dve, "v_ready", s, p)
                wait(dve, "sums_done", s, p - 3)
                if p < 3:
                    ones = v_parts[buf(s, p)][:, :, 0:nh * w].rearrange("p t (h w) -> p t h w", w=w)[:, :, :, 3 * dh:w]
                    dve.memset(ones, 1.0)
                dve.tensor_copy(parts_view(buf(s, p), s, 0), v[:, :, :].rearrange(by_head, h=nh))\
                    .then_inc(sem["v0_ready"], 1)

            by_head = "p t (h c) -> p t h c"

            def beat(flow, step, u):
                tail, heads, (s, p), (sm, m), (sa, a), (sd, d), (sn, n) = step
                total, nxt = B * len(FLOWS[flow]), after(FLOWS[flow][-1])
                f, f1, f2 = mix_step(flow, tail + total)
                if u == 0 and valid(n):
                    take_stats(sn, n, sn == "att0")
                if u == 0 and valid(d):
                    finish(sd, d)
                if u == 0 and f is not None:
                    mix_take_stats(f)
                if valid(m):
                    for h in rows_at(sm, u):
                        wait(dve, "rows_psum", sm, m, h)
                        dve.tensor_reduce(negmax[:, :, h:h + 1].rearrange("p t h -> p (t h)"),
                                          ps[:, h % 2, :].rearrange("p (t k) -> p t k", t=2),
                                          AX, ALU.max, negate=True).then_inc(sem["max_done"], 1)
                if valid(a) and u < H[sa] and low_by_dve(sa, a, u):
                    i = slot(sa, a, u)
                    wait(dve, "exp_ready", sa, a, u)
                    dve.tensor_tensor(low[:, i, :], exps[:, i, :], high[:, i, :], ALU.subtract)\
                        .then_inc(sem["low_by_dve"], 1)
                if valid(p) and u == 1:
                    if s == "att1" and p < 3:
                        wait(dve, "cols_psum", s, p - 3)
                        dve.memset(stack[buf(s, p)][64:MAXROW, 0:8, 1, :].bitcast(F32), 0.0).then_inc(rows_padded, 1)
                    wait(dve, "qk_ready", s, p)
                    if total + tail > 0 or flow == "att2":
                        prev_s, prev_b = (s, p - 1) if p else (ATT[ATT.index(s) - 1], B - 1)
                        dve.wait_ge(stack_in[buf(prev_s, prev_b)], stack_total(prev_s, prev_b))
                    dve.tensor_copy(qk_parts[:, 0:6:3, :], qk[:, :, :]).then_inc(sem["qk0_ready"], 1)
                if valid(p) and u == 2:
                    wait(dve, "qkrest_ready", s, p)
                    dve.tensor_copy(qk_parts[:, 1:6:3, :], qk_rest[:, :, :]).then_inc(sem["qk1_ready"], 1)
                if f is not None and u == 4:
                    mix_apply_norm(f)
                if f1 is not None and u == 5:
                    mix_tokens(f1)
                if valid(p) and u == 5:
                    make_value_parts(s, p)
                if f2 is not None and u == 5:
                    wait(dve, "val_ready", "ffn0", f2)
                    wait(dve, "mixed", "ffn0", f2 - 1)
                    wait(dve, "sigmoid_step", "ffn0", f2)
                    dve.reciprocal(sig, sig).then_inc(sem["sigmoid_ready"], 1)
                    wait(dve, "sigmoid_ready", "ffn0", f2)
                    dve.tensor_tensor(gv, val, sig, ALU.mult).then_inc(sem["gated"], 1)
                if valid(p) and u == 6:
                    wait(dve, "vrest_ready", s, p)
                    dve.tensor_copy(parts_view(buf(s, p), s, 1), v_rest[:, :, :].rearrange(by_head, h=H[s]))\
                        .then_inc(sem["v1_ready"], 1)
                if valid(m) and u == last_rows(sm):
                    split_max(sm, m)
                if valid(d) and u == (10 if sd == "att1" else 6):
                    residual(sd, d)
                if valid(n) and u == heads - 2:
                    apply_norm(sn, n, sn == "att0")
                if tail == 1 and u == 1:
                    stats_all(nxt, 0, GROUPS[0])
                if tail == 2 and u == 1:
                    apply_all(nxt, 0, GROUPS[0])


            def attention(flow):
                first = FLOWS[flow][0]
                nxt = after(FLOWS[flow][-1])
                dve.wait_ge(loaded[first], 16)
                if (first, 0) != EARLY:
                    take_stats(first, 0, first == "att0")
                    apply_norm(first, 0, first == "att0")
                total = B * len(FLOWS[flow])
                for step in steps_of(flow):
                    tail, heads, (s, p), (sm, m), (sa, a), (sd, d), (sn, n) = step
                    f, f1, f2 = mix_step(flow, tail + total)
                    if valid(n) and n == 0:
                        dve.wait_ge(loaded[sn], 16)
                    if f == 0:
                        dve.wait_ge(loaded["ffn0"], 16)
                    for u in range(heads) if (s, p) != EARLY else ():
                        beat(flow, step, u)
            def mix_take_stats(f):
                s = "ffn0"
                wait(dve, "x_updated", "att0", f)
                wait(dve, "mix_rstd_ready", s, f - 1)
                for t in range(2):
                    last = dve.bn_stats(mix_stats[:, t, :], x_sb[:, 2 * f + t, :])
                last.then_inc(sem["mix_stats_taken"], 1)
                wait(dve, "mix_stats_taken", s, f)
                for t in range(2):
                    last = dve.bn_aggr(mix_moments[:, t, :], mix_stats[:, t, :])
                last.then_inc(sem["mix_moments_ready"], 1)

            def mix_apply_norm(f):
                s = "ffn0"
                wait(dve, "mix_rstd_ready", s, f)
                wait(dve, "mix_moments_ready", s, f)
                wait(dve, "mix_zt_psum", s, f - 1)
                for t in range(2):
                    last = dve.tensor_scalar(z[:, 2 + t, :], x_sb[:, 2 * f + t, :], mix_moments[:, t, 0:1],
                                             mix_rstd[:, t:t + 1], ALU.subtract, ALU.mult)
                last.then_inc(sem["mix_z_ready"], 1)

            def mix_tokens(f):
                s = "ffn0"
                wait(dve, "diff_ready", s, f)
                wait(dve, "rk_psum", s, f - 1)
                for name, mix in (("muk", mixk), ("mur", mixr)):
                    last = dve.scalar_tensor_tensor(out=mix, in0=mixd, scalar=par(s, name), in1=zt[:, 1, 0:T],
                                                    op0=ALU.mult, op1=ALU.add)
                last.then_inc(sem["mix_ready"], 1)

            def single_head():
                s = "att3"
                dve.wait_ge(loaded[s], 16)
                stats_all(s, 1, GROUPS[1])
                apply_all(s, 1, GROUPS[1])
                for step in range(B + 2):
                    p, m, d = step, step - 1, step - 2
                    if valid(m):
                        wait(dve, "s_psum", s, m)
                        dve.tensor_reduce(negmax[:, :, 0:1].rearrange("p t h -> p (t h)"),
                                          ps[:, 2, :].rearrange("p (t k) -> p t k", t=2), AX, ALU.max, negate=True)\
                            .then_inc(sem["smax_ready"], 1)
                    if step >= 3 and 2 * (step - 3) in GROUPS[0]:
                        wait(dve, "x_updated", s, step - 3)
                        for t in range(2 * (step - 3), 2 * (step - 3) + 2):
                            last = dve.bn_stats(stats[:, t, :], x_sb[:, t, :])
                        if step == B:
                            last.then_inc(sem["stats_taken"], 1)
                    if step == B:
                        moments_all("moe3", 0, GROUPS[0])
                    if valid(p):
                        wait(dve, "v_psum", s, p)
                        wait(dve, "pv_psum", s, p - 3)
                        bv = par(s, "bv").unsqueeze(1).to_broadcast([P, 2, D])
                        dve.tensor_tensor(v2[:, p % 3, :, :], ps[:, 1, 0:2 * D].rearrange("p (t c) -> p t c", t=2), bv,
                                          ALU.add).then_inc(sem["v_ready"], 1)
                    if valid(d):
                        wait(dve, "rden_ready", s, d)
                        wait(dve, "pv_psum", s, d)
                        wait(dve, "ot_psum", s, d - 1)
                        for t in range(2):
                            last = dve.tensor_scalar(o[:, t, :], ps[:, 4, t * D:(t + 1) * D], rden3[:, d % 2, t:t + 1], None,
                                                     ALU.mult)
                        last.then_inc(sem["o_ready"], 1)
                    if valid(m):
                        wait(dve, "p_ready", s, m)
                        dve.reciprocal(rden3[:, m % 2, :], den3[:, m % 2, :]).then_inc(sem["rden_ready"], 1)
                    if valid(d):
                        wait(dve, "proj_psum", s, d)
                        wait(dve, "xb_ready", s, d)
                        dve.tensor_tensor(x_sb[:, 2 * d:2 * d + 2, :], ps[:, 6, 0:2 * D].rearrange("p (t c) -> p t c", t=2),
                                          xb[:, :, :], ALU.add).then_inc(sem["x_updated"], 1)
                    if step == B:
                        apply_all("moe3", 0, GROUPS[0])
                    if step == B + 1:
                        route_logits("moe3", 0)

            steps_taken = {}

            def router_of(s, g):
                ts = slice(GROUPS[g][0], GROUPS[g][-1] + 1)
                n = len(GROUPS[g])

                def chain(ins):
                    k = steps_taken.get(s, 0)
                    ins.then_inc(sem["route_steps"], 1)
                    wait(dve, "route_steps", s, 0, k)
                    steps_taken[s] = k + 1

                def over(a):
                    return a.unsqueeze(2).to_broadcast([P, n, E])

                return (chain, over, index8.unsqueeze(1).to_broadcast([P, n, E]), lg[:, ts, :],
                        [r[:, ts, :] for r in rt], [r[:, ts] for r in rs], weights[:, ts, :])

            def route_logits(s, g):
                chain, over, idx, lgg, rtg, rsg, wg = router_of(s, g)
                lp = logits_at(s, GROUPS[g]).rearrange("p (n e) -> p n e", e=E)
                wait(dve, "logits_psum", s, 0, g)
                if s == "moe2":
                    rb = par(s, "rb").unsqueeze(1).to_broadcast([P, len(GROUPS[g]), E])
                    chain(dve.tensor_tensor(lgg, lp, rb, ALU.add))
                else:
                    chain(dve.tensor_copy(lgg, lp))
                chain(dve.tensor_reduce(rsg[0], lgg, AX, ALU.max))
                dve.tensor_tensor(rtg[0], lgg, over(rsg[0]), ALU.subtract).then_inc(sem["route_exp_in"], 1)

            def route_pick(s, g):
                chain, over, idx, e_all, rtg, rsg, wg = router_of(s, g)
                wait(dve, "route_exp", s, 0, g)
                chain(dve.tensor_reduce(rsg[0], e_all, AX, ALU.add))
                chain(dve.reciprocal(rsg[3], rsg[0]))
                src = e_all
                for r in range(2):
                    chain(dve.tensor_reduce(rsg[1], src, AX, ALU.max))
                    chain(dve.tensor_tensor(rtg[1], src, over(rsg[1]), ALU.is_equal))
                    chain(dve.tensor_tensor(rtg[1], rtg[1], idx, ALU.mult))
                    chain(dve.tensor_reduce(rsg[2], rtg[1], AX, ALU.min))
                    chain(dve.tensor_tensor(rtg[2 - r], over(rsg[2]), idx, ALU.is_equal))
                    if r == 0:
                        chain(dve.scalar_tensor_tensor(out=rtg[0], in0=rtg[2], scalar=-2.0, in1=e_all,
                                                       op0=ALU.mult, op1=ALU.add))
                        src = rtg[0]

            def route_weights(s, g):
                chain, over, idx, e_all, rtg, rsg, wg = router_of(s, g)
                chain(dve.tensor_tensor(rtg[2], rtg[2], rtg[1], ALU.add))
                chain(dve.tensor_tensor(rtg[2], rtg[2], e_all, ALU.mult))
                if s == "moe3":
                    dve.tensor_tensor(wg, rtg[2], over(rsg[3]), ALU.mult).then_inc(sem["weights_ready"], 1)
                else:
                    chain(dve.tensor_tensor(rtg[2], rtg[2], over(rsg[3]), ALU.mult))
                    chain(dve.tensor_reduce(rsg[0], rtg[2], AX, ALU.add))
                    if s == "moe2":
                        chain(dve.tensor_scalar(rsg[0], rsg[0], 1e-8, None, ALU.max))
                    chain(dve.reciprocal(rsg[1], rsg[0]))
                    dve.tensor_tensor(wg, rtg[2], over(rsg[1]), ALU.mult).then_inc(sem["weights_ready"], 1)
                assert steps_taken[s] == (g + 1) * ROUTE_STEPS[s]
                wait(dve, "weights_ready", s, 0, g)

            def add_bias_of_block(i):
                s = "moe2"
                wait(dve, "bias_psum", s, 0, i)
                wait(dve, "x_updated", s, 0, i + 2)
                xs = x_sb[:, i * BT:(i + 1) * BT, :]
                dve.tensor_tensor(xs, xs, ps[:, 6, :].rearrange("p (t c) -> p t c", t=BT), ALU.add)\
                    .then_inc(sem["bias_added"], 1)
                wait(dve, "bias_added", s, 0, i)

            def beside_first_block(s, e):
                if e == 1:
                    if s == "moe2":
                        plus_norm(s, 1)
                    route_logits(s, 1)
                if e == 3:
                    route_pick(s, 1)
                if e == 4:
                    route_weights(s, 1)
                if s == "moe2" and e >= 4:
                    add_bias_of_block(e - 4)

            def mul_h(s, blk, i):
                wait(dve, "gate_done", s, blk, i)
                wait(dve, "y_psum", s, blk, i - 2)
                dve.tensor_tensor(ht[:, i % 2, 0, :], ps[:, 2 * (i % 2) + 1, :], gated[:, i % 2, :], ALU.mult)\
                    .then_inc(sem["h_ready"], 1)

            def add_y(s, blk, e):
                wait(dve, "y_psum", s, blk, e)
                wait(dve, "x_updated", s, blk, e - 1)
                for t in range(BT):
                    xt = x_sb[:, bass.ds(blk * BT + t, 1), :].rearrange("p a d -> p (a d)")
                    w = weights[:, bass.ds(blk * BT + t, 1), e:e + 1].rearrange("p a d -> p (a d)")
                    last = dve.scalar_tensor_tensor(out=xt, in0=ps[:, 4 + e % 2, t * D:(t + 1) * D],
                                                    scalar=w, in1=xt, op0=ALU.mult, op1=ALU.add)
                last.then_inc(sem["x_updated"], 1)

            def beside_last_block(e):
                first = EARLY[0]
                if e == 0:
                    dve.wait_ge(loaded[first], 16)
                    take_stats(first, 0, False)
                if e == 1:
                    apply_norm(first, 0, False)
                for u in EARLY_BEATS[e]:
                    beat(first, next(steps_of(first)), u)

            def block_of(s, blk, first=False, final=False):
                for e in range(E):
                    if s == "moe1":
                        for c in range(2):
                            wait(dve, "gate_done", s, blk, 2 * e + c)
                            wait(dve, "y_psum", s, blk, e - 2)
                            dve.tensor_tensor(ht[:, e % 2, c, :], ps[:, 2 * c + 1, :], gated[:, c, :], ALU.mult)\
                                .then_inc(sem["h_ready"], 1)
                    if first and e == 0:
                        route_logits(s, 0)
                        route_pick(s, 0)
                        route_weights(s, 0)
                    if e >= 1:
                        add_y(s, blk, e - 1)
                    elif not first:
                        add_y(s, blk - 1, E - 1)
                    if first:
                        beside_first_block(s, e)
                    if final and s == "moe1":
                        beside_last_block(e)
                    if final and s == "moe2" and e == 1:
                        stats_all("att3", 0, GROUPS[0])
                    if final and s == "moe2" and e == 3:
                        apply_all("att3", 0, GROUPS[0])

            def experts(s):
                dve.wait_ge(loaded[s], 16)
                if s == "moe3":
                    route_pick(s, 0)
                    route_weights(s, 0)
                stats_all(s, 1, GROUPS[1])
                apply_all(s, 1, GROUPS[1])
                if s == "moe2":
                    plus_norm(s, 0)
                if s == "moe3":
                    for blk in range(NBLK):
                        for i in range(E + 1):
                            if i >= 1:
                                mul_h(s, blk, i - 1)
                            if i < E:
                                n = blk * E + i
                                dve.wait_ge(scale_in[n % 2], 16 * (n // 2 + 1))
                                wait(dve, "up_psum", s, blk, i - 1) if i >= 2 else \
                                    wait(dve, "up_psum", s, blk - 1, E - 1 + i)
                                dve.tensor_tensor(zs[:, i % 2, :].rearrange("p (b t) -> p b t", b=2),
                                                  zt[:, 2 * blk:2 * blk + 2, 1:1 + T],
                                                  scale_sb[:, n % 2, :].rearrange("p (b t) -> p b t", b=2), ALU.mult)\
                                    .then_inc(sem["zs_ready"], 1)
                            if blk == 0:
                                beside_first_block(s, i)
                        mul_h(s, blk, E)
                        wait(dve, "y_psum", s, blk)
                        xs = x_sb[:, blk * BT:(blk + 1) * BT, :]
                        dve.tensor_tensor(xs, xs, ps[:, 4 + blk % 2, :].rearrange("p (t c) -> p t c", t=BT), ALU.add)\
                            .then_inc(sem["x_updated"], 1)
                    return
                block_of(s, 0, True)
                with dve.Fori(1, NBLK - 1) as blk:
                    block_of(s, blk)
                block_of(s, NBLK - 1, final=True)
                add_y(s, NBLK - 1, E - 1)

            for s in STAGES:
                if s in FLOWS:
                    attention(s)
                elif s in ("ffn0", "att1"):
                    continue
                elif s == "att3":
                    single_head()
                else:
                    experts(s)

        @block.gpsimd
        def _(pool):
            pool.wait_ge(const_ready, 1)

            def make_rstd_all(s, g, tiles):
                wait(pool, "moments_ready", s, 0, g)
                wait(pool, "z_ready", before(s), 99)
                wait(pool, "x_plus", "moe2", 99) if s == "att3" else None
                ts = slice(tiles[0], tiles[-1] + 1)
                a, b = (1.0 + EPS, EPS * EPS) if s in ("moe2", "att3") else (1.0, EPS)
                last = pool.tensor_scalar(var_eps[:, 0, ts], moments[:, ts, 1], a, b, ALU.mult, ALU.add)
                rows = 1
                if s == "moe2":
                    last = pool.tensor_scalar(var_eps[:, 1, ts], moments[:, ts, 1], 1.0, EPS, ALU.mult, ALU.add)
                    rows = 2
                last.then_inc(sem["var_ready"], 1)
                wait(pool, "var_ready", s, 0, g)
                pool.tensor_tensor(rstd[:, 0:rows, ts], var_eps[:, 0:rows, ts], neghalf[:, 0:rows, ts], ALU.pow)\
                    .then_inc(sem["rstd_ready"], 1)

            def make_rstd(s, n, context):
                wait(pool, "moments_ready", s, n)
                wait(pool, "z_ready", s, n - 1)
                c = 2
                a, b = (1.0 + EPS, EPS * EPS) if s == "att0" else (1.0, EPS)
                last = pool.tensor_scalar(var_eps[:, 0, 0:c], moments[:, 0:c, 1], a, b, ALU.mult, ALU.add)
                if context:
                    last = pool.tensor_scalar(var_eps[:, 0, 2:4], moments[:, 2:4, 1], 1.0, EPS, ALU.mult, ALU.add)
                    c = 4
                last.then_inc(sem["var_ready"], 1)
                wait(pool, "var_ready", s, n)
                pool.tensor_tensor(rstd[:, 0, 0:c], var_eps[:, 0, 0:c], neghalf[:, 0, 0:c], ALU.pow)\
                    .then_inc(sem["rstd_ready"], 1)

            def add_bias(s, d):
                wait(pool, "mixed", "ffn0", 99) if s == "att1" and d == B - 1 else None
                wait(pool, "x_updated", s, d - 1)
                bo = par(s, "bo").unsqueeze(1).to_broadcast([P, 2, D])
                pool.tensor_tensor(xb[:, :, :], x_sb[:, 2 * d:2 * d + 2, :], bo, ALU.add).then_inc(sem["xb_ready"], 1)

            def make_low(s, a, u):
                i = slot(s, a, u)
                wait(pool, "exp_ready", s, a, u)
                pool.tensor_tensor(low[:, i, :], exps[:, i, :], high[:, i, :], ALU.subtract)\
                    .then_inc(sem["low_by_pool"], 1)

            by_head = "p t (h c) -> p t h c"

            def attention(flow):
                first = FLOWS[flow][0]
                nxt = after(FLOWS[flow][-1])
                make_rstd(first, 0, first == "att0")
                total = B * len(FLOWS[flow])
                for tail, heads, (s, p), (sm, m), (sa, a), (sd, d), (sn, n) in steps_of(flow):
                    f, f1, f2 = mix_step(flow, tail + total)
                    if valid(d) and d == 0:
                        pool.wait_ge(loaded[sd], 16)
                    for u in range(heads):
                        if u == 0 and valid(n):
                            make_rstd(sn, n, sn == "att0")
                        if u == 0 and f is not None:
                            wait(pool, "mix_moments_ready", "ffn0", f)
                            wait(pool, "mix_z_ready", "ffn0", f - 1)
                            pool.tensor_scalar(mix_var[:, :], mix_moments[:, :, 1], 1.0, EPS, ALU.mult, ALU.add)\
                                .then_inc(sem["mix_var_ready"], 1)
                            wait(pool, "mix_var_ready", "ffn0", f)
                            pool.tensor_tensor(mix_rstd[:, :], mix_var[:, :], neghalf[:, 0, 0:2], ALU.pow)\
                                .then_inc(sem["mix_rstd_ready"], 1)
                        if valid(a) and u < H[sa] and not low_by_dve(sa, a, u):
                            make_low(sa, a, u)
                        if u == 1 and valid(p):
                            wait(pool, "qk0_ready", s, p)
                            pool.tensor_tensor(qk_rest[:, :, :], qk[:, :, :], qk_parts[:, 0:6:3, :], ALU.subtract)\
                                .then_inc(sem["qkrest_ready"], 1)
                        if u == 2 and valid(p):
                            wait(pool, "qk1_ready", s, p)
                            wait(pool, "qkrest_ready", s, p)
                            pool.tensor_tensor(qk_parts[:, 2:6:3, :], qk_rest[:, :, :], qk_parts[:, 1:6:3, :],
                                               ALU.subtract).then_inc(sem["qk2_ready"], 1)
                        if u == 3 and valid(d) and sd != "att0":
                            add_bias(sd, d)
                        if u == 4 and f1 is not None:
                            wait(pool, "mix_zt_ready", "ffn0", f1)
                            wait(pool, "mix_ready", "ffn0", f1 - 1)
                            pool.tensor_tensor(mixd, zt[:, 1, 1:1 + T], zt[:, 1, 0:T], ALU.subtract)\
                                .then_inc(sem["diff_ready"], 1)
                        if u == 5 and valid(p):
                            wait(pool, "v0_ready", s, p)
                            pool.tensor_tensor(v_rest[:, :, :].rearrange(by_head, h=H[s]),
                                               v[:, :, :].rearrange(by_head, h=H[s]), parts_view(buf(s, p), s, 0),
                                               ALU.subtract).then_inc(sem["vrest_ready"], 1)
                        if u == 6 and valid(p):
                            wait(pool, "v1_ready", s, p)
                            wait(pool, "vrest_ready", s, p)
                            pool.tensor_tensor(parts_view(buf(s, p), s, 2), v_rest[:, :, :].rearrange(by_head, h=H[s]),
                                               parts_view(buf(s, p), s, 1), ALU.subtract).then_inc(sem["v2_ready"], 1)
                        if u == 6 and f2 is not None:
                            wait(pool, "gated", "ffn0", f2)
                            xs = x_sb[:, 2 * f2:2 * f2 + 2, :]
                            pool.tensor_tensor(xs, xs, gv.rearrange("p (t c) -> p t c", t=2), ALU.add)\
                                .then_inc(sem["mixed"], 1)
                    if tail == 1:
                        make_rstd_all(nxt, 0, GROUPS[0])
                    if f1 is not None:
                        wait(pool, "gate_ready", "ffn0", f1)
                        wait(pool, "val_psum", "ffn0", f1 - 1)
                        pool.tensor_tensor(kact, krelu, krelu, ALU.mult).then_inc(sem["kact_ready"], 1)
                        pool.tensor_scalar(sig, sig, 1.0, 1.0, ALU.add, ALU.mult).then_inc(sem["sigmoid_step"], 1)

            for s in STAGES:
                if s in FLOWS:
                    attention(s)
                if s in ("ffn0", *ATT):
                    continue
                pool.wait_ge(loaded[s], 16)
                if s == "att3":
                    make_rstd_all(s, 0, GROUPS[0])
                make_rstd_all(s, 1, GROUPS[1])
                if s == "att3":
                    for d in range(B):
                        if d == B - 2:
                            make_rstd_all("moe3", 0, GROUPS[0])
                        add_bias(s, d)

        @block.scalar
        def _(act):
            act.wait_ge(const_ready, 1)

            def copy_turned(s, p):
                wait(act, "zt_psum", s, p)
                wait(act, "qk_psum", s, p - 1)
                dst = zt[:, 0, 1:1 + T]
                if s == "att0":
                    wait(act, "v_psum", s, p - 1)
                    nc.scalar.activation(dst, ps[:, TURN, 0:T], ACT.Identity, bias=par(s, "xb"), scale=par(s, "xg"))
                    last = nc.scalar.activation(ct[:, 0, :], ps[0:C, TURN, T:2 * T], ACT.Identity, bias=par(s, "cb", C),
                                                scale=par(s, "cg", C))
                else:
                    last = nc.scalar.activation(dst, ps[:, qk_bank(s, p), 0:T], ACT.Copy)
                last.then_inc(sem["zt_ready"], 1)

            def copy_all(s, chunks=range(4)):
                if chunks[0] == 0:
                    act.wait_ge(loaded[s], 16)
                for i in chunks:
                    wait(act, "zt_psum", s, 0, turn_event(s, i))
                    wait(act, "qk_psum", before(s), 99) if s in MOE else None
                    dst = zt[:, 2 * i:2 * i + 2, 1:1 + T]
                    src = ps[:, turn_bank(s, i), :].rearrange("p (b t) -> p b t", b=2)
                    if s in ("moe2", "att3"):
                        last = nc.scalar.activation(dst, src, ACT.Identity, bias=par(s, "xb"), scale=par(s, "xg"))
                    else:
                        last = nc.scalar.activation(dst, src, ACT.Copy)
                    last.then_inc(sem["zt_ready"], 1)

            def fill_stacks(i):
                rows = stack[i][64:MAXROW, 8:16, :, :].rearrange("p h a t -> p (h a t)").bitcast(F32)
                nc.scalar.activation(rows, zt[64:MAXROW, 0, 0:1].to_broadcast([MAXROW - 64, 8 * T]), ACT.Copy)
                ones = stack[i][MAXROW:MAXROW + 3, :, 1, :].bitcast(F32)
                half = neghalf[MAXROW:MAXROW + 3, 0, 0:1].unsqueeze(2).to_broadcast([3, 16, T // 2])
                nc.scalar.activation(ones, half, ACT.Copy, scale=-2.0 * TWO_ONES).then_inc(maxrow_ones, 1)

            def beat(flow, step, u):
                tail, heads, (s, p), (sm, m), (sa, a), (sd, d), (sn, n) = step
                total, nxt = B * len(FLOWS[flow]), after(FLOWS[flow][-1])
                f, f1, f2 = mix_step(flow, tail + total)
                if u == 3 and valid(d):
                    wait(act, "ot_psum", sd, d)
                    if sd == "att1" and d > 0:
                        wait(act, "hid_psum", sd, d - 1)
                    else:
                        wait(act, "proj_psum", sd, d - 1)
                    nc.scalar.activation(ot[:, :], ps[:, SIDE, 0:T], ACT.Copy).then_inc(sem["ot_ready"], 1)
                if tail == 2 and u == 4:
                    copy_all(nxt, range(2))
                if tail == 2 and u == 7:
                    copy_all(nxt, range(2, 3))
                if u == 3 and f1 is not None:
                    wait(act, "mix_zt_psum", "ffn0", f1)
                    wait(act, "mix_ready", "ffn0", f1 - 1)
                    nc.scalar.activation(zt[:, 1, 1:1 + T], ps[:, TURN, 0:T], ACT.Copy)\
                        .then_inc(sem["mix_zt_ready"], 1)
                if u == 3 and f2 is not None:
                    wait(act, "val_psum", "ffn0", f2)
                    wait(act, "gated", "ffn0", f2 - 1)
                    nc.scalar.activation(val, ps[:, TURN, T:2 * T], ACT.Copy).then_inc(sem["val_ready"], 1)
                if u == 6 and valid(d) and sd == "att1":
                    wait(act, "hid_psum", sd, d)
                    wait(act, "proj_psum", sd, d - 1)
                    for c in range(2):
                        last = nc.scalar.activation(hid[:, c, :], ps[:, TURN, c * T:(c + 1) * T], ACT.Relu,
                                                    bias=par(sd, "b1")[:, c:c + 1])
                    last.then_inc(sem["hid_ready"], 1)
                if u == 7 and f1 is not None:
                    wait(act, "rk_psum", "ffn0", f1)
                    wait(act, "gated", "ffn0", f1 - 1)
                    wait(act, "kact_ready", "ffn0", f1 - 1)
                    nc.scalar.activation(krelu, ps[:, SIDE, 0:T], ACT.Relu)
                    nc.scalar.activation(sig, ps[:, SIDE, T:2 * T], ACT.Exp, scale=-1.0)\
                        .then_inc(sem["gate_ready"], 1)
                if valid(a) and u < H[sa]:
                    i = slot(sa, a, u)
                    scale = float(D // H[sa]) ** -0.5
                    wait(act, "cols_psum", sa, a, u)
                    wait_sums(act, sa, a, u)
                    nc.scalar.activation(exps[:, i, :], ps[:, 2 + u % 2, :], ACT.Exp, scale=scale)
                    nc.scalar.activation(high[:, i, :], ps[:, 2 + u % 2, :], ACT.Exp, scale=scale)\
                        .then_inc(sem["exp_ready"], 1)
                if u == 0 and valid(p):
                    wait(act, "qk_psum", s, p)
                    wait(act, "qkrest_ready", s, p - 1)
                    if s == "att0":
                        nc.scalar.activation(qk[:, :, :], ps[:, TURN, :].rearrange("p (a t) -> p a t", a=2),
                                             ACT.Copy).then_inc(sem["qk_ready"], 1)
                    else:
                        nc.scalar.activation(qk[:, 0, :], ps[:, qk_bank(s, p), 0:T], ACT.Identity, bias=par(s, "bq"))
                        nc.scalar.activation(qk[:, 1, :], ps[:, qk_bank(s, p), T:2 * T], ACT.Identity, bias=par(s, "bk"))\
                            .then_inc(sem["qk_ready"], 1)
                if flow == "att0" and s == "att0" and p < 3 and u == 1:
                    fill_stacks(p)

            def attention(flow):
                first = FLOWS[flow][0]
                nxt = after(FLOWS[flow][-1])
                act.wait_ge(loaded[first], 16)
                copy_turned(first, 0) if (first, 0) != EARLY else None
                total = B * len(FLOWS[flow])
                for step in steps_of(flow):
                    tail, heads, (s, p), (sm, m), (sa, a), (sd, d), (sn, n) = step
                    f, f1, f2 = mix_step(flow, tail + total)
                    if valid(n) and n == 0:
                        act.wait_ge(loaded[sn], 16)
                    for u in range(heads) if (s, p) != EARLY else ():
                        beat(flow, step, u)
                    if valid(m):
                        wait(act, "maxt_psum", sm, m)
                        if tail + total > 1 or flow == "att2":
                            prev_s, prev_b = (sm, m - 1) if m else (ATT[ATT.index(sm) - 1], B - 1)
                            act.wait_ge(maxrow_in[buf(prev_s, prev_b)], maxrow_total(prev_s, prev_b))
                        rows = 3 * H[sm]
                        nc.scalar.activation(maxt[0:rows, :], ps[0:rows, SIDE, 0:T // 2].bitcast(BF16), ACT.Copy)\
                            .then_inc(sem["maxt_ready"], 1)
                    if valid(n) and (s, p) != EARLY:
                        copy_turned(sn, n)

            def route_exp(s, g):
                ts = slice(GROUPS[g][0], GROUPS[g][-1] + 1)
                wait(act, "route_exp_in", s, 0, g)
                nc.scalar.activation(lg[:, ts, :], rt[0][:, ts, :], ACT.Exp).then_inc(sem["route_exp"], 1)

            def copy_weights(s, i):
                wait(act, "wt_psum", s, 0, i)
                nc.scalar.activation(wt[:, i * BLK:(i + 1) * BLK], ps[0:E, wt_bank(s, i), :], ACT.Copy)\
                    .then_inc(sem["wt_ready"], 1)

            def beside_first_block(s, e):
                if e == 0 and s == "moe3":
                    for i in range(NBLK - 1):
                        copy_weights(s, i)
                if e == 0 and s != "moe3":
                    route_exp(s, 0)
                if e == 0:
                    copy_all(s, range(3, 4))
                if e == 2:
                    route_exp(s, 1)
                if s == "moe2" and 3 <= e < 3 + NBLK:
                    copy_weights(s, e - 3)
                if s == "moe3" and e == 5:
                    copy_weights(s, NBLK - 1)

            def single_head():
                s = "att3"
                scale = float(D) ** -0.5
                for step in range(B + 2):
                    p, m, d = step, step - 1, step - 2
                    if valid(p):
                        if p % 2 == 0:
                            wait(act, "zt_psum", s, 0, context_event(p // 2))
                            wait(act, "v_psum", s, p - 1)
                            nc.scalar.activation(ct[:, :, :], ps[0:C, 7, :].rearrange("p (b t) -> p b t", b=2),
                                                 ACT.Identity, bias=par(s, "cb", C), scale=par(s, "cg", C))\
                                .then_inc(sem["zt_ready"], 1)
                        wait(act, "qk_psum", s, p)
                        wait(act, "s_psum", s, p - 1)
                        nc.scalar.activation(qk[:, 0, :], ps[:, 0, 0:T], ACT.Identity, bias=par(s, "bq"))
                        nc.scalar.activation(qk[:, 1, :], ps[:, 0, T:2 * T], ACT.Identity, bias=par(s, "bk"))\
                            .then_inc(sem["qk_ready"], 1)
                    if valid(d):
                        wait(act, "pt_psum", s, d)
                        wait(act, "pv_psum", s, d - 1)
                        nc.scalar.activation(pt[:, :], ps[:, 3, :], ACT.Copy).then_inc(sem["pt_ready"], 1)
                    if step == B + 1:
                        copy_all("moe3", range(3))
                    if valid(m):
                        wait(act, "smax_ready", s, m)
                        nc.scalar.activation(nbias[:, :], negmax[:, :, 0:1].rearrange("p t h -> p (t h)"), ACT.Copy,
                                             scale=scale).then_inc(sem["nbias_ready"], 1)
                        wait(act, "nbias_ready", s, m)
                        wait(act, "pt_psum", s, m - 1)
                        for t in range(2):
                            last = nc.scalar.activation(prob[:, t, :], ps[:, 2, t * T:(t + 1) * T], ACT.Exp,
                                                        bias=nbias[:, t:t + 1], scale=scale,
                                                        accum_out=den3[:, m % 2, t:t + 1])
                        last.then_inc(sem["p_ready"], 1)
                    if valid(d):
                        wait(act, "ot_psum", s, d)
                        wait(act, "proj_psum", s, d - 1)
                        nc.scalar.activation(ot[:, :], ps[:, 5, 0:T], ACT.Copy).then_inc(sem["ot_ready"], 1)
                    if step == 0:
                        copy_all(s, range(3, 4))
                    if step == B + 1:
                        route_exp("moe3", 0)

            def beside_last_block(e):
                first = EARLY[0]
                if e == 2:
                    act.wait_ge(loaded[first], 16)
                    copy_turned(first, 0)
                for u in EARLY_BEATS[e]:
                    beat(first, next(steps_of(first)), u)
                if e == E - 1:
                    copy_turned(first, 1)

            def block_of(s, blk, first=False, final=False):
                for e in range(E):
                    for c in range(2):
                        k = 2 * e + c
                        wait(act, "up_psum", s, blk, k)
                        if s == "moe1":
                            wait(act, "h_ready", s, blk, k - 2)
                            nc.scalar.activation(gated[:, c, :], ps[:, 2 * c, :], ACT.Silu).then_inc(sem["gate_done"], 1)
                        else:
                            wait(act, "y_psum", s, blk, e - 2)
                            nc.scalar.activation(ht[:, e % 2, c, :], ps[:, 2 * (e % 2) + c, :], ACT.Gelu,
                                                 bias=par(s, "b1")[:, k:k + 1]).then_inc(sem["h_ready"], 1)
                    if first:
                        beside_first_block(s, e)
                    if final and s == "moe1":
                        beside_last_block(e)
                    if final and s == "moe2" and 5 <= e < 8:
                        copy_all("att3", range(e - 5, e - 4))

            def experts(s):
                if s == "moe3":
                    for blk in range(NBLK):
                        for i in range(E + 1):
                            wait(act, "up_psum", s, blk, i)
                            wait(act, "h_ready", s, blk, i - 2) if i >= 2 else wait(act, "h_ready", s, blk - 1)
                            nc.scalar.activation(gated[:, i % 2, :], ps[:, 2 * (i % 2), :], ACT.Silu)\
                                .then_inc(sem["gate_done"], 1)
                            if blk == 0 and i < E:
                                beside_first_block(s, i)
                    return
                block_of(s, 0, True)
                with act.Fori(1, NBLK - 1) as blk:
                    block_of(s, blk)
                block_of(s, NBLK - 1, final=True)

            for s in STAGES:
                if s in FLOWS:
                    attention(s)
                if s in ("ffn0", *ATT):
                    continue
                act.wait_ge(loaded[s], 16)
                if s == "att3":
                    single_head()
                else:
                    experts(s)

        @block.tensor
        def _(pe):
            pe.wait_ge(const_ready, 1)

            def turn(s, p):
                wait(pe, "z_ready", s, p)
                for t in range(2):
                    last = pe.transpose(ps[:, qk_bank(s, p), t * P:(t + 1) * P], z[:, t, :], ident)
                if s == "att0":
                    for t in range(2):
                        last = pe.transpose(ps[0:C, TURN, T + t * P:T + (t + 1) * P], ctx_sb[:, 2 * p + t, :], ident)
                last.then_inc(sem["zt_psum"], 1)

            def turn_all(s, chunks=range(4)):
                for i in chunks:
                    wait(pe, "z_ready", s, 0, i)
                    if i == 2:
                        wait(pe, "zt_ready", s, 0, 0)
                    for t in range(4):
                        last = pe.transpose(ps[:, turn_bank(s, i), t * P:(t + 1) * P], z[:, 4 * i + t, :], ident)
                    last.then_inc(sem["zt_psum"], 1)

            def logits(s, g):
                pe.wait_ge(loaded[s], 16)
                wait(pe, "zt_ready", s, 0, GROUPS[g][-1] // 4)
                for t in GROUPS[g]:
                    last = pe.matmul(logits_at(s, [t]), zt[:, t // 2, 1 + (t % 2) * P:1 + (t % 2 + 1) * P],
                                     par(s, "router"), start=True, stop=True)
                last.then_inc(sem["logits_psum"], 1)

            def turn_weights(s, i):
                wait(pe, "weights_ready", s, 0, 0 if i < NBLK - 1 else 1)
                if i and wt_bank(s, i) == wt_bank(s, i - 1):
                    wait(pe, "wt_ready", s, 0, i - 1)
                for t in range(BT):
                    last = pe.transpose(ps[0:E, wt_bank(s, i), t * P:(t + 1) * P], weights[:, i * BT + t, :], ident)
                last.then_inc(sem["wt_psum"], 1)

            def biases(s, i):
                wait(pe, "wt_ready", s, 0, i)
                wait(pe, "bias_added", s, 0, i - 1) if i else wait(pe, "zt_ready", s, 0)
                for t in range(BT):
                    last = pe.matmul(ps[:, 6, t * D:(t + 1) * D], wt[:, (i * BT + t) * P:(i * BT + t + 1) * P],
                                     par(s, "b2", E), start=True, stop=True)
                last.then_inc(sem["bias_psum"], 1)

            def beside_first_block(s, e):
                if e == 0 and s == "moe3":
                    for i in range(NBLK - 1):
                        turn_weights(s, i)
                if e == 0 and s != "moe3":
                    logits(s, 0)
                if e == 0:
                    turn_all(s, range(3, 4))
                if e == 1:
                    if s == "moe3":
                        wait(pe, "wt_ready", s, 0, NBLK - 2)
                    logits(s, 1)
                if s == "moe2" and 3 <= e < 3 + NBLK:
                    wait(pe, "route_exp_in", s, 0, 1)
                    turn_weights(s, e - 3)
                if s == "moe2" and e >= 4:
                    biases(s, e - 4)
                if s == "moe3" and e == 5:
                    turn_weights(s, NBLK - 1)

            def turn_o(s, d, bank):
                wait(pe, "o_ready", s, d)
                for t in range(2):
                    last = pe.transpose(ps[:, bank, t * P:(t + 1) * P], o[:, t, :], ident)
                last.then_inc(sem["ot_psum"], 1)

            def project_o(s, d, bank):
                wait(pe, "ot_ready", s, d)
                for t in range(2):
                    last = pe.matmul(ps[:, bank, t * D:(t + 1) * D], ot[:, t * P:(t + 1) * P], par(s, "wo"),
                                     start=True, stop=True)
                last.then_inc(sem["proj_psum"], 1)

            def rows(s, m, h):
                st = stack[buf(s, m)]
                if h == 0:
                    pe.wait_ge(stack_in[buf(s, m)], stack_total(s, m))
                wait(pe, "max_done", s, m, h - 2)
                for t in range(2):
                    last = pe.matmul(ps[:, h % 2, t * T:(t + 1) * T], st[0:MAXROW, h, 0, t * P:(t + 1) * P],
                                     st[0:MAXROW, h, 1, :], start=True, stop=True)
                last.then_inc(sem["rows_psum"], 1)

            def columns(s, a, h):
                st = stack[buf(s, a)]
                if h == 0:
                    pe.wait_ge(maxrow_in[buf(s, a)], maxrow_total(s, a))
                    pe.wait_ge(maxrow_ones, min(a + 1, 3) if s == "att0" else 3)
                wait(pe, "exp_ready", s, a, h - 2)
                for t in range(2):
                    last = pe.matmul(ps[:, 2 + h % 2, t * T:(t + 1) * T], st[0:MAXROW + 3, h, 1, t * P:(t + 1) * P],
                                     st[0:MAXROW + 3, h, 0, :], start=True, stop=True)
                last.then_inc(sem["cols_psum"], 1)

            def sums(s, a, h):
                w = 3 * (D // H[s]) + 1
                name, low_value = lows_done(s, a, h)
                if h == 0:
                    wait(pe, "sums_read", s, a - 1)
                    wait(pe, "v2_ready", s, a)
                wait(pe, "exp_ready", s, a, h)
                pe.wait_ge(sem[name], low_value)
                i = slot(s, a, h)
                for t in range(2):
                    n = 0
                    for kt in range(2):
                        for part in (high, low):
                            last = pe.matmul(ps[:, 5 + t, h * w:(h + 1) * w],
                                             part[:, i, kt * T + t * P:kt * T + (t + 1) * P],
                                             v_parts[buf(s, a)][:, kt, h * w:(h + 1) * w],
                                             start=(n == 0), stop=(n == 3), skip_group_check=True)
                            n += 1
                last.then_inc(sem["sums_done"], 1)

            def beat(flow, step, u):
                tail, heads, (s, p), (sm, m), (sa, a), (sd, d), (sn, n) = step
                total, nxt = B * len(FLOWS[flow]), after(FLOWS[flow][-1])
                f, f1, f2 = mix_step(flow, tail + total)
                kv = ct[:, 0, :] if s == "att0" else ctxt_sb[:, p % B * T:(p % B + 1) * T]
                if valid(a) and u < H[sa]:
                    columns(sa, a, u)
                if u == 0 and valid(p):
                    wait(pe, "zt_ready", s, p)
                    pe.matmul(ps[:, qk_bank(s, p), 0:T], par(s, "wq"), zt[:, 0, 1:1 + T], start=True, stop=True)
                    pe.matmul(ps[:, qk_bank(s, p), T:2 * T], par(s, "wk", C), kv, start=True, stop=True)\
                        .then_inc(sem["qk_psum"], 1)
                if u == 2 and valid(d):
                    wait(pe, "maxt_ready", sm, m - 1)
                    turn_o(sd, d, SIDE)
                if u == 2 and (f1 is not None or f2 is not None):
                    wait(pe, "qk_ready", s, p)
                    wait(pe, "x_updated", sd, d - 1)
                if u == 2 and f2 is not None:
                    wait(pe, "kact_ready", "ffn0", f2)
                    for t in range(2):
                        last = pe.matmul(ps[:, TURN, T + t * D:T + (t + 1) * D], kact[:, t * P:(t + 1) * P],
                                         par("ffn0", "wv"), start=True, stop=True)
                    last.then_inc(sem["val_psum"], 1)
                if u == 2 and f1 is not None:
                    wait(pe, "mix_z_ready", "ffn0", f1)
                    for t in range(2):
                        last = pe.transpose(ps[:, TURN, t * P:(t + 1) * P], z[:, 2 + t, :], ident)
                    last.then_inc(sem["mix_zt_psum"], 1)
                if u == 4 and valid(d):
                    wait(pe, "qk_ready", s, p)
                    wait(pe, "mix_zt_ready", "ffn0", f1) if f1 is not None else None
                    wait(pe, "val_ready", "ffn0", f2) if f2 is not None else None
                    if sd == "att1":
                        wait(pe, "ot_ready", sd, d)
                        for c in range(2):
                            last = pe.matmul(ps[:, TURN, c * T:(c + 1) * T], par(sd, "w1")[:, c * P:(c + 1) * P],
                                             ot[:, :], start=True, stop=True)
                        last.then_inc(sem["hid_psum"], 1)
                    else:
                        project_o(sd, d, TURN)
                if u == 4 and valid(p):
                    wait(pe, "ot_ready", sd, d)
                    wait(pe, "maxt_ready", sm, m - 1)
                    for t in range(2):
                        last = pe.matmul(ps[:, SIDE, t * D:(t + 1) * D], kv[:, t * P:(t + 1) * P],
                                         par(s, "wv", C), start=True, stop=True)
                    last.then_inc(sem["v_psum"], 1)
                if u == 6 and f1 is not None:
                    wait(pe, "mix_ready", "ffn0", f1)
                    wait(pe, "v_ready", s, p)
                    pe.matmul(ps[:, SIDE, 0:T], par("ffn0", "wk"), mixk, start=True, stop=True)
                    for t in range(2):
                        last = pe.matmul(ps[:, SIDE, T + t * D:T + (t + 1) * D], mixr[:, t * P:(t + 1) * P],
                                         par("ffn0", "wr"), start=True, stop=True)
                    last.then_inc(sem["rk_psum"], 1)
                if u == 8 and valid(d) and sd == "att1":
                    wait(pe, "hid_ready", sd, d)
                    wait(pe, "v_ready", s, p)
                    wait(pe, "gate_ready", "ffn0", f1) if f1 is not None else None
                    for t in range(2):
                        for c in range(2):
                            last = pe.matmul(ps[:, SIDE, t * D:(t + 1) * D], hid[:, c, t * P:(t + 1) * P],
                                             par(sd, "w2")[:, c * P:(c + 1) * P], start=(c == 0), stop=(c == 1))
                    last.then_inc(sem["proj_psum"], 1)
                if tail == 2 and u == 3:
                    wait(pe, "max_done", FLOWS[flow][-1], 99)
                    turn_all(nxt, range(2))
                if tail == 2 and u == 5:
                    turn_all(nxt, range(2, 3))
                if valid(m):
                    for h in rows_at(sm, u):
                        rows(sm, m, h)
                if valid(a) and LAG <= u < H[sa] + LAG:
                    sums(sa, a, u - LAG)

            def attention(flow):
                first = FLOWS[flow][0]
                nxt = after(FLOWS[flow][-1])
                pe.wait_ge(loaded[first], 16)
                turn(first, 0) if (first, 0) != EARLY else None
                total = B * len(FLOWS[flow])
                for step in steps_of(flow):
                    tail, heads, (s, p), (sm, m), (sa, a), (sd, d), (sn, n) = step
                    f, f1, f2 = mix_step(flow, tail + total)
                    if valid(p) and p == 0:
                        pe.wait_ge(loaded[s], 16)
                        if s == "att1":
                            pe.wait_ge(loaded["ctxt"], 16)
                    if f1 == 0:
                        pe.wait_ge(loaded["ffn0"], 16)
                    for u in range(heads) if (s, p) != EARLY else ():
                        beat(flow, step, u)
                    if valid(m):
                        wait(pe, "max_ready", sm, m)
                        wait(pe, "v_ready", s, p)
                        wait(pe, "x_updated", sd, d) if sd == "att1" else None
                        wait(pe, "gate_ready", "ffn0", f1) if f1 is not None else None
                        rows_of = 3 * H[sm]
                        for t in range(2):
                            last = pe.transpose(ps[0:rows_of, SIDE, t * 64:(t + 1) * 64].bitcast(BF16),
                                                negmax_parts[:, t, 0:rows_of], ident16[:, :])
                        last.then_inc(sem["maxt_psum"], 1)
                    if valid(n) and (s, p) != EARLY:
                        wait(pe, "qk_ready", s, p)
                        wait(pe, "hid_ready", sd, d) if sd == "att1" else wait(pe, "x_updated", sd, d)
                        wait(pe, "val_ready", "ffn0", f2) if f2 is not None else None
                        wait(pe, "mix_zt_ready", "ffn0", f1) if f1 is not None else None
                        turn(sn, n)
                    if valid(a):
                        for h in range(max(heads - LAG, 0), H[sa]):
                            sums(sa, a, h)

            def single_head():
                s = "att3"

                def turn_context(i):
                    wait(pe, "zt_ready", s, 0, context_event(i - 1) if i else 1)
                    for t in range(4):
                        last = pe.transpose(ps[0:C, 7, t * P:(t + 1) * P], ctx_sb[:, 4 * i + t, :], ident)
                    last.then_inc(sem["zt_psum"], 1)

                turn_context(0)
                for step in range(B + 2):
                    p, m, d = step, step - 1, step - 2
                    if valid(p):
                        wait(pe, "zt_ready", s, 0, context_event(p // 2))
                        wait(pe, "qk_ready", s, p - 1)
                        pe.matmul(ps[:, 0, 0:T], par(s, "wq"), zt[:, p, 1:1 + T], start=True, stop=True)
                        pe.matmul(ps[:, 0, T:2 * T], par(s, "wk", C), ct[:, p % 2, :], start=True, stop=True)\
                            .then_inc(sem["qk_psum"], 1)
                    if valid(d):
                        wait(pe, "p_ready", s, d)
                        wait(pe, "pt_ready", s, d - 1)
                        for kt in range(2):
                            for t in range(2):
                                last = pe.transpose(ps[:, 3, kt * T + t * P:kt * T + (t + 1) * P],
                                                    prob[:, t, kt * P:(kt + 1) * P], ident)
                        last.then_inc(sem["pt_psum"], 1)
                    if step == B + 1:
                        turn_all("moe3", range(3))
                    if valid(p):
                        wait(pe, "v_ready", s, p - 1)
                        for t in range(2):
                            last = pe.matmul(ps[:, 1, t * D:(t + 1) * D], ct[:, p % 2, t * P:(t + 1) * P],
                                             par(s, "wv", C), start=True, stop=True)
                        last.then_inc(sem["v_psum"], 1)
                        if p % 2 == 1 and p < B - 1:
                            turn_context(p // 2 + 1)
                    if valid(d):
                        wait(pe, "pt_ready", s, d)
                        wait(pe, "v_ready", s, d)
                        wait(pe, "o_ready", s, d - 1)
                        wait_x(pe, s) if d == 0 else None
                        for t in range(2):
                            for kt in range(2):
                                last = pe.matmul(ps[:, 4, t * D:(t + 1) * D], pt[:, kt * T + t * P:kt * T + (t + 1) * P],
                                                 v2[:, d % 3, kt, :], start=(kt == 0), stop=(kt == 1))
                        last.then_inc(sem["pv_psum"], 1)
                    if valid(p):
                        wait(pe, "qk_ready", s, p)
                        wait(pe, "p_ready", s, p - 1)
                        for t in range(2):
                            last = pe.matmul(ps[:, 2, t * T:(t + 1) * T], qk[:, 0, t * P:(t + 1) * P], qk[:, 1, :],
                                             start=True, stop=True)
                        last.then_inc(sem["s_psum"], 1)
                    if valid(d):
                        wait(pe, "ot_ready", s, d - 1)
                        turn_o(s, d, 5)
                        wait(pe, "x_updated", s, d - 1)
                        project_o(s, d, 6)
                    if step == 0:
                        turn_all(s, range(3, 4))
                    if step == B + 1:
                        logits("moe3", 0)

            def down(s, blk, e):
                wait(pe, "h_ready", s, blk, 2 * e + 1)
                if isinstance(blk, int) and blk == 0 and e == 0:
                    wait_x(pe, s)
                if isinstance(blk, int) and blk == 0 and e == 1:
                    wait(pe, "route_exp_in", s, 0, 0)
                wait(pe, "x_updated", s, blk, e - 2)
                for t in range(BT):
                    for c in range(2):
                        k = 2 * e + c
                        last = pe.matmul(ps[:, 4 + e % 2, t * D:(t + 1) * D], ht[:, e % 2, c, t * P:(t + 1) * P],
                                         par(s, "wd" if s == "moe1" else "w2")[:, k * P:(k + 1) * P],
                                         start=(c == 0), stop=(c == 1))
                last.then_inc(sem["y_psum"], 1)

            def beside_last_block(e):
                first = EARLY[0]
                if e == 2:
                    pe.wait_ge(loaded[first], 16)
                    turn(first, 0)
                for u in EARLY_BEATS[e]:
                    beat(first, next(steps_of(first)), u)
                if e == E - 1:
                    wait(pe, "qk_ready", first, 0)
                    turn(first, 1)

            def block_of(s, blk, first=False, final=False):
                for e in range(E):
                    for c in range(2):
                        k = 2 * e + c
                        if s == "moe1":
                            wait(pe, "h_ready", s, blk, k - 2)
                            if first and k == 0:
                                wait(pe, "zt_ready", s, 0, 2)
                            products = (("wg", 2 * c), ("wu", 2 * c + 1))
                        else:
                            wait(pe, "h_ready", s, blk, k - 4)
                            if first and k == 0:
                                wait(pe, "zt_ready", s, 0, 2)
                            products = (("w1", 2 * (e % 2) + c),)
                        for name, bank in products:
                            last = pe.matmul(ps[:, bank, :], par(s, name)[:, k * P:(k + 1) * P],
                                             zt[:, bass.ds(2 * blk, 2), 1:1 + T], start=True, stop=True)
                        last.then_inc(sem["up_psum"], 1)
                    if e >= 1:
                        down(s, blk, e - 1)
                    elif not first:
                        down(s, blk - 1, E - 1)
                    if first:
                        beside_first_block(s, e)
                    if final and s == "moe1":
                        beside_last_block(e)
                    if final and s == "moe2" and 4 <= e < 7:
                        turn_all("att3", range(e - 4, e - 3))

            def experts(s):
                if s == "moe3":
                    for blk in range(NBLK):
                        for i in range(E + 2):
                            if i <= E:
                                w = E if i == 0 else i - 1
                                if blk == 0 and i == 0:
                                    wait(pe, "route_exp_in", s, 0, 0)
                                if blk == 0 and i == 1:
                                    wait(pe, "wt_ready", s, 0, 1)
                                wait(pe, "h_ready", s, blk, i - 2) if i >= 2 else wait(pe, "h_ready", s, blk - 1)
                                if i:
                                    wait(pe, "zs_ready", s, blk, i - 1)
                                rhs = zs[:, (i - 1) % 2, :] if i else zt[:, 2 * blk:2 * blk + 2, 1:1 + T]
                                pe.matmul(ps[:, 2 * (i % 2), :], par(s, "w1")[:, w * P:(w + 1) * P], rhs,
                                          start=True, stop=True)
                                pe.matmul(ps[:, 2 * (i % 2) + 1, :], par(s, "w3")[:, w * P:(w + 1) * P], rhs,
                                          start=True, stop=True).then_inc(sem["up_psum"], 1)
                            if i >= 1:
                                q = i - 1
                                w = E if q == 0 else q - 1
                                wait(pe, "h_ready", s, blk, q)
                                if q == 0:
                                    wait_x(pe, s) if blk == 0 else None
                                    wait(pe, "x_updated", s, blk - 2)
                                for t in range(BT):
                                    last = pe.matmul(ps[:, 4 + blk % 2, t * D:(t + 1) * D],
                                                     ht[:, q % 2, 0, t * P:(t + 1) * P],
                                                     par(s, "w2")[:, w * P:(w + 1) * P], start=(q == 0 and t == 0),
                                                     stop=(q == E), skip_group_check=True)
                                last.then_inc(sem["y_psum"], 1)
                            if blk == 0 and i < E:
                                beside_first_block(s, i)
                    return
                block_of(s, 0, True)
                with pe.Fori(1, NBLK - 1) as blk:
                    block_of(s, blk)
                block_of(s, NBLK - 1, final=True)
                down(s, NBLK - 1, E - 1)

            for s in STAGES:
                if s in ("ffn0", "att1"):
                    continue
                pe.wait_ge(loaded[s], 16)
                if s in ATT:
                    wait_x(pe, s)
                if s in ATT:
                    attention(s)
                elif s == "att3":
                    single_head()
                else:
                    experts(s)


def columns(inputs):
    f = {k: np.asarray(a) for k, a in inputs.items()}

    def col(v):
        return v[:, None]

    def row(v):
        return np.broadcast_to(v[None, :], (P, v.shape[0]))

    def heads_last(w, s):
        return w.reshape(w.shape[0], H[s], D // H[s]).transpose(0, 2, 1).reshape(w.shape[0], D)

    def att(s, name, bias=True):
        q, k = f[name + "Wq"], f[name + "Wk"]
        one = {"wq": q, "wk": k, "wv": f[name + "Wv"]}
        if s in H:
            one["wq"], one["wk"] = heads_last(q, s), heads_last(k, s)
        bq, bk = f[name + "bq"], f[name + "bk"]
        if s in H:
            bq, bk = heads_last(bq[None], s)[0], heads_last(bk[None], s)[0]
        one.update(bq=col(bq), bk=col(bk), bv=row(f[name + "bv"]))
        return one

    got = {}
    got["consts"] = {"ident": np.eye(P, dtype=np.float32), "index": row(np.arange(E, dtype=np.float32) - E)}
    n = "L0_xattn_"
    got["att0"] = {"wq": heads_last(f[n + "W_Q"], "att0"), "wk": heads_last(f[n + "W_K"], "att0"), "wv": f[n + "W_V"],
                   "xg": col(f[n + "ln_lat_g"]), "xb": col(f[n + "ln_lat_b"]),
                   "cg": col(f[n + "ln_in_g"]), "cb": col(f[n + "ln_in_b"]), "wo": f[n + "W_O"]}
    n = "L0_ffn_"
    got["ffn0"] = {"wr": f[n + "W_r"].T, "wk": f[n + "W_k"].T, "wv": f[n + "W_v"].T,
                   "mur": col(f[n + "mu_r"]), "muk": col(f[n + "mu_k"])}
    n = "L1_xattn_"
    got["att1"] = {**att("att1", n), "w1": f[n + "W1"], "b1": f[n + "b1"].reshape(2, P).T,
                   "w2": f[n + "W2"].reshape(2, P, D).transpose(1, 0, 2).reshape(P, 2 * D), "bo": row(f[n + "b2"])}
    n = "L1_ffn_"
    got["moe1"] = {"router": f[n + "router_w"].T, "wg": f[n + "w_gate"].transpose(2, 0, 1).reshape(P, -1),
                   "wu": f[n + "w_up"].transpose(2, 0, 1).reshape(P, -1),
                   "wd": f[n + "w_down"].reshape(E, D, 2, P).transpose(3, 0, 2, 1).reshape(P, -1)}
    n = "L2_xattn_"
    got["att2"] = {**att("att2", n), "wo": f[n + "Wo"], "bo": row(f[n + "bo"])}
    n = "L2_ffn_"
    got["moe2"] = {"router": f[n + "rW"], "rb": row(f[n + "rb"]), "xg": col(f[n + "ln_g"]), "xb": col(f[n + "ln_b"]),
                   "w1": f[n + "W1"].transpose(1, 0, 2).reshape(P, -1), "b1": f[n + "b1"].reshape(2 * E, P).T,
                   "w2": f[n + "W2"].reshape(E, 2, P, D).transpose(2, 0, 1, 3).reshape(P, -1), "b2": f[n + "b2"]}
    n = "L3_xattn_"
    got["att3"] = {**att("att3", n), "wo": f[n + "Wo"], "bo": row(f[n + "bo"]),
                   "xg": col(f[n + "ln1_g"]), "xb": col(f[n + "ln1_b"]),
                   "cg": col(f[n + "ln2_g"]), "cb": col(f[n + "ln2_b"])}
    n = "L3_ffn_"
    both = {w: np.concatenate([f[n + w], f[n + w + "s"]]).transpose(1, 0, 2).reshape(P, -1) for w in ("w1", "w2", "w3")}
    got["moe3"] = {"router": f[n + "gate_w"].T, **both}

    packed = {}
    for s, names in PACKS.items():
        a = np.zeros((P, sum(w for _, w in names)), np.float32)
        at = 0
        for name, w in names:
            part = got[s][name]
            a[0:part.shape[0], at:at + w] = part
            at += w
        packed[s] = a
    return packed


def kernel(**inputs):
    import concourse.bacc as bacc
    from concourse.bass_utils import run_bass_kernel_spmd

    x = np.asarray(inputs["x"])
    ctx = np.asarray(inputs["ctx_768"]).reshape(B * T, C)
    arrays = {"x": x.reshape(B * T, D), "ctx": ctx, "ctxt": ctx.T, **columns(inputs)}
    arrays = {f"in_{k}": np.ascontiguousarray(a) for k, a in arrays.items()}
    nc = bacc.Bacc("TRN2", target_bir_lowering=False, num_devices=1)
    args = {k[3:]: nc.dram_tensor(k, a.shape, mybir.dt.from_np(a.dtype), kind="ExternalInput").ap()
            for k, a in arrays.items()}
    out = nc.dram_tensor("out", (B * T, D), F32, kind="ExternalOutput").ap()
    build(nc, args, out)
    r = run_bass_kernel_spmd(nc, [arrays], core_ids=[0])
    return r.results[0]["out"].reshape(x.shape)
```
